# Optimizing a Trainium2 kernel written in Bass

```python
import numpy as np
import jax
import jax.numpy as jnp

def _softmax(x, axis=-1):
    return jax.nn.softmax(x, axis=axis)

def _gelu(x):
    return jax.nn.gelu(x, approximate=True)

def _silu(x):
    return jax.nn.silu(x)

def _sigmoid(x):
    return jax.nn.sigmoid(x)

def _layernorm(x, axis=-1, eps=1e-05):
    m = jnp.mean(x, axis=axis, keepdims=True)
    v = jnp.var(x, axis=axis, keepdims=True)
    return (x - m) / jnp.sqrt(v + eps)

def _scatter_add(tgt, idx, src, axis=0):
    return tgt.at[idx].add(src)

def _segment_sum(src, seg, n):
    return jax.ops.segment_sum(src, seg, n)
kernel_name = 'mk_lm_tower_d1_tok_ids1024_r4_835627'

def setup_inputs(seed: int=0):
    np.random.seed(seed)
    _w = jnp.asarray

    def _rec_inputs():
        import jax
        import jax.numpy as jnp
        _rk = jax.random.key(seed)
        x = jax.random.randint(jax.random.fold_in(_rk, 1), (4, 512), 0, 12564, jnp.int32)
        return x
    x = _rec_inputs()

    def _L0_tok_setup():
        import jax, jax.numpy as jnp
        import numpy as np
        VOCAB = 50257
        NUM_DIM = 256
        BATCH = 4
        SEQ = 1024
        key = jax.random.key(seed)
        k_tok, k_w, k_b = jax.random.split(key, 3)
        tokens = jax.random.randint(k_tok, (BATCH, SEQ), 0, VOCAB)
        weight = jax.random.normal(k_w, (NUM_DIM, VOCAB), dtype=jnp.float32) * 0.02
        bias = jax.random.normal(k_b, (NUM_DIM,), dtype=jnp.float32) * 0.02
        return {'tokens': tokens, 'weight': weight, 'bias': bias}
    _L0_tok_all = _L0_tok_setup()
    _L0_tok_in = {k: v for k, v in _L0_tok_all.items() if k in ('weight', 'bias')}
    del _L0_tok_all

    def _L0_attn_setup():
        import jax, jax.numpy as jnp
        import numpy as np
        DIM = 256
        HEADS = 16
        KDIM = DIM // 2
        VDIM = DIM
        DK = KDIM // HEADS
        DV = VDIM // HEADS
        LOW = 16
        NORMALIZER = 16.0
        EPS = 1e-05
        B, T = (2, 1024)

        def _gla_scan(q, k, v, gk):
            scale = DK ** (-0.5)

            def step(h, inp):
                qt, kt, vt, gt = inp
                h = h * jnp.exp(gt)[..., None] + kt[..., None] * vt[..., None, :]
                ot = jnp.einsum('bhk,bhkv->bhv', qt * scale, h)
                return (h, ot)
            h0 = jnp.zeros((q.shape[0], HEADS, DK, DV), q.dtype)
            xs = tuple((jnp.moveaxis(a, 1, 0) for a in (q, k, v, gk)))
            _, o = jax.lax.scan(step, h0, xs)
            return jnp.moveaxis(o, 0, 1)
        key = jax.random.key(seed)
        ks = jax.random.split(key, 9)

        def lin(k, sh, fan_in):
            return jax.random.normal(k, sh, jnp.float32) * fan_in ** (-0.5)
        return {'x': jax.random.normal(ks[0], (B, T, DIM), jnp.float32), 'Wq': lin(ks[1], (DIM, KDIM), DIM), 'Wk': lin(ks[2], (DIM, KDIM), DIM), 'Wv': lin(ks[3], (DIM, VDIM), DIM), 'Wgk1': lin(ks[4], (DIM, LOW), DIM), 'Wgk2': lin(ks[5], (LOW, KDIM), LOW), 'bgk2': jnp.zeros((KDIM,), jnp.float32), 'Wg': lin(ks[6], (DIM, VDIM), DIM), 'gnw': jnp.ones((DV,), jnp.float32), 'Wo': lin(ks[7], (VDIM, DIM), VDIM)}
    _L0_attn_all = _L0_attn_setup()
    _L0_attn_in = {k: v for k, v in _L0_attn_all.items() if k in ('Wq', 'Wk', 'Wv', 'Wgk1', 'Wgk2', 'bgk2', 'Wg', 'gnw', 'Wo')}
    del _L0_attn_all

    def _L0_ffn_setup():
        import jax, jax.numpy as jnp
        import numpy as np
        EMBED = 256
        HEADS = 16
        HEAD_DIM = EMBED // HEADS
        NUM_EXPERTS = 8
        TOP_K = 2
        HIDDEN = (int(2 * (4 * EMBED) / 3) + 63) // 64 * 64
        SEQ = 512
        BATCH = 2
        ROPE_BASE = 10000.0
        EPS = 1e-06

        def _rope_tables(seq_len, dim):
            inv_freq = 1.0 / ROPE_BASE ** (np.arange(0, dim, 2, dtype=np.float32) / dim)
            t = np.arange(seq_len, dtype=np.float32)
            freqs = np.einsum('i,j->ij', t, inv_freq)
            emb = np.concatenate([freqs, freqs], axis=-1)
            return (jnp.asarray(np.cos(emb)), jnp.asarray(np.sin(emb)))

        def _rotate_half(x):
            x1, x2 = jnp.split(x, 2, axis=-1)
            return jnp.concatenate([-x2, x1], axis=-1)

        def _rmsnorm(x, w):
            return x * jax.lax.rsqrt(jnp.mean(x * x, axis=-1, keepdims=True) + EPS) * w

        def _attention(x, wq, wk, wv, wo):
            B, S, _ = x.shape
            q = (x @ wq).reshape(B, S, HEADS, HEAD_DIM).transpose(0, 2, 1, 3)
            k = (x @ wk).reshape(B, S, HEADS, HEAD_DIM).transpose(0, 2, 1, 3)
            v = (x @ wv).reshape(B, S, HEADS, HEAD_DIM).transpose(0, 2, 1, 3)
            cos, sin = _rope_tables(S, HEAD_DIM)
            cos = cos[None, None]
            sin = sin[None, None]
            q = q * cos + _rotate_half(q) * sin
            k = k * cos + _rotate_half(k) * sin
            scale = HEAD_DIM ** (-0.5)
            scores = jnp.einsum('bhqd,bhkd->bhqk', q, k) * scale
            causal = jnp.triu(jnp.ones((S, S), bool), k=1)
            scores = jnp.where(causal, -jnp.inf, scores)
            attn = jax.nn.softmax(scores, axis=-1)
            out = jnp.einsum('bhqk,bhkd->bhqd', attn, v)
            out = out.transpose(0, 2, 1, 3).reshape(B, S, EMBED)
            return out @ wo

        def _moe(x, w_router, wg, wu, wd):
            B, S, E = x.shape
            xf = x.reshape(-1, E)
            logits = xf @ w_router
            probs = jax.nn.softmax(logits, axis=-1)
            topw, topi = jax.lax.top_k(probs, TOP_K)
            topw = topw / jnp.sum(topw, axis=-1, keepdims=True)
            combine = jnp.sum(jax.nn.one_hot(topi, NUM_EXPERTS, dtype=xf.dtype) * topw[..., None], axis=1)
            g = jax.nn.silu(jnp.einsum('td,xdh->txh', xf, wg))
            u = jnp.einsum('td,xdh->txh', xf, wu)
            eo = jnp.einsum('txh,xhd->txd', g * u, wd)
            out = jnp.einsum('txd,tx->td', eo, combine)
            return out.reshape(B, S, E)
        key = jax.random.key(seed)
        ks = jax.random.split(key, 12)
        s = 0.02
        return {'x': jax.random.normal(ks[0], (BATCH, SEQ, EMBED), jnp.float32), 'wq': jax.random.normal(ks[1], (EMBED, EMBED), jnp.float32) * s, 'wk': jax.random.normal(ks[2], (EMBED, EMBED), jnp.float32) * s, 'wv': jax.random.normal(ks[3], (EMBED, EMBED), jnp.float32) * s, 'wo': jax.random.normal(ks[4], (EMBED, EMBED), jnp.float32) * s, 'w_router': jax.random.normal(ks[5], (EMBED, NUM_EXPERTS), jnp.float32) * s, 'wg': jax.random.normal(ks[6], (NUM_EXPERTS, EMBED, HIDDEN), jnp.float32) * s, 'wu': jax.random.normal(ks[7], (NUM_EXPERTS, EMBED, HIDDEN), jnp.float32) * s, 'wd': jax.random.normal(ks[8], (NUM_EXPERTS, HIDDEN, EMBED), jnp.float32) * s, 'g1': jnp.ones((EMBED,), jnp.float32), 'g2': jnp.ones((EMBED,), jnp.float32)}
    _L0_ffn_all = _L0_ffn_setup()
    _L0_ffn_in = {k: v for k, v in _L0_ffn_all.items() if k in ('wq', 'wk', 'wv', 'wo', 'w_router', 'wg', 'wu', 'wd', 'g1', 'g2')}
    del _L0_ffn_all
    return {'x': x, 'L0_tok_weight': _L0_tok_in['weight'], 'L0_tok_bias': _L0_tok_in['bias'], 'L0_attn_Wq': _L0_attn_in['Wq'], 'L0_attn_Wk': _L0_attn_in['Wk'], 'L0_attn_Wv': _L0_attn_in['Wv'], 'L0_attn_Wgk1': _L0_attn_in['Wgk1'], 'L0_attn_Wgk2': _L0_attn_in['Wgk2'], 'L0_attn_bgk2': _L0_attn_in['bgk2'], 'L0_attn_Wg': _L0_attn_in['Wg'], 'L0_attn_gnw': _L0_attn_in['gnw'], 'L0_attn_Wo': _L0_attn_in['Wo'], 'L0_ffn_wq': _L0_ffn_in['wq'], 'L0_ffn_wk': _L0_ffn_in['wk'], 'L0_ffn_wv': _L0_ffn_in['wv'], 'L0_ffn_wo': _L0_ffn_in['wo'], 'L0_ffn_w_router': _L0_ffn_in['w_router'], 'L0_ffn_wg': _L0_ffn_in['wg'], 'L0_ffn_wu': _L0_ffn_in['wu'], 'L0_ffn_wd': _L0_ffn_in['wd'], 'L0_ffn_g1': _L0_ffn_in['g1'], 'L0_ffn_g2': _L0_ffn_in['g2']}

def reference(x, L0_tok_weight, L0_tok_bias, L0_attn_Wq, L0_attn_Wk, L0_attn_Wv, L0_attn_Wgk1, L0_attn_Wgk2, L0_attn_bgk2, L0_attn_Wg, L0_attn_gnw, L0_attn_Wo, L0_ffn_wq, L0_ffn_wk, L0_ffn_wv, L0_ffn_wo, L0_ffn_w_router, L0_ffn_wg, L0_ffn_wu, L0_ffn_wd, L0_ffn_g1, L0_ffn_g2):
    import jax
    import jax.numpy as jnp

    def _L0_tok_ref(tokens, weight, bias):
        import jax, jax.numpy as jnp
        import numpy as np
        VOCAB = 50257
        NUM_DIM = 256
        BATCH = 4
        SEQ = 1024
        table = weight.T
        return jnp.take(table, tokens, axis=0) + bias

    def _L0_attn_ref(x, Wq, Wk, Wv, Wgk1, Wgk2, bgk2, Wg, gnw, Wo):
        import jax, jax.numpy as jnp
        import numpy as np
        DIM = 256
        HEADS = 16
        KDIM = DIM // 2
        VDIM = DIM
        DK = KDIM // HEADS
        DV = VDIM // HEADS
        LOW = 16
        NORMALIZER = 16.0
        EPS = 1e-05
        B, T = (2, 1024)

        def _gla_scan(q, k, v, gk):
            scale = DK ** (-0.5)

            def step(h, inp):
                qt, kt, vt, gt = inp
                h = h * jnp.exp(gt)[..., None] + kt[..., None] * vt[..., None, :]
                ot = jnp.einsum('bhk,bhkv->bhv', qt * scale, h)
                return (h, ot)
            h0 = jnp.zeros((q.shape[0], HEADS, DK, DV), q.dtype)
            xs = tuple((jnp.moveaxis(a, 1, 0) for a in (q, k, v, gk)))
            _, o = jax.lax.scan(step, h0, xs)
            return jnp.moveaxis(o, 0, 1)
        Bx, Tx, _ = x.shape
        q = (x @ Wq).reshape(Bx, Tx, HEADS, DK)
        k = (x @ Wk).reshape(Bx, Tx, HEADS, DK)
        v = (x @ Wv).reshape(Bx, Tx, HEADS, DV)
        gk = jax.nn.log_sigmoid(x @ Wgk1 @ Wgk2 + bgk2)
        gk = gk.reshape(Bx, Tx, HEADS, DK) / NORMALIZER
        o = _gla_scan(q, k, v, gk)
        g = (x @ Wg).reshape(Bx, Tx, HEADS, DV)
        o = o * jax.lax.rsqrt(jnp.mean(o * o, axis=-1, keepdims=True) + EPS) * gnw
        o = o * (g * jax.nn.sigmoid(g))
        return o.reshape(Bx, Tx, VDIM) @ Wo

    def _L0_ffn_ref(x, wq, wk, wv, wo, w_router, wg, wu, wd, g1, g2):
        import jax, jax.numpy as jnp
        import numpy as np
        EMBED = 256
        HEADS = 16
        HEAD_DIM = EMBED // HEADS
        NUM_EXPERTS = 8
        TOP_K = 2
        HIDDEN = (int(2 * (4 * EMBED) / 3) + 63) // 64 * 64
        SEQ = 512
        BATCH = 2
        ROPE_BASE = 10000.0
        EPS = 1e-06

        def _rope_tables(seq_len, dim):
            inv_freq = 1.0 / ROPE_BASE ** (np.arange(0, dim, 2, dtype=np.float32) / dim)
            t = np.arange(seq_len, dtype=np.float32)
            freqs = np.einsum('i,j->ij', t, inv_freq)
            emb = np.concatenate([freqs, freqs], axis=-1)
            return (jnp.asarray(np.cos(emb)), jnp.asarray(np.sin(emb)))

        def _rotate_half(x):
            x1, x2 = jnp.split(x, 2, axis=-1)
            return jnp.concatenate([-x2, x1], axis=-1)

        def _rmsnorm(x, w):
            return x * jax.lax.rsqrt(jnp.mean(x * x, axis=-1, keepdims=True) + EPS) * w

        def _attention(x, wq, wk, wv, wo):
            B, S, _ = x.shape
            q = (x @ wq).reshape(B, S, HEADS, HEAD_DIM).transpose(0, 2, 1, 3)
            k = (x @ wk).reshape(B, S, HEADS, HEAD_DIM).transpose(0, 2, 1, 3)
            v = (x @ wv).reshape(B, S, HEADS, HEAD_DIM).transpose(0, 2, 1, 3)
            cos, sin = _rope_tables(S, HEAD_DIM)
            cos = cos[None, None]
            sin = sin[None, None]
            q = q * cos + _rotate_half(q) * sin
            k = k * cos + _rotate_half(k) * sin
            scale = HEAD_DIM ** (-0.5)
            scores = jnp.einsum('bhqd,bhkd->bhqk', q, k) * scale
            causal = jnp.triu(jnp.ones((S, S), bool), k=1)
            scores = jnp.where(causal, -jnp.inf, scores)
            attn = jax.nn.softmax(scores, axis=-1)
            out = jnp.einsum('bhqk,bhkd->bhqd', attn, v)
            out = out.transpose(0, 2, 1, 3).reshape(B, S, EMBED)
            return out @ wo

        def _moe(x, w_router, wg, wu, wd):
            B, S, E = x.shape
            xf = x.reshape(-1, E)
            logits = xf @ w_router
            probs = jax.nn.softmax(logits, axis=-1)
            topw, topi = jax.lax.top_k(probs, TOP_K)
            topw = topw / jnp.sum(topw, axis=-1, keepdims=True)
            combine = jnp.sum(jax.nn.one_hot(topi, NUM_EXPERTS, dtype=xf.dtype) * topw[..., None], axis=1)
            g = jax.nn.silu(jnp.einsum('td,xdh->txh', xf, wg))
            u = jnp.einsum('td,xdh->txh', xf, wu)
            eo = jnp.einsum('txh,xhd->txd', g * u, wd)
            out = jnp.einsum('txd,tx->td', eo, combine)
            return out.reshape(B, S, E)
        h = x + _attention(_rmsnorm(x, g1), wq, wk, wv, wo)
        y = h + _moe(_rmsnorm(h, g2), w_router, wg, wu, wd)
        return y
    h = _L0_tok_ref(x, L0_tok_weight, L0_tok_bias)
    h = h + _L0_attn_ref(_layernorm(h, axis=-1), L0_attn_Wq, L0_attn_Wk, L0_attn_Wv, L0_attn_Wgk1, L0_attn_Wgk2, L0_attn_bgk2, L0_attn_Wg, L0_attn_gnw, L0_attn_Wo)
    h = h + _L0_ffn_ref(_layernorm(h, axis=-1), L0_ffn_wq, L0_ffn_wk, L0_ffn_wv, L0_ffn_wo, L0_ffn_w_router, L0_ffn_wg, L0_ffn_wu, L0_ffn_wd, L0_ffn_g1, L0_ffn_g2)
    return h

_drawn_inputs = setup_inputs


def setup_inputs(seed=0):
    import zlib

    import numpy as np

    out = dict(_drawn_inputs(seed))
    spreads = {'L0_attn_bgk2': (0.0, 0.1),
     'L0_attn_gnw': (1.0, 0.2),
     'L0_ffn_g1': (1.0, 0.6),
     'L0_ffn_g2': (1.0, 0.6)}
    factors = {'L0_ffn_wq': 8.0,
     'L0_ffn_wk': 8.0,
     'L0_ffn_w_router': 4.804,
     'L0_ffn_wg': 4.199,
     'L0_ffn_wu': 4.204,
     'L0_ffn_wd': 4.16}
    for name, (base, spread) in spreads.items():
        noise = np.random.default_rng([zlib.crc32(name.encode()), seed]).standard_normal(out[name].shape)
        drawn = base * np.exp(spread * noise) if base else spread * noise
        out[name] = jnp.asarray(drawn.astype(out[name].dtype))
    for name, factor in factors.items():
        out[name] = (out[name] * factor).astype(out[name].dtype)
    return out
```

```python
from contextlib import ExitStack

import numpy as np

import concourse.bass as bass
from concourse import mybir

ALU = mybir.AluOpType
ACT = mybir.ActivationFunctionType
AX = mybir.AxisListType
F32 = mybir.dt.float32
F16 = mybir.dt.float16
I32 = mybir.dt.int32

P = 128
B, T, D = 4, 512, 256
KC = D // P
TT = T // P
NT = B * TT
H = 16
DK, DV = 8, 16
HPG, G = 4, 4
LOW = 16
SUB = 64
HD = 16
VW = H * (HD + 1) + 32 - (HD + 1)
ST = 64
X, HID, TOP = 8, 704, 2
HC = [(c * P, min(P, HID - c * P)) for c in range(-(-HID // P))]
XT = (NT * P * TOP + X * (P - 1)) // P
ROWS = XT * P
W_SCALE = 256.0
DC, DQ = 2, len(HC) // 2
NEVER = -60000.0


def shape_constants():
    i = np.arange(P)
    inv = 1.0 / 10000.0 ** (np.arange(0, HD, 2, dtype=np.float32) / HD)
    ang = np.einsum("i,j->ij", np.arange(T, dtype=np.float32), inv)
    cos = np.cos(np.concatenate([ang, ang], -1)).astype(np.float32)
    sin = np.sin(np.concatenate([ang, ang], -1)).astype(np.float32)
    sin[:, :HD // 2] *= -1
    tile = lambda a: np.ascontiguousarray(a.reshape(TT, P, HD).transpose(1, 0, 2).reshape(P, -1))
    gate = np.ones(T, np.float32)
    gate[::SUB] = 0
    rows = H * DK
    e_reset = np.ones((X, NT), np.float32)
    e_reset[:, 0] = 0
    f = lambda a: np.ascontiguousarray(a, np.float32)
    parts = [
        ("ident", f(np.eye(P))),
        ("upto", f(i[:, None] <= i[None, :])),
        ("before", f(i[:, None] < i[None, :])),
        ("ones", f(np.ones((P, P)))),
        ("cos", tile(cos)), ("sin", tile(sin)),
        ("powers", f(np.broadcast_to(np.float32(-0.5), (P, TT * H)))),
        ("rank8", f(np.broadcast_to(X - np.arange(X), (P, X)))),
        ("ereset", f(np.broadcast_to(e_reset.reshape(-1), (P, X * NT)))),
        ("xreset", f(np.broadcast_to(np.float32([0] + [1] * (X - 1)), (P, X)))),
        ("tileno", f(np.broadcast_to(np.arange(XT), (P, XT)))),
    ]
    first = [
        ("subreset", f(np.broadcast_to(gate, (P, T)))),
        ("headblock", f(np.arange(rows)[:, None] // DK == np.arange(H * DV)[None, :] // DV)),
        ("headmask", f((np.arange(rows)[:, None] // DK) % HPG == np.arange(HPG)[None, :])),
    ]
    half = [
        ("ident16", np.eye(P)),
        ("future_k", np.where(i[None, :] > i[:, None], NEVER, 0)),
        ("future_q", np.where(i[:, None] > i[None, :], NEVER, 0)),
    ]
    return packed(parts), packed(first), packed([(n, a.astype(np.float16)) for n, a in half])


def packed(parts):
    at, where = 0, {}
    for name, a in parts:
        where[name] = (at, a.shape[1])
        at += a.shape[1]
    return np.ascontiguousarray(np.concatenate([a for _, a in parts], 1)), where


UNROLL = True
CONST, CONST_FIRST, CONST_HALF = shape_constants()


class Arena:

    def __init__(self, tensor, words):
        self.tensor, self.words, self.at = tensor, words, 0

    def take(self, *shape, dtype=F32):
        n = int(np.prod(shape))
        words = n if dtype != F16 else n // 2
        assert self.at + words <= self.words, (self.at, words, self.words)
        ap = self.tensor[:, self.at:self.at + words]
        self.at += words
        if dtype != F32:
            ap = ap.bitcast(dtype)
        if len(shape) > 1:
            names = "abcd"[:len(shape)]
            ap = ap.rearrange(f"p ({' '.join(names)}) -> p {' '.join(names)}",
                              **{k: v for k, v in zip(names, shape)})
        return ap


def spread(ap, axis, n):
    ap = ap.unsqueeze(axis)
    shape = list(ap.shape)
    shape[axis] = n
    return ap.broadcast_to(shape)


def nds(t):
    return bass.ds(t, 1)


def repeat(eng, n, body):
    if UNROLL:
        for i in range(n):
            body(i)
    else:
        with eng.Fori(0, n) as i:
            body(i)


class Order:

    def __init__(self, eng, sem, base=0):
        self.eng, self.sem, self.base, self.n = eng, sem, base, 0

    def after(self, ins):
        self.n += 1
        ins.then_inc(self.sem, 1)
        self.eng.wait_ge(self.sem, self.base + self.n)


def linear_attention(nc, ctx, s):
    ar = Arena(s.scratch, s.scratch_words)
    xn = ar.take(TT, D)
    xT = ar.take(KC, T)
    z1T = ar.take(T)
    zb = ar.take(T)
    e1 = ar.take(T)
    ls = ar.take(T)
    e_in = ar.take(T)
    e_inv = ar.take(T)
    e_out = ar.take(T)
    qd = ar.take(TT, P)
    qi = ar.take(TT, P)
    qx = ar.take(HPG, TT, P)
    ka = ar.take(TT, P)
    kb = ar.take(TT, P)
    ks = ar.take(TT, P)
    ksT = ar.take(TT, P)
    vg = ar.take(TT, 2 * D)
    att = ar.take(2, HPG, P)
    state = ar.take(D)
    dstate = ar.take(D)
    dec = ar.take(TT)
    th = ar.take(D)
    sq = ar.take(D)
    og = ar.take(TT, D)
    ogT = xT
    stats = ar.take(TT, 6)
    mv = ar.take(TT, 2)
    rstd = ar.take(TT)
    ms = ar.take(H)
    rms = ar.take(H)
    ps, c = s.psum, s.const
    names = ["h", "mv", "rstd", "xn", "xTp", "xT", "z1p", "z1", "gkp", "qp", "kp", "vgp", "vg", "zb", "lsig",
             "ls", "dout", "exps", "kst", "qx", "ksTp", "ksT", "ap", "att", "sp", "sadd", "op", "sq", "th", "ms",
             "rms", "og", "ogTp", "ogT", "yp", "y", "dve", "act", "pool", "zeros"]
    sem = {n: ctx.enter_context(nc.semaphore("gla_" + n)) for n in names}
    block = ctx.enter_context(nc.Block())

    @block.gpsimd
    def _(eng):
        eng.wait_ge(s.ids_in, 16)
        for t in range(NT):
            nc.gpsimd.indirect_dma_start(
                out=s.h[:, t, :], out_offset=None, in_=s.table,
                in_offset=bass.IndirectOffsetOnAxis(ap=s.ids[:, t:t + 1], axis=0),
            ).then_inc(s.rows_in[t // TT], 16)
        eng.wait_ge(s.const_in, 48)
        o = Order(eng, sem["pool"])

        def sequence(b):
            eng.wait_ge(sem["mv"], b + 1)
            o.after(eng.tensor_scalar(rstd, mv[:, :, 1], 1e-5, None, ALU.add))
            eng.tensor_tensor(rstd, rstd, c("powers")[:, 0:TT], ALU.pow).then_inc(sem["rstd"], 1)
            for t in range(TT):
                eng.wait_ge(sem["ms"], b * TT + t + 1)
                o.after(eng.tensor_scalar(rms, ms, 1.0 / DV, 1e-5, ALU.mult, ALU.add))
                eng.tensor_tensor(rms, rms, c("powers")[:, 0:H], ALU.pow).then_inc(sem["rms"], 1)
                eng.wait_ge(sem["rms"], b * TT + t + 1)
        repeat(eng, B, sequence)

    @block.scalar
    def _(eng):
        o = Order(eng, sem["act"])

        def sequence(b):
            for k in range(KC):
                eng.wait_ge(sem["xTp"], b * KC + k + 1)
                eng.activation(xT[:, k, :], ps[:, k, :], ACT.Copy).then_inc(sem["xT"], 1)
            eng.wait_ge(sem["z1p"], b + 1)
            eng.activation(z1T[0:LOW, :], ps[0:LOW, 4, :], ACT.Copy).then_inc(sem["z1"], 1)
            for t in range(TT):
                eng.wait_ge(sem["vgp"], b * TT + t + 1)
                eng.activation(vg[:, t, :], ps[:, 6 + t % 2, :], ACT.Copy).then_inc(sem["vg"], 1)
            eng.wait_ge(sem["zb"], b + 1)
            o.after(eng.activation(e1, zb, ACT.Abs))
            o.after(eng.activation(e1, e1, ACT.Exp, scale=-1.0))
            eng.activation(e1, e1, ACT.Ln, bias=1.0).then_inc(sem["lsig"], 1)
            eng.wait_ge(sem["ls"], b + 1)
            eng.activation(e_in, ls, ACT.Exp, scale=1.0 / 16).then_inc(sem["exps"], 1)
            eng.activation(e_inv, ls, ACT.Exp, scale=-1.0 / 16).then_inc(sem["exps"], 1)
            eng.wait_ge(sem["dout"], b + 1)
            eng.activation(e_out, e_out, ACT.Exp, scale=1.0 / 16).then_inc(sem["exps"], 1)
            eng.wait_ge(sem["ksTp"], b + 1)
            eng.activation(ksT, ps[:, 6, :].rearrange("p (t n) -> p t n", t=TT), ACT.Copy).then_inc(sem["ksT"], 1)
            for t in range(TT):
                eng.wait_ge(sem["op"], b * TT + t + 1)
                if t:
                    eng.wait_ge(sem["ms"], b * TT + t)
                else:
                    eng.wait_ge(sem["ms"], b * TT)
                eng.activation(sq, ps[:, 4 + t % 2, 0:D], ACT.Square).then_inc(sem["sq"], 1)
                eng.wait_ge(sem["og"], b * TT + t)
                eng.activation(th, vg[:, t, D:2 * D], ACT.Tanh, scale=0.5).then_inc(sem["th"], 1)
            for k in range(KC):
                eng.wait_ge(sem["ogTp"], b * KC + k + 1)
                eng.activation(ogT[:, k, :], ps[:, k, :], ACT.Copy).then_inc(sem["ogT"], 1)
        repeat(eng, B, sequence)

    @block.tensor
    def _(eng):
        eng.wait_ge(s.const_in, 48)
        def sequence(b):
            for k in range(KC):
                for t in range(TT):
                    if k == 0:
                        eng.wait_ge(sem["xn"], b * TT + t + 1)
                    m = eng.transpose(ps[:, k, t * P:(t + 1) * P], xn[:, t, k * P:(k + 1) * P], c("ident"))
                m.then_inc(sem["xTp"], 1)
            eng.wait_ge(s.gla_w_in, s.gla_w_n)
            eng.wait_ge(sem["xT"], (b + 1) * KC)

            def project(bank, w, n, name):
                for k in range(KC):
                    m = eng.matmul(ps[0:n, bank, :], w[:, k, :], xT[:, k, :], start=k == 0, stop=k == KC - 1)
                m.then_inc(sem[name], 1)

            project(4, s.wgk1, LOW, "z1p")
            project(2, s.gwq, P, "qp")
            project(3, s.gwk, P, "kp")
            eng.wait_ge(sem["z1"], b + 1)
            eng.matmul(ps[:, 5, :], s.wgk2[0:LOW, :], z1T[0:LOW, :], start=True, stop=True).then_inc(sem["gkp"], 1)
            for t in range(TT):
                if t >= 2:
                    eng.wait_ge(sem["vg"], b * TT + t - 1)
                for k in range(KC):
                    m = eng.matmul(ps[:, 6 + t % 2, :], xT[:, k, t * P:(t + 1) * P], s.wvg[:, k, :],
                                   start=k == 0, stop=k == KC - 1)
                m.then_inc(sem["vgp"], 1)
            eng.wait_ge(sem["vg"], (b + 1) * TT)
            eng.wait_ge(sem["kst"], b + 1)
            for t in range(TT):
                m = eng.transpose(ps[:, 6, t * P:(t + 1) * P], ks[:, t, :], c("ident"))
            m.then_inc(sem["ksTp"], 1)
            eng.wait_ge(sem["qx"], b + 1)
            eng.wait_ge(sem["ksT"], b + 1)
            for t in range(TT):
                def scores(g):
                    n = (t * G + g)
                    if t:
                        eng.wait_ge(sem["att"], b * TT * G + n - G + 1)
                    for i, k in enumerate((ka, kb)):
                        m = eng.matmul(
                            ps[:, g, :].rearrange("p (j n) -> p j n", j=HPG)[:, :, i * SUB:(i + 1) * SUB],
                            k[32 * g:32 * g + 32, t, :], qx[32 * g:32 * g + 32, :, t, i * SUB:(i + 1) * SUB],
                            start=True, stop=True)
                    m.then_inc(sem["ap"], 1)

                scores(0)
                scores(1)
                ob = ps[:, 4 + t % 2, 0:D]
                if t >= 2:
                    eng.wait_ge(sem["og"], b * TT + t - 1)
                if t:
                    eng.wait_ge(sem["sadd"], b * (TT - 1) + t)
                    eng.matmul(ob, qi[:, t, :], state, start=True, stop=True, skip_group_check=True)
                if t < TT - 1:
                    eng.matmul(ps[:, 7, 0:D], ksT[:, t, :], vg[:, t, 0:D], start=True, stop=True).then_inc(sem["sp"], 1)
                for g in range(G):
                    eng.wait_ge(sem["att"], b * TT * G + t * G + g + 1)
                    for j in range(HPG):
                        h = g * HPG + j
                        m = eng.matmul(ob[:, h * DV:(h + 1) * DV], att[:, g % 2, j, :], vg[:, t, h * DV:(h + 1) * DV],
                                       start=t == 0, stop=True, skip_group_check=True)
                    m.then_inc(sem["y"], 1)
                    if g + 2 < G:
                        scores(g + 2)
                eng.wait_ge(sem["y"], b * TT * G + t * G + G)
                eng.sem_inc(sem["op"], 1)
            for k in range(KC):
                for t in range(TT):
                    if k == 0:
                        eng.wait_ge(sem["og"], b * TT + t + 1)
                    m = eng.transpose(ps[:, k, t * P:(t + 1) * P], og[:, t, k * P:(k + 1) * P], c("ident"))
                m.then_inc(sem["ogTp"], 1)
            eng.wait_ge(sem["ogT"], (b + 1) * KC)
            for t in range(TT):
                for k in range(KC):
                    m = eng.matmul(ps[:, 2 + t // 2, (t % 2) * D:(t % 2 + 1) * D], ogT[:, k, t * P:(t + 1) * P],
                                   s.gwo[:, k, :], start=k == 0, stop=k == KC - 1)
                if t % 2:
                    m.then_inc(sem["yp"], 1)
            eng.wait_ge(sem["h"], (b + 1) * 2)
        repeat(eng, B, sequence)

    @block.vector
    def _(eng):
        eng.wait_ge(s.const_in, 48)
        eng.memset(ka[:, :, SUB:P], 0.0).then_inc(sem["zeros"], 1)
        eng.wait_ge(sem["zeros"], 1)
        eng.wait_ge(s.vec_in, s.vec_n)
        o = Order(eng, sem["dve"])

        def sequence(b):
            hb = s.h[:, bass.ds(b * TT, TT), :]
            eng.wait_ge(s.rows_in[b], 16 * TT)
            o.after(eng.tensor_tensor(hb, hb, spread(s.tok_bias, 1, TT), ALU.add))
            for t in range(TT):
                eng.bn_stats(stats[:, t, :], s.h[:, bass.ds(b * TT + t, 1), :].rearrange("p a d -> p (a d)"))\
                   .then_inc(sem["dve"], 1)
                o.n += 1
            eng.wait_ge(sem["dve"], o.base + o.n)
            for t in range(TT):
                m = eng.bn_aggr(mv[:, t, :], stats[:, t, :])
                if t < TT - 1:
                    m.then_inc(sem["dve"], 1)
                    o.n += 1
            eng.wait_ge(sem["dve"], o.base + o.n)
            m.then_inc(sem["mv"], 1)
            eng.wait_ge(sem["mv"], b + 1)
            eng.wait_ge(sem["rstd"], b + 1)
            for t in range(TT):
                eng.tensor_scalar(xn[:, t, :], s.h[:, bass.ds(b * TT + t, 1), :].rearrange("p a d -> p (a d)"),
                                  mv[:, t, 0:1], rstd[:, t:t + 1], ALU.subtract, ALU.mult).then_inc(sem["xn"], 1)
            eng.wait_ge(sem["gkp"], b + 1)
            eng.tensor_scalar(zb, ps[:, 5, :], s.bgk2, None, ALU.add).then_inc(sem["zb"], 1)
            eng.wait_ge(sem["zb"], b + 1)
            eng.wait_ge(sem["lsig"], b + 1)
            o.after(eng.scalar_tensor_tensor(zb, zb, 0.0, e1, ALU.min, ALU.subtract))
            eng.tensor_tensor_scan(ls, c("subreset"), zb, 0.0, ALU.mult, ALU.add).then_inc(sem["ls"], 1)
            eng.wait_ge(sem["ls"], b + 1)
            ls_s = ls.rearrange("p (a n) -> p a n", n=SUB)
            eng.tensor_tensor(e_out.rearrange("p (a n) -> p a n", n=SUB),
                              ls_s[:, :, SUB - 1:SUB].broadcast_to([P, T // SUB, SUB]), ls_s,
                              ALU.subtract).then_inc(sem["dout"], 1)
            ei, ev, eo = (x.rearrange("p (t n) -> p t n", n=P) for x in (e_in, e_inv, e_out))
            eng.wait_ge(sem["exps"], (b + 1) * 3)
            eng.wait_ge(sem["qp"], b + 1)
            o.after(eng.scalar_tensor_tensor(qd, ps[:, 2, :].rearrange("p (t n) -> p t n", n=P), DK ** -0.5, ei,
                                             ALU.mult, ALU.mult))
            kp = ps[:, 3, :].rearrange("p (t n) -> p t n", n=P)
            lo, hi = slice(0, SUB), slice(SUB, P)
            eng.wait_ge(sem["kp"], b + 1)
            o.after(eng.tensor_tensor(ka[:, :, lo], kp[:, :, lo], ev[:, :, lo], ALU.mult))
            o.after(eng.tensor_tensor(kb[:, :, hi], kp[:, :, hi], ev[:, :, hi], ALU.mult))
            o.after(eng.tensor_tensor(kb[:, :, lo], kp[:, :, lo], eo[:, :, lo], ALU.mult))
            o.after(eng.tensor_tensor(ks[:, :, hi], kp[:, :, hi], eo[:, :, hi], ALU.mult))
            eng.tensor_tensor(ks[:, :, lo], kb[:, :, lo], ei[:, :, P - 1:P].broadcast_to([P, TT, SUB]),
                              ALU.mult).then_inc(sem["kst"], 1)
            o.after(eng.tensor_copy(qi[:, :, lo], qd[:, :, lo]))
            o.after(eng.tensor_tensor(qi[:, :, hi], qd[:, :, hi], ei[:, :, SUB - 1:SUB].broadcast_to([P, TT, SUB]),
                                      ALU.mult))
            o.after(eng.tensor_tensor(dec.unsqueeze(2), ei[:, :, SUB - 1:SUB], ei[:, :, P - 1:P], ALU.mult))
            for j in range(HPG):
                m = eng.tensor_scalar(qx[:, j, :, :], qd, c("headmask")[:, j:j + 1], None, ALU.mult)
                if j < HPG - 1:
                    o.after(m)
            m.then_inc(sem["qx"], 1)
            for t in range(TT):
                for g in range(G):
                    n = t * G + g
                    eng.wait_ge(sem["ap"], b * TT * G + n + 1)
                    if n >= 2:
                        eng.wait_ge(sem["y"], b * TT * G + n - 1)
                    eng.tensor_tensor(att[:, g % 2, :, :], ps[:, g, :].rearrange("p (j n) -> p j n", j=HPG),
                                      spread(c("upto"), 1, HPG), ALU.mult).then_inc(sem["att"], 1)
                    if g == 1 and t < TT - 1:
                        eng.wait_ge(sem["sp"], b * (TT - 1) + t + 1)
                        own = dstate if t else state
                        m = eng.tensor_tensor(own, ps[:, 7, 0:D], c("headblock"), ALU.mult)
                        if t:
                            o.after(m)
                            m = eng.scalar_tensor_tensor(state, state, dec[:, t:t + 1], dstate, ALU.mult, ALU.add)
                        m.then_inc(sem["sadd"], 1)
                        eng.wait_ge(sem["sadd"], b * (TT - 1) + t + 1)
                eng.wait_ge(sem["sq"], b * TT + t + 1)
                eng.tensor_reduce(ms, sq.rearrange("p (h d) -> p h d", h=H), AX.X, ALU.add).then_inc(sem["ms"], 1)
                eng.wait_ge(sem["th"], b * TT + t + 1)
                o.after(eng.scalar_tensor_tensor(og[:, t, :], th, 1.0, vg[:, t, D:2 * D], ALU.add, ALU.mult))
                o.after(eng.tensor_tensor(og[:, t, :], og[:, t, :], s.gnw_half, ALU.mult))
                eng.wait_ge(sem["rms"], b * TT + t + 1)
                hv = lambda a: a.rearrange("p (h d) -> p h d", h=H)
                o.after(eng.tensor_tensor(hv(og[:, t, :]), hv(og[:, t, :]), spread(rms, 2, DV), ALU.mult))
                eng.tensor_tensor(og[:, t, :], ps[:, 4 + t % 2, 0:D], og[:, t, :], ALU.mult).then_inc(sem["og"], 1)
            for i in range(2):
                eng.wait_ge(sem["yp"], b * 2 + i + 1)
                hh = s.h[:, bass.ds(b * TT + 2 * i, 2), :]
                eng.tensor_tensor(hh, hh, ps[:, 2 + i, :].rearrange("p (t d) -> p t d", t=2),
                                  ALU.add).then_inc(sem["h"], 1)
        repeat(eng, B, sequence)

def softmax_attention(nc, ctx, s):
    ar = Arena(s.scratch, s.scratch_words)
    x = ar.take(TT, D)
    n1 = ar.take(TT, D)
    n1T = ar.take(KC, T)
    qk = ar.take(2 * D)
    rot = ar.take(2 * D)
    sq = ar.take(TT, H, ST, dtype=F16)
    sk = ar.take(TT, H, ST, dtype=F16)
    qT = ar.take(H // 2, T, dtype=F16)
    kT = ar.take(H // 2, T, dtype=F16)
    va = ar.take(TT, VW)
    pT = ar.take(2, 10 * P)
    mx = ar.take(TT, H)
    rden = ar.take(TT, 4)
    stats, mv, rn = ar.take(TT, 6), ar.take(TT, 2), ar.take(2, TT)
    ssq, r2 = ar.take(TT), ar.take(TT)
    oT = n1T
    nT = n1T
    vh = va[:, :, 0:H * (HD + 1)].rearrange("p t (h d) -> p t h d", h=H)
    oq = rot
    stage = ar.take(2, HID)
    PER = 2 * X * KC // B
    heads = n1
    ps, c = s.psum, s.const
    at = {0: 0, 1: 4, 3: 7, 2: 8}
    block_of = lambda kt, qt: at[kt] + qt - kt
    names = ["mv", "rn", "n1", "n1Tp", "n1T", "qkp", "vp", "va", "rope", "hi", "stk", "sTp", "qT", "kT", "mp", "mx",
             "neg", "s2Tp", "q2T", "pp", "exp", "pv", "on", "oTp", "oT", "yp", "g", "ssq", "r2", "n2", "nTp",
             "nT", "lp", "lg", "qkr", "oq", "oqTp", "split", "w0", "w1", "dve", "act", "pool"]
    sem = {n: ctx.enter_context(nc.semaphore("att_" + n)) for n in names}
    block = ctx.enter_context(nc.Block())

    @block.gpsimd
    def _(eng):
        o = Order(eng, sem["pool"])

        def sequence(b):
            eng.wait_ge(sem["mv"], b + 1)
            eng.tensor_scalar(rn[:, 0, :], mv[:, :, 1], 1e-5, None, ALU.add).then_inc(sem["pool"], 1)
            eng.tensor_scalar(rn[:, 1, :], mv[:, :, 1], 1.0 + 1e-6, 1e-11, ALU.mult, ALU.add).then_inc(sem["pool"], 1)
            o.n += 2
            eng.wait_ge(sem["pool"], o.base + o.n)
            rf = rn.rearrange("p a t -> p (a t)")
            eng.tensor_tensor(rf, rf, c("powers")[:, 0:2 * TT], ALU.pow).then_inc(sem["rn"], 1)
            for n in range(PER):
                eng.wait_ge(sem[f"w{n % 2}"], 16 * (b * (PER // 2) + n // 2 + 1))
                w, w16, xk = stage[:, n % 2, :], (s.wg, s.wu)[n % 2], b * (PER // 2) + n // 2
                part = lambda i: w16[:, bass.ds(xk, 1), i, :].rearrange("p a n -> p (a n)")
                o.after(eng.tensor_scalar(w, w, W_SCALE, None, ALU.mult))
                o.after(eng.tensor_copy(part(0), w))
                eng.tensor_tensor(part(1), w, part(0), ALU.subtract).then_inc(sem["split"], 1)
            eng.wait_ge(sem["ssq"], (b + 1) * TT)
            o.after(eng.tensor_scalar(r2, ssq, 1.0 / D, 1e-6, ALU.mult, ALU.add))
            eng.tensor_tensor(r2, r2, c("powers")[:, 0:TT], ALU.pow).then_inc(sem["r2"], 1)

        repeat(eng, B, sequence)

    @block.sync
    def _(eng):
        def sequence(b):
            for n in range(PER):
                if b * PER + n >= 2:
                    eng.wait_ge(sem["split"], b * PER + n - 1)
                w, xk = s.wgu_dram[n % 2], b * (PER // 2) + n // 2
                eng.dma_start(stage[:, n % 2, :], w[bass.ds(xk, 1)].rearrange("a p n -> p (a n)"))\
                   .then_inc(sem[f"w{n % 2}"], 16)

        repeat(eng, B, sequence)

    @block.scalar
    def _(eng):
        o = Order(eng, sem["act"])

        def sequence(b):
            for k in range(KC):
                eng.wait_ge(sem["n1Tp"], b * KC + k + 1)
                eng.activation(n1T[:, k, :], ps[:, k, :], ACT.Copy).then_inc(sem["n1T"], 1)
            for t in range(TT):
                eng.wait_ge(sem["vp"], b * TT + t + 1)
                eng.activation(vh[:, t, :, 0:HD], ps[:, 4 + t % 2, 0:D].rearrange("p (h d) -> p h d", h=H),
                               ACT.Copy).then_inc(sem["va"], 1)
                eng.wait_ge(sem["rope"], b * TT + t + 1)
                hv = lambda a: a.rearrange("p (h d) -> p h d", h=H)
                two = lambda a: a.rearrange("p h (j d) -> p h j d", d=HD)
                eng.activation(two(sq[:, t, :, 0:2 * HD]), spread(hv(qk[:, 0:D]), 2, 2), ACT.Copy, scale=HD ** -0.5)\
                   .then_inc(sem["hi"], 1)
                eng.activation(two(sk[:, t, :, 0:3 * HD])[:, :, 0:3:2, :], spread(hv(qk[:, D:2 * D]), 2, 2), ACT.Copy)\
                   .then_inc(sem["hi"], 1)
                eng.wait_ge(sem["sTp"], b * TT + t + 1)
                eng.activation(qT[:, :, t * P:(t + 1) * P],
                               ps[:, 6, :].bitcast(F16).rearrange("p (a n) -> p a n", n=P), ACT.Copy)\
                   .then_inc(sem["qT"], 1)
            for t in range(TT):
                eng.wait_ge(sem["s2Tp"], b * TT + t + 1)
                eng.activation(qT[:, :, t * P:(t + 1) * P],
                               ps[:, 6 + t % 2, :].bitcast(F16).rearrange("p (a n) -> p a n", n=P), ACT.Copy)\
                   .then_inc(sem["q2T"], 1)
            for h in range(H):
                eng.wait_ge(sem["pp"], b * H + h + 1)
                if h >= 2:
                    eng.wait_ge(sem["pv"], b * H + h - 1)
                src = ps[:, 3 * (h % 2):3 * (h % 2) + 3, :].rearrange("p a n -> p (a n)")[:, 0:10 * P]
                eng.activation(pT[:, h % 2, :], src, ACT.Exp).then_inc(sem["exp"], 1)
            for k in range(KC):
                eng.wait_ge(sem["oTp"], b * KC + k + 1)
                eng.activation(oT[:, k, :], ps[:, k, :], ACT.Copy).then_inc(sem["oT"], 1)
            for t in range(TT):
                eng.wait_ge(sem["g"], b * 2 + t // 2 + 1)
                eng.activation(rot[:, 0:D], x[:, t, :], ACT.Square, accum_out=ssq[:, t:t + 1]).then_inc(sem["ssq"], 1)
                eng.wait_ge(sem["ssq"], b * TT + t + 1)
            for k in range(KC):
                eng.wait_ge(sem["nTp"], b * KC + k + 1)
                eng.activation(nT[:, k, :], ps[:, 4 + k, :], ACT.Copy).then_inc(sem["nT"], 1)

        repeat(eng, B, sequence)

    @block.tensor
    def _(eng):
        eng.wait_ge(s.att_w_in, s.att_w_n)

        def sequence(b):
            for k in range(KC):
                for t in range(TT):
                    if k == 0:
                        eng.wait_ge(sem["n1"], b * TT + t + 1)
                    m = eng.transpose(ps[:, k, t * P:(t + 1) * P], n1[:, t, k * P:(k + 1) * P], c("ident"))
                m.then_inc(sem["n1Tp"], 1)
            eng.wait_ge(sem["n1T"], (b + 1) * KC)
            def project(t):
                if t >= 2:
                    eng.wait_ge(sem["qkr"], b * TT + t - 1)
                    eng.wait_ge(sem["va"], b * TT + t - 1)
                for k in range(KC):
                    m = eng.matmul(ps[:, 2 + t % 2, :], n1T[:, k, t * P:(t + 1) * P], s.wqkv[:, k, 0:2 * D],
                                   start=k == 0, stop=k == KC - 1)
                m.then_inc(sem["qkp"], 1)
                for k in range(KC):
                    m = eng.matmul(ps[:, 4 + t % 2, 0:D], n1T[:, k, t * P:(t + 1) * P], s.wqkv[:, k, 2 * D:3 * D],
                                   start=k == 0, stop=k == KC - 1)
                m.then_inc(sem["vp"], 1)

            def stack_up(t):
                eng.wait_ge(sem["stk"], b * TT + t + 1)
                if t:
                    eng.wait_ge(sem["qT"], b * TT + t)
                    eng.wait_ge(sem["kT"], b * TT + t)
                for bank, stack in ((6, sq), (7, sk)):
                    for a in range(H // 2):
                        m = eng.transpose(ps[:, bank, a * 64:(a + 1) * 64].bitcast(F16),
                                          stack[:, t, 2 * a:2 * a + 2, :].rearrange("p h d -> p (h d)"), s.ident16)
                m.then_inc(sem["sTp"], 1)

            project(0)
            project(1)
            for t in range(TT):
                stack_up(t)
                if t + 2 < TT:
                    project(t + 2)
            eng.wait_ge(sem["kT"], (b + 1) * TT)
            eng.wait_ge(sem["qT"], (b + 1) * TT)
            eng.wait_ge(sem["va"], (b + 1) * TT)
            for t in range(TT):
                for a in range(H // 2):
                    n = t * (H // 2) + a
                    if n >= 3:
                        eng.wait_ge(sem["mx"], b * TT * (H // 2) + n - 2)
                    for r in range(2):
                        rows = slice(r * ST, (r + 1) * ST)
                        m = eng.matmul(ps[:, 2 * (n % 3) + r, 0:(t + 1) * P], qT[rows, a, t * P:(t + 1) * P],
                                       kT[rows, a, 0:(t + 1) * P], start=True, stop=True)
                    for r in range(2):
                        m = eng.matmul(ps[:, 2 * (n % 3) + r, t * P:(t + 1) * P], s.ident16, s.future_k,
                                       start=False, stop=True, skip_group_check=True)
                    m.then_inc(sem["mp"], 1)
            for t in range(TT):
                eng.wait_ge(sem["neg"], b * TT + t + 1)
                if t >= 2:
                    eng.wait_ge(sem["q2T"], b * TT + t - 1)
                for a in range(H // 2):
                    m = eng.transpose(ps[:, 6 + t % 2, a * 64:(a + 1) * 64].bitcast(F16),
                                      sq[:, t, 2 * a:2 * a + 2, :].rearrange("p h d -> p (h d)"), s.ident16)
                m.then_inc(sem["s2Tp"], 1)
            eng.wait_ge(sem["q2T"], (b + 1) * TT)
            eng.wait_ge(sem["mx"], (b + 1) * TT * (H // 2))

            def scores(h):
                rows = slice((h % 2) * ST, (h % 2 + 1) * ST)
                if h >= 2:
                    eng.wait_ge(sem["exp"], b * H + h - 1)
                spot = lambda kt, n: ps[:, 3 * (h % 2) + at[kt] // 4, at[kt] % 4 * P:(at[kt] % 4 + n) * P]
                for kt in range(TT):
                    eng.matmul(spot(kt, TT - kt), kT[rows, h // 2, kt * P:(kt + 1) * P], qT[rows, h // 2, kt * P:T],
                               start=kt != 3, stop=True, skip_group_check=True)
                for kt in range(TT):
                    m = eng.matmul(spot(kt, 1), s.ident16, s.future_q, start=False, stop=True, skip_group_check=True)
                m.then_inc(sem["pp"], 1)

            def queries_back(quad):
                eng.wait_ge(sem["oq"], b * 4 + quad + 1)
                if quad:
                    eng.wait_ge(sem["on"], b * 4 + quad)
                for t in range(TT):
                    m = eng.transpose(ps[:, 7, t * P:(t + 1) * P], oq[:, t * P:(t + 1) * P], c("ident"))
                m.then_inc(sem["oqTp"], 1)

            scores(0)
            scores(1)
            for h in range(H):
                eng.wait_ge(sem["exp"], b * H + h + 1)
                if h % 4 == 0 and h:
                    eng.wait_ge(sem["oq"], b * 4 + h // 4)
                j = h % 4
                for kt in range(TT):
                    m = eng.matmul(ps[32 * j:32 * j + 32, 6, kt * P:T], va[:, kt, h * (HD + 1):h * (HD + 1) + 32],
                                   pT[:, h % 2, at[kt] * P:(at[kt] + TT - kt) * P],
                                   start=kt == 0, stop=True, skip_group_check=True)
                m.then_inc(sem["pv"], 1)
                if h + 2 < H:
                    scores(h + 2)
                if j == 0 and h:
                    queries_back(h // 4 - 1)
            queries_back(3)
            eng.wait_ge(sem["on"], (b + 1) * 4)
            for k in range(KC):
                for t in range(TT):
                    m = eng.transpose(ps[:, k, t * P:(t + 1) * P], heads[:, t, k * P:(k + 1) * P], c("ident"))
                m.then_inc(sem["oTp"], 1)
            eng.wait_ge(sem["oT"], (b + 1) * KC)
            for t in range(TT):
                for k in range(KC):
                    m = eng.matmul(ps[:, 2 + t // 2, (t % 2) * D:(t % 2 + 1) * D], oT[:, k, t * P:(t + 1) * P],
                                   s.wo[:, k, :], start=k == 0, stop=k == KC - 1)
                if t % 2:
                    m.then_inc(sem["yp"], 1)
            for k in range(KC):
                for t in range(TT):
                    if k == 0:
                        eng.wait_ge(sem["n2"], b * TT + t + 1)
                    m = eng.transpose(ps[:, 4 + k, t * P:(t + 1) * P],
                                      s.n2[:, nds(b * TT + t), k * P:(k + 1) * P].rearrange("p a d -> p (a d)"),
                                      c("ident"))
                m.then_inc(sem["nTp"], 1)
            eng.wait_ge(sem["nT"], (b + 1) * KC)
            for t in range(TT):
                for k in range(KC):
                    m = eng.matmul(ps[:, 6, t * X:(t + 1) * X], nT[:, k, t * P:(t + 1) * P], s.wr[:, k, :],
                                   start=k == 0, stop=k == KC - 1)
            m.then_inc(sem["lp"], 1)
            eng.wait_ge(sem["lg"], b + 1)

        repeat(eng, B, sequence)

    @block.vector
    def _(eng):
        eng.wait_ge(s.att_w_in, s.att_w_n - 1)
        o = Order(eng, sem["dve"])
        for k in range(KC):
            m = eng.tensor_scalar(s.wqkv[:, k, :], s.wqkv[:, k, :], s.g1[:, k:k + 1], None, ALU.mult)
            if k < KC - 1:
                o.after(m)
        m.then_inc(s.att_w_in, 1)
        o.after(eng.memset(sq[:, :, :, 3 * HD:ST], 0.0))
        o.after(eng.memset(sk[:, :, :, 3 * HD:ST], 0.0))
        o.after(eng.memset(sk[:, :, :, 3 * HD:3 * HD + 1], 1.0))
        o.after(eng.memset(va[:, :, H * (HD + 1):VW], 0.0))
        o.after(eng.memset(vh[:, :, :, HD:HD + 1], 1.0))

        def sequence(b):
            row = lambda t: s.h[:, nds(b * TT + t), :].rearrange("p a d -> p (a d)")
            for t in range(TT):
                eng.bn_stats(stats[:, t, :], row(t)).then_inc(sem["dve"], 1)
            o.n += TT
            eng.wait_ge(sem["dve"], o.base + o.n)
            for t in range(TT):
                m = eng.bn_aggr(mv[:, t, :], stats[:, t, :])
                if t < TT - 1:
                    m.then_inc(sem["dve"], 1)
            o.n += TT - 1
            m.then_inc(sem["mv"], 1)
            eng.wait_ge(sem["mv"], b + 1)
            eng.wait_ge(sem["dve"], o.base + o.n)
            eng.wait_ge(sem["rn"], b + 1)
            for t in range(TT):
                o.after(eng.tensor_scalar(x[:, t, :], row(t), mv[:, t, 0:1], rn[:, 0, t:t + 1], ALU.subtract, ALU.mult))
                eng.tensor_scalar(n1[:, t, :], row(t), mv[:, t, 0:1], rn[:, 1, t:t + 1], ALU.subtract, ALU.mult)\
                   .then_inc(sem["n1"], 1)
            v3 = lambda a: a.rearrange("p (h d) -> p h d", d=HD)
            half = HD // 2
            for t in range(TT):
                eng.wait_ge(sem["qkp"], b * TT + t + 1)
                if t:
                    eng.wait_ge(sem["hi"], b * TT * 2 + 2 * t)
                else:
                    eng.wait_ge(sem["hi"], b * TT * 2)
                qkp = v3(ps[:, 2 + t % 2, :])
                cos, sin = (c(n)[:, t * HD:(t + 1) * HD] for n in ("cos", "sin"))
                o.after(eng.tensor_tensor(v3(qk), qkp, spread(cos, 1, 2 * H), ALU.mult))
                o.after(eng.tensor_tensor(v3(rot)[:, :, 0:half], qkp[:, :, half:HD], spread(sin[:, 0:half], 1, 2 * H),
                                          ALU.mult))
                eng.tensor_tensor(v3(rot)[:, :, half:HD], qkp[:, :, 0:half], spread(sin[:, half:HD], 1, 2 * H),
                                  ALU.mult).then_inc(sem["qkr"], 1)
                eng.wait_ge(sem["qkr"], b * TT + t + 1)
                eng.tensor_tensor(qk, qk, rot, ALU.add).then_inc(sem["rope"], 1)
                eng.wait_ge(sem["rope"], b * TT + t + 1)
                o.after(eng.memset(sq[:, t, :, 3 * HD:3 * HD + 1], 0.0))
                eng.wait_ge(sem["hi"], (b * TT + t) * 2 + 2)
                o.after(eng.scalar_tensor_tensor(sq[:, t, :, 2 * HD:3 * HD], v3(qk[:, 0:D]), HD ** -0.5,
                                                 sq[:, t, :, 0:HD], ALU.mult, ALU.subtract))
                eng.tensor_tensor(sk[:, t, :, HD:2 * HD], v3(qk[:, D:2 * D]), sk[:, t, :, 0:HD], ALU.subtract)\
                   .then_inc(sem["stk"], 1)
                eng.wait_ge(sem["stk"], b * TT + t + 1)
                eng.wait_ge(sem["sTp"], b * TT + t + 1)
                eng.tensor_copy(kT[:, :, t * P:(t + 1) * P],
                                ps[:, 7, :].bitcast(F16).rearrange("p (a n) -> p a n", n=P)).then_inc(sem["kT"], 1)
            for t in range(TT):
                for a in range(H // 2):
                    n = t * (H // 2) + a
                    eng.wait_ge(sem["mp"], b * TT * (H // 2) + n + 1)
                    eng.tensor_reduce(mx[:, t, 2 * a:2 * a + 2], ps[:, 2 * (n % 3):2 * (n % 3) + 2, 0:(t + 1) * P], AX.X,
                                      ALU.max).then_inc(sem["mx"], 1)
                eng.wait_ge(sem["mx"], b * TT * (H // 2) + (t + 1) * (H // 2))
                eng.tensor_scalar(sq[:, t, :, 3 * HD:3 * HD + 1], mx[:, t, :].unsqueeze(2), -1.0, None, ALU.mult)\
                   .then_inc(sem["neg"], 1)
            for quad in range(4):
                eng.wait_ge(sem["pv"], b * H + 4 * quad + 4)
                eng.tensor_copy(oq, ps[:, 6, :]).then_inc(sem["oq"], 1)
                eng.wait_ge(sem["oqTp"], b * 4 + quad + 1)
                out = ps[:, 7, :].rearrange("p (t h d) -> p t h d", t=TT, h=4)
                o.after(eng.reciprocal(rden.unsqueeze(3), out[:, :, :, HD:HD + 1]))
                hq = heads[:, :, quad * 4 * HD:(quad + 1) * 4 * HD].rearrange("p t (h d) -> p t h d", h=4)
                for t in range(TT):
                    m = eng.tensor_tensor(hq[:, t], out[:, t, :, 0:HD], spread(rden[:, t, :], 2, HD), ALU.mult)
                    if t < TT - 1:
                        o.after(m)
                m.then_inc(sem["on"], 1)
                eng.wait_ge(sem["on"], b * 4 + quad + 1)
            for i in range(2):
                eng.wait_ge(sem["yp"], b * 2 + i + 1)
                eng.tensor_tensor(x[:, 2 * i:2 * i + 2, :], x[:, 2 * i:2 * i + 2, :],
                                  ps[:, 2 + i, :].rearrange("p (t d) -> p t d", t=2), ALU.add).then_inc(sem["g"], 1)
            hb = s.h[:, bass.ds(b * TT, TT), :]
            eng.wait_ge(sem["g"], (b + 1) * 2)
            o.after(eng.tensor_tensor(hb, hb, x, ALU.add))
            eng.wait_ge(sem["r2"], b + 1)
            eng.wait_ge(s.rows_zeroed, 16)
            for t in range(TT):
                eng.scalar_tensor_tensor(s.n2[:, nds(b * TT + t), :].rearrange("p a d -> p (a d)"), x[:, t, :],
                                         r2[:, t:t + 1], s.g2, ALU.mult, ALU.mult).then_inc(sem["n2"], 1)
            eng.wait_ge(sem["lp"], b + 1)
            eng.tensor_copy(s.logits[:, bass.ds(b * TT, TT), :],
                            ps[:, 6, 0:TT * X].rearrange("p (t e) -> p t e", e=X)).then_inc(sem["lg"], 1)

        repeat(eng, B, sequence)


def routing(nc, ctx, s):
    ar = Arena(s.scratch, s.scratch_words)
    ar.at = s.wd_words
    stage = ar.take(DQ, DC, D)
    tx = lambda: ar.take(NT, X)
    eq, one1, one2, lg2, both, pref, tot = (tx() for _ in range(7))
    m1, m2, pick, w1s, w2s = (ar.take(NT) for _ in range(5))
    incl, excl, tot_e = ar.take(X, NT), ar.take(X, NT), ar.take(X, NT)
    n_t, end_t = ar.take(X), ar.take(X)
    slot = ar.take(2, NT)
    cmp_t, own = ar.take(XT, X), ar.take(XT)
    tiles_i = ar.tensor[:, ar.at:ar.at + X].bitcast(I32)
    ps, c = s.psum, s.const
    names = ["both", "cnt", "slots", "e", "we", "dve", "pad", "wd0", "wd1", "wd2", "hi", "lo"]
    sem = {n: ctx.enter_context(nc.semaphore("route_" + n)) for n in names}
    block = ctx.enter_context(nc.Block())

    @block.vector
    def _(eng):
        o = Order(eng, sem["dve"])
        eng.memset(stage[HC[-1][1]:P, DQ - 1, DC - 1, :], 0.0).then_inc(sem["pad"], 1)

        def first_of_the_largest(values, top, onehot):
            o.after(eng.tensor_reduce(top, values, AX.X, ALU.max))
            o.after(eng.tensor_tensor(eq, values, spread(top, 2, X), ALU.is_equal))
            o.after(eng.tensor_tensor(eq, eq, spread(c("rank8"), 1, NT), ALU.mult))
            o.after(eng.tensor_reduce(pick, eq, AX.X, ALU.max))
            o.after(eng.tensor_tensor(onehot, eq, spread(pick, 2, X), ALU.is_equal))

        lg = s.logits[:, :, :]
        first_of_the_largest(lg, m1, one1)
        o.after(eng.scalar_tensor_tensor(lg2, one1, -3e38, lg, ALU.mult, ALU.add))
        first_of_the_largest(lg2, m2, one2)
        eng.tensor_tensor(both, one1, one2, ALU.add).then_inc(sem["both"], 1)
        eng.tensor_tensor(w2s, m2, m1, ALU.subtract).then_inc(sem["e"], 1)
        eng.wait_ge(sem["we"], 1)
        o.after(eng.tensor_scalar(w1s, w2s, 1.0, None, ALU.add))
        o.after(eng.reciprocal(s.w[:, 0, :], w1s))
        o.after(eng.tensor_tensor(s.w[:, 1, :], w2s, s.w[:, 0, :], ALU.mult))
        eng.wait_ge(sem["cnt"], 1)
        o.after(eng.tensor_copy(pref, ps[:, 0, 0:NT * X].rearrange("p (t e) -> p t e", e=X)))
        o.after(eng.tensor_copy(tot_e, ps[:, 1, 0:NT * X].rearrange("p (t e) -> p e t", e=X)))
        o.after(eng.tensor_tensor_scan(incl.rearrange("p e t -> p (e t)"), c("ereset"),
                                       tot_e.rearrange("p e t -> p (e t)"), 0.0, ALU.mult, ALU.add))
        o.after(eng.tensor_tensor(excl, incl, tot_e, ALU.subtract))
        o.after(eng.tensor_scalar(tiles_i, incl[:, :, NT - 1], P - 1.0, None, ALU.add))
        o.after(eng.tensor_scalar(tiles_i, tiles_i, 7, None, ALU.arith_shift_right))
        o.after(eng.tensor_copy(n_t, tiles_i))
        o.after(eng.tensor_tensor_scan(end_t, c("ones")[:, 0:X], n_t, 0.0, ALU.mult, ALU.add))
        o.after(eng.tensor_tensor(cmp_t, spread(end_t, 1, XT), spread(c("tileno"), 2, X), ALU.is_le))
        o.after(eng.tensor_reduce(own, cmp_t, AX.X, ALU.add))
        o.after(eng.tensor_scalar(s.expert[:, :], own, X - 1.0, None, ALU.min))
        o.after(eng.tensor_tensor(n_t, end_t, n_t, ALU.subtract))
        o.after(eng.tensor_scalar(n_t, n_t, float(P), None, ALU.mult))
        o.after(eng.tensor_tensor(excl, excl, spread(n_t, 2, NT), ALU.add))
        o.after(eng.tensor_tensor(pref, pref, excl.rearrange("p e t -> p t e"), ALU.add))
        for i, onehot in enumerate((one1, one2)):
            o.after(eng.tensor_tensor(lg2, onehot, pref, ALU.mult))
            o.after(eng.tensor_reduce(slot[:, i, :], lg2, AX.X, ALU.add))
        eng.tensor_copy(s.slots[:, :, :], slot).then_inc(sem["slots"], 1)
        for n in range(X * DQ):
            eng.wait_ge(sem["hi"], n + 1)
            eng.scalar_tensor_tensor(s.wd[:, n * DC:(n + 1) * DC, 1, :], stage[:, n % DQ, :, :], W_SCALE,
                                     s.wd[:, n * DC:(n + 1) * DC, 0, :], ALU.mult, ALU.subtract).then_inc(sem["lo"], 1)

    @block.scalar
    def _(eng):
        eng.wait_ge(sem["e"], 1)
        eng.activation(w2s, w2s, ACT.Exp).then_inc(sem["we"], 1)
        for n in range(X * DQ):
            eng.wait_ge(sem[f"wd{n % DQ}"], 16 * DC * (n // DQ + 1))
            eng.activation(s.wd[:, n * DC:(n + 1) * DC, 0, :], stage[:, n % DQ, :, :], ACT.Copy, scale=W_SCALE)\
               .then_inc(sem["hi"], 1)

    @block.tensor
    def _(eng):
        eng.wait_ge(sem["both"], 1)
        rhs = both.rearrange("p t e -> p (t e)")
        eng.matmul(ps[:, 0, 0:NT * X], c("before"), rhs, start=True, stop=True)
        eng.matmul(ps[:, 1, 0:NT * X], c("ones"), rhs, start=True, stop=True).then_inc(sem["cnt"], 1)

    @block.sync
    def _(eng):
        eng.wait_ge(sem["pad"], 1)
        for n in range(X * DQ):
            x, q = divmod(n, DQ)
            if n >= DQ:
                eng.wait_ge(sem["lo"], n - DQ + 1)
            for i in range(DC):
                h0, size = HC[q * DC + i]
                eng.dma_start(stage[0:size, q, i, :], s.wd_dram[x, h0:h0 + size, :]).then_inc(sem[f"wd{q}"], 16)

    @block.gpsimd
    def _(eng):
        eng.wait_ge(s.rows_zeroed, 16)
        eng.wait_ge(sem["slots"], 1)
        for t in range(NT):
            for i in range(TOP):
                eng.indirect_dma_start(
                    out=s.rows, out_offset=bass.IndirectOffsetOnAxis(ap=s.slots[:, i, t:t + 1], axis=0),
                    in_=s.n2[:, t, :], in_offset=None).then_inc(s.rows_out, 16)
        eng.wait_ge(s.rows_out, 16 * NT * TOP)


def experts(nc, ctx, s):
    ar = Arena(s.scratch, s.scratch_words)
    ar.at = s.wd_words
    xin = ar.take(2, D)
    hid = ar.take(2, HID)
    y = ar.take(2, D)
    xT = ar.take(2, 2, KC, P, dtype=F16)
    hT = ar.take(2, len(HC), P, dtype=F16)
    HH = HID // 2
    PRODUCTS = ((0, 0), (0, 1), (1, 0))
    ps, c = s.psum, s.const
    names = ["x0", "x1", "xTp", "xTh", "xT", "gp", "sil", "hid", "hTp", "hTh", "lo4", "hT", "yp", "y", "out0", "out1"]
    sem = {n: ctx.enter_context(nc.semaphore("exp_" + n)) for n in names}
    block = ctx.enter_context(nc.Block())
    rows = lambda dram, j: dram[bass.ds(j * P, P), :]

    def turns(tile, eng):
        for j in range(3):
            tile(j, j % 2, (j + 1) // 2 + 1, first=j == 0)
        pairs = (XT - 5) // 2
        with eng.Fori(0, pairs) as i:
            tile(2 * i + 3, 1, i + 3)
            tile(2 * i + 4, 0, i + 3)
        for j in range(2 * pairs + 3, XT):
            tile(j, j % 2, (j + 1) // 2 + 1, last=j == XT - 1)

    @block.sync
    def _(eng):
        for r in range(2):
            eng.dma_start(xin[:, r, :], rows(s.rows, r)).then_inc(sem[f"x{r}"], 16)

        def tile(j, r, nth, first=False, last=False):
            if not (isinstance(j, int) and j + 2 >= XT):
                eng.wait_ge(sem["xTp"], j + 1)
                eng.dma_start(xin[:, r, :], rows(s.rows, j + 2)).then_inc(sem[f"x{r}"], 16)
            eng.wait_ge(sem["y"], j + 1)
            eng.dma_start(rows(s.results, j), y[:, r, :]).then_inc(sem[f"out{r}"], 16)

        turns(tile, eng)
        for r in range(2):
            eng.wait_ge(sem[f"out{r}"], 16 * ((XT + 1 - r) // 2))

    @block.tensor
    def _(eng):
        def load(r, nth):
            eng.wait_ge(sem[f"x{r}"], 16 * nth)
            for k in range(KC):
                m = eng.transpose(ps[:, 6, k * P:(k + 1) * P], xin[:, r, k * P:(k + 1) * P], c("ident"))
            m.then_inc(sem["xTp"], 1)

        def down(j, e, first=False):
            eng.wait_ge(sem["hT"], j + 1)
            if not first:
                eng.wait_ge(sem["y"], j)
            n = 0
            for q, (_, size) in enumerate(HC):
                for a, b in PRODUCTS:
                    n += 1
                    m = eng.matmul(ps[:, 7, 0:D], hT[0:size, a, q, :],
                                   s.wd[0:size, bass.ds(e * len(HC) + q, 1), b, :].rearrange("p a n -> p (a n)"),
                                   start=n == 1, stop=n == 3 * len(HC))
            m.then_inc(sem["yp"], 1)

        def expert(j):
            return eng.value_load(s.expert[0:1, bass.ds(j, 1)], min_val=0, max_val=X - 1)

        def tile(j, r, nth, first=False, last=False):
            e = expert(j)
            if first:
                load(0, 1)
            eng.wait_ge(sem["xT"], j + 1)
            for u in range(2):
                if not first:
                    eng.wait_ge(sem["hid"], 2 * j - 1 + u)
                for which, w in enumerate((s.wg, s.wu)):
                    n = 0
                    for k in range(KC):
                        for a, b in PRODUCTS:
                            n += 1
                            m = eng.matmul(ps[:, 2 * u + which, 0:HH], xT[:, r, a, k, :],
                                           w[:, bass.ds(e * KC + k, 1), b, u * HH:(u + 1) * HH]
                                           .rearrange("p a n -> p (a n)"), start=n == 1, stop=n == 3 * KC)
                m.then_inc(sem["gp"], 1)
            if not last:
                load(1 - r, nth)
            if not first:
                down(j - 1, expert(j - 1), first=isinstance(j, int) and j == 1)
            eng.wait_ge(sem["hid"], 2 * j + 2)
            for q, (h0, n) in enumerate(HC):
                m = eng.transpose(ps[0:n, 4 + q // 4, (q % 4) * P:(q % 4 + 1) * P], hid[:, r, h0:h0 + n], c("ident"))
            m.then_inc(sem["hTp"], 1)
            if last:
                down(j, e)

        turns(tile, eng)

    full = HID // P
    rest = HC[-1][1]
    chunk = lambda n: ps[:, 4:6, :].rearrange("p a (q n) -> p (a q) n", n=P)[:, 0:n, :]

    @block.scalar
    def _(eng):
        def x_high(j, r):
            eng.wait_ge(sem["xTp"], j + 1)
            eng.activation(xT[:, r, 0, :, :], ps[:, 6, 0:D].rearrange("p (k n) -> p k n", k=KC), ACT.Copy)\
               .then_inc(sem["xTh"], 1)

        def tile(j, r, nth, first=False, last=False):
            if first:
                x_high(0, 0)
            for u in range(2):
                eng.wait_ge(sem["gp"], 2 * j + u + 1)
                eng.activation(hid[:, r, u * HH:(u + 1) * HH], ps[:, 2 * u, 0:HH], ACT.Silu, scale=1 / W_SCALE)\
                   .then_inc(sem["sil"], 1)
            if not last:
                x_high(j + 1, 1 - r)
            eng.wait_ge(sem["hTp"], j + 1)
            if not first:
                eng.wait_ge(sem["yp"], j)
            eng.activation(hT[:, 0, 0:full, :], chunk(full), ACT.Copy).then_inc(sem["hTh"], 1)
            eng.activation(hT[0:rest, 0, full, :], chunk(full + 1)[0:rest, full, :], ACT.Copy).then_inc(sem["hTh"], 1)

        turns(tile, eng)

    @block.vector
    def _(eng):
        def x_low(j, r):
            eng.wait_ge(sem["xTh"], j + 1)
            eng.tensor_tensor(xT[:, r, 1, :, :], ps[:, 6, 0:D].rearrange("p (k n) -> p k n", k=KC), xT[:, r, 0, :, :],
                              ALU.subtract).then_inc(sem["xT"], 1)

        def result(j, r, stored):
            eng.wait_ge(sem["yp"], j + 1)
            if not isinstance(stored, int) or stored > 0:
                eng.wait_ge(sem[f"out{r}"], 16 * stored)
            eng.tensor_scalar(y[:, r, :], ps[:, 7, 0:D], 1 / W_SCALE, None, ALU.mult).then_inc(sem["y"], 1)

        def tile(j, r, nth, first=False, last=False):
            if first:
                x_low(0, 0)
            for u in range(2):
                eng.wait_ge(sem["sil"], 2 * j + u + 1)
                half = hid[:, r, u * HH:(u + 1) * HH]
                eng.scalar_tensor_tensor(half, ps[:, 2 * u + 1, 0:HH], 1 / W_SCALE, half, ALU.mult, ALU.mult)\
                   .then_inc(sem["hid"], 1)
            if not last:
                x_low(j + 1, 1 - r)
            if not first:
                result(j - 1, 1 - r, nth - 2)
            eng.wait_ge(sem["hTh"], 2 * j + 2)
            eng.tensor_tensor(hT[:, 1, 0:full, :], chunk(full), hT[:, 0, 0:full, :], ALU.subtract)\
               .then_inc(sem["lo4"], 1)
            eng.tensor_tensor(hT[0:rest, 1, full, :], chunk(full + 1)[0:rest, full, :], hT[0:rest, 0, full, :],
                              ALU.subtract).then_inc(sem["hT"], 1)
            if last:
                result(j, r, j // 2)

        turns(tile, eng)


def combine(nc, ctx, s, out):
    ar = Arena(s.scratch, s.scratch_words)
    got = ar.take(NT * TOP, D)
    names = ["y"]
    sem = {n: ctx.enter_context(nc.semaphore("comb_" + n)) for n in names}
    back = [ctx.enter_context(nc.semaphore(f"comb_back{i}")) for i in range(NT)]
    done = ctx.enter_context(nc.semaphore("comb_done"))
    block = ctx.enter_context(nc.Block())
    out_t = out.rearrange("(t p) d -> p t d", p=P)

    @block.gpsimd
    def _(eng):
        for t in range(NT):
            for i in range(TOP):
                eng.indirect_dma_start(
                    out=got[:, t * TOP + i, :], out_offset=None, in_=s.results,
                    in_offset=bass.IndirectOffsetOnAxis(ap=s.slots[:, i, t:t + 1], axis=0)).then_inc(back[t], 16)

    @block.vector
    def _(eng):
        for t in range(NT):
            eng.wait_ge(back[t], 16 * TOP)
            for i in range(TOP):
                m = eng.scalar_tensor_tensor(s.h[:, t, :], got[:, t * TOP + i, :], s.w[:, i, t:t + 1], s.h[:, t, :],
                                             ALU.mult, ALU.add)
                m.then_inc(sem["y"], 1)
                eng.wait_ge(sem["y"], t * TOP + i + 1)

    @block.sync
    def _(eng):
        for t in range(0, NT, 2):
            eng.wait_ge(sem["y"], (t + 2) * TOP)
            eng.dma_start(out_t[:, t:t + 2, :], s.h[:, t:t + 2, :]).then_inc(done, 16)
        eng.wait_ge(done, 16 * NT // 2)


class Shared:
    pass


def build(nc, a, out):
    s = Shared()
    with ExitStack() as ctx:
        sb = lambda name, shape, dt=F32: ctx.enter_context(nc.sbuf_tensor(name, shape, dt))
        sem = lambda name: ctx.enter_context(nc.semaphore(name))
        s.psum = ctx.enter_context(nc.psum_tensor("psum", [P, 8, 512], F32))
        s.h = sb("h", [P, NT, D])
        s.scratch_words = 17536
        s.scratch = sb("scratch", [P, s.scratch_words])
        s.junk = sb("junk", [P, 4])
        tables = {}

        def table_views(tile, packed_tables):
            for name, (at, n) in packed_tables[1].items():
                tables[name] = tile[:, at:at + n]

        const = sb("const", [P, CONST[0].shape[1]])
        const_half = sb("const_half", [P, CONST_HALF[0].shape[1]], F16)
        table_views(const, CONST)
        table_views(const_half, CONST_HALF)
        s.const = lambda name: tables[name]
        s.ids = sb("ids", [P, NT], I32)
        s.table = a["table"]
        s.n2 = sb("n2", [P, NT, D])
        w3 = lambda name, n: sb(name, [P, KC, n])
        early = Arena(s.n2[:, :, :].rearrange("p t d -> p (t d)"), NT * D)
        s.gwq, s.gwk, s.wgk1, s.wvg, s.gwo = (early.take(KC, n) for n in (P, P, LOW, 2 * D, D))
        s.wgk2 = early.take(P)
        s.wg, s.wu = (sb(n, [P, X * KC, 2, HID], F16) for n in ("w_gate", "w_up"))
        s.wd_words = X * len(HC) * D
        s.wd = s.scratch[:, 0:s.wd_words].bitcast(F16).rearrange("p (q a n) -> p q a n", a=2, n=D)
        s.wgu_dram = [a[n].rearrange("x (k p) n -> (x k) p n", p=P) for n in ("wg", "wu")]
        s.wd_dram = a["wd"]
        sem_zero = sem("zero_set")
        s.rows = nc.dram_tensor("rows", [ROWS, D], F32).ap()
        s.results = nc.dram_tensor("results", [ROWS, D], F32).ap()
        s.slots, s.expert = sb("slots", [P, TOP, NT], I32), sb("expert", [P, XT], I32)
        w_choice = sb("w_choice", [P, TOP, NT]); s.w = w_choice[:, :, :]
        s.rows_out, s.rows_zeroed = sem("rows_out"), sem("rows_zeroed")
        s.tok_bias, s.gnw_half, zero = (early.take(D) for _ in range(3))
        const_first = early.take(CONST_FIRST[0].shape[1])
        table_views(const_first, CONST_FIRST)
        s.bgk2_t = sb("bgk2", [P, 1]); s.bgk2 = s.bgk2_t[:, :]
        gnw = sb("gnw", [P, DV])
        s.ids_in, s.const_in, s.gla_w_in, s.vec_in = sem("ids_in"), sem("const_in"), sem("gla_w_in"), sem("vec_in")
        s.rows_in = [sem(f"rows_in{b}") for b in range(B)]
        s.gla_w_n, s.vec_n = 16 * 7, 16 * 3 + 1
        s.logits = sb("logits", [P, NT, X])
        s.wqkv, s.wo, s.wr = w3("wqkv", 3 * D), w3("wo", D), w3("wr", X)
        s.g1_t = sb("g1", [P, KC]); s.g1 = s.g1_t[:, :]
        s.g2_t = sb("g2", [P, D]); s.g2 = s.g2_t[:, :]
        s.ident16, s.future_k, s.future_q = (tables[n] for n in ("ident16", "future_k", "future_q"))
        s.att_w_in = sem("att_w_in")
        s.att_w_n = 16 * 7 + 1
        block = nc.Block()
        with block:
            @block.sync
            def _(eng):
                eng.dma_start(s.ids[:, :], a["ids"]).then_inc(s.ids_in, 16)
                for tile, name in ((const[:, :], "const"), (const_first, "const_first"), (const_half[:, :], "const_half")):
                    eng.dma_start(tile, a[name]).then_inc(s.const_in, 16)
                eng.dma_start(s.tok_bias, a["tok_bias"].partition_broadcast(P)).then_inc(s.vec_in, 16)
                kc = lambda name: a[name].rearrange("(k p) n -> p k n", p=P)
                eng.dma_start(s.gwq[:, :, :], kc("Wq")).then_inc(s.gla_w_in, 16)
                eng.dma_start(s.gwk[:, :, :], kc("Wk")).then_inc(s.gla_w_in, 16)
                eng.dma_start(s.wgk1[:, :, :], kc("Wgk1")).then_inc(s.gla_w_in, 16)
                eng.dma_start(s.wgk2[0:LOW, :], a["Wgk2"]).then_inc(s.gla_w_in, 16)
                eng.dma_start(s.wvg[:, :, 0:D], kc("Wv")).then_inc(s.gla_w_in, 16)
                eng.dma_start(s.wvg[:, :, D:2 * D], kc("Wg")).then_inc(s.gla_w_in, 16)
                eng.dma_start(s.gwo[:, :, :], kc("Wo")).then_inc(s.gla_w_in, 16)
                for i, name in enumerate(("wq", "wk", "wv")):
                    eng.dma_start(s.wqkv[:, :, i * D:(i + 1) * D], kc(name)).then_inc(s.att_w_in, 16)
                eng.dma_start(s.wo[:, :, :], kc("wo")).then_inc(s.att_w_in, 16)
                eng.dma_start(s.wr[:, :, :], kc("w_router")).then_inc(s.att_w_in, 16)
                eng.dma_start(s.g1, a["g1"]).then_inc(s.att_w_in, 16)
                eng.dma_start(s.g2, a["g2"].partition_broadcast(P)).then_inc(s.att_w_in, 16)
                eng.dma_start(s.bgk2, a["bgk2"]).then_inc(s.vec_in, 16)
                eng.dma_start(gnw[:, :], a["gnw"].partition_broadcast(P)).then_inc(s.vec_in, 16)

                eng.wait_ge(sem_zero, 1)
                eng.dma_start(s.rows.rearrange("(j p) d -> p j d", p=P), spread(zero, 1, XT)).then_inc(s.rows_zeroed, 16)

            @block.vector
            def _(eng):
                eng.memset(s.junk[:, :], 0.0)
                eng.memset(zero, 0.0).then_inc(sem_zero, 1)
                eng.wait_ge(s.vec_in, 48)
                eng.tensor_scalar(s.gnw_half.rearrange("p (h d) -> p h d", h=H), spread(gnw[:, :], 1, H), 0.5, None,
                                  ALU.mult).then_inc(s.vec_in, 1)
        with ExitStack() as stage:
            linear_attention(nc, stage, s)
        with ExitStack() as stage:
            softmax_attention(nc, stage, s)
        with ExitStack() as stage:
            routing(nc, stage, s)
        with ExitStack() as stage:
            experts(nc, stage, s)
        with ExitStack() as stage:
            combine(nc, stage, s, out)


def kernel(**inputs):
    import concourse.bacc as bacc
    from concourse.bass_utils import run_bass_kernel_spmd as run

    src = {
        "ids": inputs["x"].reshape(NT, P).T,
        "table": inputs["L0_tok_weight"].T,
        "tok_bias": inputs["L0_tok_bias"],
        "const": CONST[0],
        "const_first": CONST_FIRST[0],
        "const_half": CONST_HALF[0],
    }
    for n in ("Wq", "Wk", "Wv", "Wgk1", "Wgk2", "bgk2", "Wg", "gnw", "Wo"):
        src[n] = inputs["L0_attn_" + n]
    for n in ("wq", "wk", "wv", "wo", "w_router", "g1", "g2", "wg", "wu", "wd"):
        src[n] = inputs["L0_ffn_" + n]
    src["g1"] = src["g1"].reshape(KC, P).T
    src["bgk2"] = src["bgk2"].reshape(P, 1)
    nc = bacc.Bacc("TRN2", target_bir_lowering=False, num_devices=1)
    arrays, aps = {}, {}
    for name, v in src.items():
        v = np.ascontiguousarray(v)
        arrays["in_" + name] = v
        aps[name] = nc.dram_tensor("in_" + name, list(v.shape), mybir.dt.from_np(v.dtype), kind="ExternalInput").ap()
    out = nc.dram_tensor("out_y", [NT * P, D], F32, kind="ExternalOutput").ap()
    build(nc, aps, out)
    r = run(nc, [arrays], core_ids=[0])
    return r.results[0]["out_y"].reshape(B, T, D)
```

```python
from contextlib import ExitStack

import numpy as np

import concourse.bass as bass
from concourse import mybir

ALU = mybir.AluOpType
ACT = mybir.ActivationFunctionType
AX = mybir.AxisListType
F32 = mybir.dt.float32
F16 = mybir.dt.float16
I32 = mybir.dt.int32

P = 128
B, T, D = 4, 512, 256
KC = D // P
TT = T // P
NT = B * TT
H = 16
DK, DV = 8, 16
HPG, G = 4, 4
LOW = 16
SUB = 64
HD = 16
VW = H * (HD + 1) + 32 - (HD + 1)
ST = 64
X, HID, TOP = 8, 704, 2
HC = [(c * P, min(P, HID - c * P)) for c in range(-(-HID // P))]
XT = (NT * P * TOP + X * (P - 1)) // P
ROWS = XT * P
W_SCALE = 256.0
DC, DQ = 2, len(HC) // 2
NEVER = -60000.0


def shape_constants():
    i = np.arange(P)
    inv = 1.0 / 10000.0 ** (np.arange(0, HD, 2, dtype=np.float32) / HD)
    ang = np.einsum("i,j->ij", np.arange(T, dtype=np.float32), inv)
    cos = np.cos(np.concatenate([ang, ang], -1)).astype(np.float32)
    sin = np.sin(np.concatenate([ang, ang], -1)).astype(np.float32)
    sin[:, :HD // 2] *= -1
    tile = lambda a: np.ascontiguousarray(a.reshape(TT, P, HD).transpose(1, 0, 2).reshape(P, -1))
    gate = np.ones(T, np.float32)
    gate[::SUB] = 0
    rows = H * DK
    e_reset = np.ones((X, NT), np.float32)
    e_reset[:, 0] = 0
    f = lambda a: np.ascontiguousarray(a, np.float32)
    parts = [
        ("ident", f(np.eye(P))),
        ("upto", f(i[:, None] <= i[None, :])),
        ("before", f(i[:, None] < i[None, :])),
        ("ones", f(np.ones((P, P)))),
        ("cos", tile(cos)), ("sin", tile(sin)),
        ("powers", f(np.broadcast_to(np.float32(-0.5), (P, TT * H)))),
        ("rank8", f(np.broadcast_to(X - np.arange(X), (P, X)))),
        ("ereset", f(np.broadcast_to(e_reset.reshape(-1), (P, X * NT)))),
        ("xreset", f(np.broadcast_to(np.float32([0] + [1] * (X - 1)), (P, X)))),
        ("eps", f(np.full((P, 1), 1e-5))),
        ("tileno", f(np.broadcast_to(np.arange(XT), (P, XT)))),
    ]
    heads = i // DV
    first = [
        ("subreset", f(np.broadcast_to(gate, (P, T)))),
        ("headblock", f(np.arange(rows)[:, None] // DK == np.arange(H * DV)[None, :] // DV)),
        ("headmean", f((heads[:, None] == heads[None, :]) / DV)),
        ("headmask", f((np.arange(rows)[:, None] // DK) % HPG == np.arange(HPG)[None, :])),
    ]
    half = [
        ("ident16", np.eye(P)),
        ("future_k", np.where(i[None, :] > i[:, None], NEVER, 0)),
        ("future_q", np.where(i[:, None] > i[None, :], NEVER, 0)),
    ]
    return packed(parts), packed(first), packed([(n, a.astype(np.float16)) for n, a in half])


def packed(parts):
    at, where = 0, {}
    for name, a in parts:
        where[name] = (at, a.shape[1])
        at += a.shape[1]
    return np.ascontiguousarray(np.concatenate([a for _, a in parts], 1)), where


UNROLL = True
CONST, CONST_FIRST, CONST_HALF = shape_constants()


class Arena:

    def __init__(self, tensor, words):
        self.tensor, self.words, self.at = tensor, words, 0

    def take(self, *shape, dtype=F32):
        n = int(np.prod(shape))
        words = n if dtype != F16 else n // 2
        assert self.at + words <= self.words, (self.at, words, self.words)
        ap = self.tensor[:, self.at:self.at + words]
        self.at += words
        if dtype != F32:
            ap = ap.bitcast(dtype)
        if len(shape) > 1:
            names = "abcd"[:len(shape)]
            ap = ap.rearrange(f"p ({' '.join(names)}) -> p {' '.join(names)}",
                              **{k: v for k, v in zip(names, shape)})
        return ap


def spread(ap, axis, n):
    ap = ap.unsqueeze(axis)
    shape = list(ap.shape)
    shape[axis] = n
    return ap.broadcast_to(shape)


def nds(t):
    return bass.ds(t, 1)


def repeat(eng, n, body):
    if UNROLL:
        for i in range(n):
            body(i)
    else:
        with eng.Fori(0, n) as i:
            body(i)


class Order:

    def __init__(self, eng, sem, base=0):
        self.eng, self.sem, self.base, self.n = eng, sem, base, 0

    def after(self, ins):
        self.n += 1
        ins.then_inc(self.sem, 1)
        self.eng.wait_ge(self.sem, self.base + self.n)


def linear_attention(nc, ctx, s):
    ar = Arena(s.scratch, s.scratch_words)
    xn = ar.take(TT, D)
    xT = ar.take(KC, T)
    z1T = ar.take(T)
    zb = ar.take(T)
    e1 = ar.take(T)
    ls = ar.take(T)
    e_in = ar.take(T)
    e_inv = ar.take(T)
    e_out = ar.take(T)
    qd = ar.take(TT, P)
    qi = ar.take(TT, P)
    qx = ar.take(HPG, TT, P)
    ka = ar.take(TT, P)
    kb = ar.take(TT, P)
    ks = ar.take(TT, P)
    ksT = ar.take(TT, P)
    vz = ar.take(TT, H // 2, 4, DV)
    att = ar.take(2, HPG, P)
    state = ar.take(2, D)
    dstate = ar.take(D)
    dec = ar.take(TT)
    th = e_out
    sg = ar.take(KC, T)
    ogT = ar.take(KC, T)
    stats = ar.take(TT, 6)
    mv = ar.take(TT, 2)
    rstd = ar.take(TT)
    ps, c = s.psum, s.const
    oT = lambda k: ps[:, 4 + k, :]
    v_of = lambda t: vz[:, t, :, 0:4:3, :]
    names = ["h", "mv", "rstd", "xn", "xTp", "xT", "z1p", "z1", "gkp", "qp", "kp", "vp", "v", "gp", "th", "sg", "zb",
             "lsig", "ls", "dout", "exps", "kst", "qx", "ksTp", "ksT", "ap", "att", "used", "sp", "sadd", "oT", "sq",
             "msp", "ln", "rinv", "og", "yp", "dve", "act", "pool"]
    sem = {n: ctx.enter_context(nc.semaphore("gla_" + n)) for n in names}
    block = ctx.enter_context(nc.Block())

    @block.gpsimd
    def _(eng):
        eng.wait_ge(s.ids_in, 16)
        for t in range(NT):
            nc.gpsimd.indirect_dma_start(
                out=s.h[:, t, :], out_offset=None, in_=s.table,
                in_offset=bass.IndirectOffsetOnAxis(ap=s.ids[:, t:t + 1], axis=0),
            ).then_inc(s.rows_in[t // TT], 16)
        eng.wait_ge(s.const_in, 48)
        o = Order(eng, sem["pool"])
        for b in range(B):
            eng.wait_ge(sem["mv"], b + 1)
            if b:
                eng.wait_ge(sem["xn"], b * TT)
            o.after(eng.tensor_scalar(rstd, mv[:, :, 1], 1e-5, None, ALU.add))
            eng.tensor_tensor(rstd, rstd, c("powers")[:, 0:TT], ALU.pow).then_inc(sem["rstd"], 1)

    @block.scalar
    def _(eng):
        eng.wait_ge(s.const_in, 48)
        o = Order(eng, sem["act"])

        def x_and_low_rank(b):
            for k in range(KC):
                eng.wait_ge(sem["xTp"], b * KC + k + 1)
                eng.activation(xT[:, k, :], ps[:, k, :], ACT.Copy).then_inc(sem["xT"], 1)
            eng.wait_ge(sem["z1p"], b + 1)
            eng.activation(z1T[0:LOW, :], ps[0:LOW, 6, :], ACT.Copy).then_inc(sem["z1"], 1)

        def decays(b):
            eng.wait_ge(sem["zb"], b + 1)
            o.after(eng.activation(e1, zb, ACT.Abs))
            o.after(eng.activation(e1, e1, ACT.Exp, scale=-1.0))
            eng.activation(e1, e1, ACT.Ln, bias=1.0).then_inc(sem["lsig"], 1)
            for t in range(TT):
                eng.wait_ge(sem["vp"], b * 2 + t // 2 + 1)
                eng.activation(v_of(t), ps[:, t // 2, t % 2 * D:(t % 2 + 1) * D].rearrange(
                    "p (a j d) -> p a j d", j=2, d=DV), ACT.Copy).then_inc(sem["v"], 1)
            eng.wait_ge(sem["ls"], b + 1)
            eng.activation(e_in, ls, ACT.Exp, scale=1.0 / 16).then_inc(sem["exps"], 1)
            eng.activation(e_inv, ls, ACT.Exp, scale=-1.0 / 16).then_inc(sem["exps"], 1)
            eng.wait_ge(sem["dout"], b + 1)
            eng.activation(e_out, e_out, ACT.Exp, scale=1.0 / 16).then_inc(sem["exps"], 1)
            eng.wait_ge(sem["ksTp"], b + 1)
            eng.activation(ksT, ps[:, 0, :].rearrange("p (t n) -> p t n", t=TT), ACT.Copy).then_inc(sem["ksT"], 1)
            for k in range(KC):
                eng.wait_ge(sem["gp"], b * KC + k + 1)
                if k:
                    eng.wait_ge(sem["sg"], b * KC + k)
                else:
                    eng.wait_ge(sem["kst"], b + 1)
                eng.activation(th, ps[:, 6 + k, :], ACT.Tanh, scale=0.5).then_inc(sem["th"], 1)

        def one_over_rms(b):
            for k in range(KC):
                eng.wait_ge(sem["msp"], b * KC + k + 1)
                eng.activation(ogT[:, k, :], ps[:, 2 + k, :], ACT.Ln, bias=c("eps")).then_inc(sem["ln"], 1)
            for k in range(KC):
                eng.wait_ge(sem["ln"], b * KC + k + 1)
                eng.activation(ogT[:, k, :], ogT[:, k, :], ACT.Exp, scale=-0.5).then_inc(sem["rinv"], 1)

        x_and_low_rank(0)
        for b in range(B):
            decays(b)
            for k in range(KC):
                eng.wait_ge(sem["oT"], b + 1)
                if b:
                    eng.wait_ge(sem["yp"], b * 2)
                eng.activation(ogT[:, k, :], oT(k), ACT.Square).then_inc(sem["sq"], 1)
            if b + 1 < B:
                x_and_low_rank(b + 1)
            one_over_rms(b)

    @block.tensor
    def _(eng):
        eng.wait_ge(s.const_in, 48)

        def transposes(b):
            for k in range(KC):
                for t in range(TT):
                    if k == 0:
                        eng.wait_ge(sem["xn"], b * TT + t + 1)
                    m = eng.transpose(ps[:, k, t * P:(t + 1) * P], xn[:, t, k * P:(k + 1) * P], c("ident"))
                m.then_inc(sem["xTp"], 1)

        def project(bank, w, n, name):
            for k in range(KC):
                m = eng.matmul(ps[0:n, bank, :], w[:, k, :], xT[:, k, :], start=k == 0, stop=k == KC - 1)
            m.then_inc(sem[name], 1)

        def gate_projections(b):
            eng.wait_ge(s.gla_w_in, s.gla_w_n)
            eng.wait_ge(sem["xT"], (b + 1) * KC)
            project(6, s.wgk1, LOW, "z1p")

        def projections(b):
            eng.wait_ge(sem["z1"], b + 1)
            eng.matmul(ps[:, 7, :], s.wgk2[0:LOW, :], z1T[0:LOW, :], start=True, stop=True).then_inc(sem["gkp"], 1)
            if b:
                eng.wait_ge(sem["ln"], b * KC)
            project(2, s.gwq, P, "qp")
            project(3, s.gwk, P, "kp")
            for t in range(TT):
                for k in range(KC):
                    m = eng.matmul(ps[:, t // 2, t % 2 * D:(t % 2 + 1) * D], xT[:, k, t * P:(t + 1) * P],
                                   s.wvg[:, k, 0:D], start=k == 0, stop=k == KC - 1)
                if t % 2:
                    m.then_inc(sem["vp"], 1)
            project(6, s.wvg[:, :, D:D + P], P, "gp")
            eng.wait_ge(sem["zb"], b + 1)
            project(7, s.wvg[:, :, D + P:2 * D], P, "gp")

        def chunks(b):
            eng.wait_ge(sem["v"], (b + 1) * TT)
            eng.wait_ge(sem["kst"], b + 1)
            for t in range(TT):
                m = eng.transpose(ps[:, 0, t * P:(t + 1) * P], ks[:, t, :], c("ident"))
            m.then_inc(sem["ksTp"], 1)
            eng.wait_ge(sem["qx"], b + 1)
            eng.wait_ge(sem["ksT"], b + 1)
            if b:
                eng.wait_ge(sem["h"], b * 2)
            for t in range(TT):
                def scores(g):
                    n = t * G + g
                    if t:
                        eng.wait_ge(sem["att"], b * TT * G + n - G + 1)
                    for i, k in enumerate((ka, kb)):
                        m = eng.matmul(
                            ps[:, g, :].rearrange("p (j n) -> p j n", j=HPG)[:, :, i * SUB:(i + 1) * SUB],
                            k[32 * g:32 * g + 32, t, :], qx[32 * g:32 * g + 32, :, t, i * SUB:(i + 1) * SUB],
                            start=True, stop=True)
                    m.then_inc(sem["ap"], 1)

                scores(0)
                scores(1)
                if t < TT - 1:
                    if t == 0:
                        eng.wait_ge(sem["sg"], (b + 1) * KC)
                    eng.matmul(ps[:, 7, 0:D], ksT[:, t, :], v_of(t), start=True, stop=True).then_inc(sem["sp"], 1)
                cols = slice(t * P, (t + 1) * P)
                for g in range(G):
                    eng.wait_ge(sem["att"], b * TT * G + t * G + g + 1)
                    for j in range(HPG):
                        pair = (g * HPG + j) // 2
                        rows = slice(32 * (pair % 4), 32 * (pair % 4) + 32)
                        m = eng.matmul(ps[rows, 4 + pair // 4, cols],
                                       vz[:, t, pair, 2 * (j % 2):2 * (j % 2) + 2, :].rearrange("p a d -> p (a d)"),
                                       att[:, g % 2, j, :], start=j % 2 == 0, stop=True, skip_group_check=True)
                    m.then_inc(sem["used"], 1)
                    if g + 2 < G:
                        scores(g + 2)
                if t:
                    eng.wait_ge(sem["sadd"], b * (TT - 1) + t)
                    for k in range(KC):
                        m = eng.matmul(ps[:, 4 + k, cols], state[:, t % 2, k * P:(k + 1) * P], qi[:, t, :],
                                       start=False, stop=True, skip_group_check=True)
            m.then_inc(sem["oT"], 1)

        def mean_squares(b):
            for k in range(KC):
                eng.wait_ge(sem["sq"], b * KC + k + 1)
                eng.matmul(ps[:, 2 + k, :], c("headmean"), ogT[:, k, :], start=True, stop=True)\
                   .then_inc(sem["msp"], 1)

        def outputs(b):
            eng.wait_ge(sem["og"], (b + 1) * KC)
            for t in range(TT):
                for k in range(KC):
                    m = eng.matmul(ps[:, 4 + t // 2, (t % 2) * D:(t % 2 + 1) * D], ogT[:, k, t * P:(t + 1) * P],
                                   s.gwo[:, k, :], start=k == 0, stop=k == KC - 1)
                if t % 2:
                    m.then_inc(sem["yp"], 1)

        transposes(0)
        gate_projections(0)
        projections(0)
        for b in range(B):
            chunks(b)
            eng.wait_ge(sem["att"], (b + 1) * TT * G)
            if b + 1 < B:
                transposes(b + 1)
            mean_squares(b)
            if b + 1 < B:
                gate_projections(b + 1)
                projections(b + 1)
            outputs(b)

    @block.vector
    def _(eng):
        eng.wait_ge(s.const_in, 48)
        o = Order(eng, sem["dve"])
        o.after(eng.memset(ka[:, :, SUB:P], 0.0))
        o.after(eng.memset(vz[:, :, :, 1:3, :], 0.0))
        eng.wait_ge(s.vec_in, s.vec_n)

        def moments(b):
            hb = s.h[:, b * TT:(b + 1) * TT, :]
            eng.wait_ge(s.rows_in[b], 16 * TT)
            o.after(eng.tensor_tensor(hb, hb, spread(s.tok_bias, 1, TT), ALU.add))
            for t in range(TT):
                eng.bn_stats(stats[:, t, :], s.h[:, b * TT + t, :]).then_inc(sem["dve"], 1)
            o.n += TT
            eng.wait_ge(sem["dve"], o.n)
            for t in range(TT):
                m = eng.bn_aggr(mv[:, t, :], stats[:, t, :])
                if t < TT - 1:
                    m.then_inc(sem["dve"], 1)
            o.n += TT - 1
            eng.wait_ge(sem["dve"], o.n)
            m.then_inc(sem["mv"], 1)

        def layernorm(b):
            eng.wait_ge(sem["mv"], b + 1)
            eng.wait_ge(sem["rstd"], b + 1)
            if b:
                eng.wait_ge(sem["xTp"], b * KC)
            for t in range(TT):
                eng.tensor_scalar(xn[:, t, :], s.h[:, b * TT + t, :], mv[:, t, 0:1], rstd[:, t:t + 1],
                                  ALU.subtract, ALU.mult).then_inc(sem["xn"], 1)

        def gate_bias(b):
            eng.wait_ge(sem["gkp"], b + 1)
            eng.tensor_scalar(zb, ps[:, 7, :], s.bgk2, None, ALU.add).then_inc(sem["zb"], 1)

        def queries_and_keys(b):
            eng.wait_ge(sem["zb"], b + 1)
            eng.wait_ge(sem["lsig"], b + 1)
            o.after(eng.scalar_tensor_tensor(zb, zb, 0.0, e1, ALU.min, ALU.subtract))
            eng.tensor_tensor_scan(ls, c("subreset"), zb, 0.0, ALU.mult, ALU.add).then_inc(sem["ls"], 1)
            eng.wait_ge(sem["ls"], b + 1)
            ls_s = ls.rearrange("p (a n) -> p a n", n=SUB)
            eng.tensor_tensor(e_out.rearrange("p (a n) -> p a n", n=SUB),
                              ls_s[:, :, SUB - 1:SUB].broadcast_to([P, T // SUB, SUB]), ls_s,
                              ALU.subtract).then_inc(sem["dout"], 1)
            ei, ev, eo = (x.rearrange("p (t n) -> p t n", n=P) for x in (e_in, e_inv, e_out))
            eng.wait_ge(sem["exps"], b * 3 + 2)
            eng.wait_ge(sem["qp"], b + 1)
            o.after(eng.scalar_tensor_tensor(qd, ps[:, 2, :].rearrange("p (t n) -> p t n", n=P), DK ** -0.5, ei,
                                             ALU.mult, ALU.mult))
            kp = ps[:, 3, :].rearrange("p (t n) -> p t n", n=P)
            lo, hi = slice(0, SUB), slice(SUB, P)
            eng.wait_ge(sem["kp"], b + 1)
            o.after(eng.tensor_tensor(ka[:, :, lo], kp[:, :, lo], ev[:, :, lo], ALU.mult))
            o.after(eng.tensor_tensor(kb[:, :, hi], kp[:, :, hi], ev[:, :, hi], ALU.mult))
            eng.wait_ge(sem["exps"], (b + 1) * 3)
            o.after(eng.tensor_tensor(kb[:, :, lo], kp[:, :, lo], eo[:, :, lo], ALU.mult))
            o.after(eng.tensor_tensor(ks[:, :, hi], kp[:, :, hi], eo[:, :, hi], ALU.mult))
            eng.tensor_tensor(ks[:, :, lo], kb[:, :, lo], ei[:, :, P - 1:P].broadcast_to([P, TT, SUB]),
                              ALU.mult).then_inc(sem["kst"], 1)
            eng.wait_ge(sem["kst"], b + 1)
            for j in range(HPG):
                m = eng.tensor_scalar(qx[:, j, :, :], qd, c("headmask")[:, j:j + 1], None, ALU.mult)
                if j < HPG - 1:
                    o.after(m)
            m.then_inc(sem["qx"], 1)
            o.after(eng.tensor_copy(qi[:, :, lo], qd[:, :, lo]))
            o.after(eng.tensor_tensor(qi[:, :, hi], qd[:, :, hi], ei[:, :, SUB - 1:SUB].broadcast_to([P, TT, SUB]),
                                      ALU.mult))
            o.after(eng.tensor_tensor(dec.unsqueeze(2), ei[:, :, SUB - 1:SUB], ei[:, :, P - 1:P], ALU.mult))

        def gate(b):
            for k in range(KC):
                eng.wait_ge(sem["th"], b * KC + k + 1)
                eng.scalar_tensor_tensor(sg[:, k, :], th, 1.0, ps[:, 6 + k, :], ALU.add, ALU.mult)\
                   .then_inc(sem["sg"], 1)
                eng.wait_ge(sem["sg"], b * KC + k + 1)

        def chunks(b):
            for t in range(TT):
                for g in range(G):
                    n = t * G + g
                    eng.wait_ge(sem["ap"], b * TT * G + n + 1)
                    if n >= 2:
                        eng.wait_ge(sem["used"], b * TT * G + n - 1)
                    eng.tensor_tensor(att[:, g % 2, :, :], ps[:, g, :].rearrange("p (j n) -> p j n", j=HPG),
                                      spread(c("upto"), 1, HPG), ALU.mult).then_inc(sem["att"], 1)
                    if g == 1 and t < TT - 1:
                        eng.wait_ge(sem["sp"], b * (TT - 1) + t + 1)
                        own = dstate if t else state[:, 1, :]
                        m = eng.tensor_tensor(own, ps[:, 7, 0:D], c("headblock"), ALU.mult)
                        if t:
                            o.after(m)
                            m = eng.scalar_tensor_tensor(state[:, (t + 1) % 2, :], state[:, t % 2, :],
                                                         dec[:, t:t + 1], dstate, ALU.mult, ALU.add)
                        m.then_inc(sem["sadd"], 1)
                        eng.wait_ge(sem["sadd"], b * (TT - 1) + t + 1)
                if b + 1 < B and t == 1:
                    moments(b + 1)
                if b + 1 < B and t == 2:
                    layernorm(b + 1)

        def normalise(b):
            for k in range(KC):
                eng.wait_ge(sem["rinv"], b * KC + k + 1)
                o.after(eng.scalar_tensor_tensor(ogT[:, k, :], oT(k), s.gnw_half, ogT[:, k, :], ALU.mult, ALU.mult))
                eng.tensor_tensor(ogT[:, k, :], ogT[:, k, :], sg[:, k, :], ALU.mult).then_inc(sem["og"], 1)

        def add_outputs(b):
            for i in range(2):
                eng.wait_ge(sem["yp"], b * 2 + i + 1)
                hh = s.h[:, b * TT + 2 * i:b * TT + 2 * i + 2, :]
                eng.tensor_tensor(hh, hh, ps[:, 4 + i, :].rearrange("p (t d) -> p t d", t=2),
                                  ALU.add).then_inc(sem["h"], 1)

        moments(0)
        layernorm(0)
        gate_bias(0)
        for b in range(B):
            queries_and_keys(b)
            gate(b)
            if b:
                add_outputs(b - 1)
            chunks(b)
            if b + 1 < B:
                gate_bias(b + 1)
            normalise(b)
        add_outputs(B - 1)


def softmax_attention(nc, ctx, s):
    ar = Arena(s.scratch, s.scratch_words)
    x = ar.take(TT, D)
    n1 = ar.take(TT, D)
    n1T = ar.take(KC, T)
    qk = ar.take(2 * D)
    rot = ar.take(2 * D)
    sq = ar.take(TT, H, ST, dtype=F16)
    sk = ar.take(TT, H, ST, dtype=F16)
    qT = ar.take(H // 2, T, dtype=F16)
    kT = ar.take(H // 2, T, dtype=F16)
    va = ar.take(TT, VW)
    pT = ar.take(2, 10 * P)
    mx = ar.take(TT, H)
    rden = ar.take(TT, 4)
    stats, mv, rn = ar.take(TT, 6), ar.take(TT, 2), ar.take(2, TT)
    ssq, r2 = ar.take(TT), ar.take(TT)
    oT = n1T
    nT = n1T
    vh = va[:, :, 0:H * (HD + 1)].rearrange("p t (h d) -> p t h d", h=H)
    oq = rot
    stage = ar.take(2, HID)
    PER = 2 * X * KC // B
    heads = n1
    ps, c = s.psum, s.const
    at = {0: 0, 1: 4, 3: 7, 2: 8}
    block_of = lambda kt, qt: at[kt] + qt - kt
    names = ["mv", "rn", "n1", "n1Tp", "n1T", "qkp", "vp", "va", "rope", "hi", "stk", "sTp", "qT", "kT", "mp", "mx",
             "neg", "s2Tp", "q2T", "pp", "exp", "pv", "on", "oTp", "oT", "yp", "g", "ssq", "r2", "n2", "nTp",
             "nT", "lp", "lg", "qkr", "oq", "oqTp", "split", "w0", "w1", "dve", "act", "pool"]
    sem = {n: ctx.enter_context(nc.semaphore("att_" + n)) for n in names}
    block = ctx.enter_context(nc.Block())

    @block.gpsimd
    def _(eng):
        o = Order(eng, sem["pool"])

        def sequence(b):
            eng.wait_ge(sem["mv"], b + 1)
            eng.tensor_scalar(rn[:, 0, :], mv[:, :, 1], 1e-5, None, ALU.add).then_inc(sem["pool"], 1)
            eng.tensor_scalar(rn[:, 1, :], mv[:, :, 1], 1.0 + 1e-6, 1e-11, ALU.mult, ALU.add).then_inc(sem["pool"], 1)
            o.n += 2
            eng.wait_ge(sem["pool"], o.base + o.n)
            rf = rn.rearrange("p a t -> p (a t)")
            eng.tensor_tensor(rf, rf, c("powers")[:, 0:2 * TT], ALU.pow).then_inc(sem["rn"], 1)
            for n in range(PER):
                eng.wait_ge(sem[f"w{n % 2}"], 16 * (b * (PER // 2) + n // 2 + 1))
                w, w16, xk = stage[:, n % 2, :], (s.wg, s.wu)[n % 2], b * (PER // 2) + n // 2
                part = lambda i: w16[:, bass.ds(xk, 1), i, :].rearrange("p a n -> p (a n)")
                o.after(eng.tensor_scalar(w, w, W_SCALE, None, ALU.mult))
                o.after(eng.tensor_copy(part(0), w))
                eng.tensor_tensor(part(1), w, part(0), ALU.subtract).then_inc(sem["split"], 1)
            eng.wait_ge(sem["ssq"], (b + 1) * TT)
            o.after(eng.tensor_scalar(r2, ssq, 1.0 / D, 1e-6, ALU.mult, ALU.add))
            eng.tensor_tensor(r2, r2, c("powers")[:, 0:TT], ALU.pow).then_inc(sem["r2"], 1)

        repeat(eng, B, sequence)

    @block.sync
    def _(eng):
        def sequence(b):
            for n in range(PER):
                if b * PER + n >= 2:
                    eng.wait_ge(sem["split"], b * PER + n - 1)
                w, xk = s.wgu_dram[n % 2], b * (PER // 2) + n // 2
                eng.dma_start(stage[:, n % 2, :], w[bass.ds(xk, 1)].rearrange("a p n -> p (a n)"))\
                   .then_inc(sem[f"w{n % 2}"], 16)

        repeat(eng, B, sequence)

    @block.scalar
    def _(eng):
        o = Order(eng, sem["act"])

        def sequence(b):
            for k in range(KC):
                eng.wait_ge(sem["n1Tp"], b * KC + k + 1)
                eng.activation(n1T[:, k, :], ps[:, k, :], ACT.Copy).then_inc(sem["n1T"], 1)
            for t in range(TT):
                eng.wait_ge(sem["vp"], b * TT + t + 1)
                eng.activation(vh[:, t, :, 0:HD], ps[:, 4 + t % 2, 0:D].rearrange("p (h d) -> p h d", h=H),
                               ACT.Copy).then_inc(sem["va"], 1)
                eng.wait_ge(sem["rope"], b * TT + t + 1)
                hv = lambda a: a.rearrange("p (h d) -> p h d", h=H)
                two = lambda a: a.rearrange("p h (j d) -> p h j d", d=HD)
                eng.activation(two(sq[:, t, :, 0:2 * HD]), spread(hv(qk[:, 0:D]), 2, 2), ACT.Copy, scale=HD ** -0.5)\
                   .then_inc(sem["hi"], 1)
                eng.activation(two(sk[:, t, :, 0:3 * HD])[:, :, 0:3:2, :], spread(hv(qk[:, D:2 * D]), 2, 2), ACT.Copy)\
                   .then_inc(sem["hi"], 1)
                eng.wait_ge(sem["sTp"], b * TT + t + 1)
                eng.activation(qT[:, :, t * P:(t + 1) * P],
                               ps[:, 6, :].bitcast(F16).rearrange("p (a n) -> p a n", n=P), ACT.Copy)\
                   .then_inc(sem["qT"], 1)
            for t in range(TT):
                eng.wait_ge(sem["s2Tp"], b * TT + t + 1)
                eng.activation(qT[:, :, t * P:(t + 1) * P],
                               ps[:, 6 + t % 2, :].bitcast(F16).rearrange("p (a n) -> p a n", n=P), ACT.Copy)\
                   .then_inc(sem["q2T"], 1)
            for h in range(H):
                eng.wait_ge(sem["pp"], b * H + h + 1)
                if h >= 2:
                    eng.wait_ge(sem["pv"], b * H + h - 1)
                src = ps[:, 3 * (h % 2):3 * (h % 2) + 3, :].rearrange("p a n -> p (a n)")[:, 0:10 * P]
                eng.activation(pT[:, h % 2, :], src, ACT.Exp).then_inc(sem["exp"], 1)
            for k in range(KC):
                eng.wait_ge(sem["oTp"], b * KC + k + 1)
                eng.activation(oT[:, k, :], ps[:, k, :], ACT.Copy).then_inc(sem["oT"], 1)
            for t in range(TT):
                eng.wait_ge(sem["g"], b * 2 + t // 2 + 1)
                eng.activation(rot[:, 0:D], x[:, t, :], ACT.Square, accum_out=ssq[:, t:t + 1]).then_inc(sem["ssq"], 1)
                eng.wait_ge(sem["ssq"], b * TT + t + 1)
            for k in range(KC):
                eng.wait_ge(sem["nTp"], b * KC + k + 1)
                eng.activation(nT[:, k, :], ps[:, 4 + k, :], ACT.Copy).then_inc(sem["nT"], 1)

        repeat(eng, B, sequence)

    @block.tensor
    def _(eng):
        eng.wait_ge(s.att_w_in, s.att_w_n)

        def sequence(b):
            for k in range(KC):
                for t in range(TT):
                    if k == 0:
                        eng.wait_ge(sem["n1"], b * TT + t + 1)
                    m = eng.transpose(ps[:, k, t * P:(t + 1) * P], n1[:, t, k * P:(k + 1) * P], c("ident"))
                m.then_inc(sem["n1Tp"], 1)
            eng.wait_ge(sem["n1T"], (b + 1) * KC)
            def project(t):
                if t >= 2:
                    eng.wait_ge(sem["qkr"], b * TT + t - 1)
                    eng.wait_ge(sem["va"], b * TT + t - 1)
                for k in range(KC):
                    m = eng.matmul(ps[:, 2 + t % 2, :], n1T[:, k, t * P:(t + 1) * P], s.wqkv[:, k, 0:2 * D],
                                   start=k == 0, stop=k == KC - 1)
                m.then_inc(sem["qkp"], 1)
                for k in range(KC):
                    m = eng.matmul(ps[:, 4 + t % 2, 0:D], n1T[:, k, t * P:(t + 1) * P], s.wqkv[:, k, 2 * D:3 * D],
                                   start=k == 0, stop=k == KC - 1)
                m.then_inc(sem["vp"], 1)

            def stack_up(t):
                eng.wait_ge(sem["stk"], b * TT + t + 1)
                if t:
                    eng.wait_ge(sem["qT"], b * TT + t)
                    eng.wait_ge(sem["kT"], b * TT + t)
                for bank, stack in ((6, sq), (7, sk)):
                    for a in range(H // 2):
                        m = eng.transpose(ps[:, bank, a * 64:(a + 1) * 64].bitcast(F16),
                                          stack[:, t, 2 * a:2 * a + 2, :].rearrange("p h d -> p (h d)"), s.ident16)
                m.then_inc(sem["sTp"], 1)

            project(0)
            project(1)
            for t in range(TT):
                stack_up(t)
                if t + 2 < TT:
                    project(t + 2)
            eng.wait_ge(sem["kT"], (b + 1) * TT)
            eng.wait_ge(sem["qT"], (b + 1) * TT)
            eng.wait_ge(sem["va"], (b + 1) * TT)
            for t in range(TT):
                for a in range(H // 2):
                    n = t * (H // 2) + a
                    if n >= 3:
                        eng.wait_ge(sem["mx"], b * TT * (H // 2) + n - 2)
                    for r in range(2):
                        rows = slice(r * ST, (r + 1) * ST)
                        m = eng.matmul(ps[:, 2 * (n % 3) + r, 0:(t + 1) * P], qT[rows, a, t * P:(t + 1) * P],
                                       kT[rows, a, 0:(t + 1) * P], start=True, stop=True)
                    for r in range(2):
                        m = eng.matmul(ps[:, 2 * (n % 3) + r, t * P:(t + 1) * P], s.ident16, s.future_k,
                                       start=False, stop=True, skip_group_check=True)
                    m.then_inc(sem["mp"], 1)
            for t in range(TT):
                eng.wait_ge(sem["neg"], b * TT + t + 1)
                if t >= 2:
                    eng.wait_ge(sem["q2T"], b * TT + t - 1)
                for a in range(H // 2):
                    m = eng.transpose(ps[:, 6 + t % 2, a * 64:(a + 1) * 64].bitcast(F16),
                                      sq[:, t, 2 * a:2 * a + 2, :].rearrange("p h d -> p (h d)"), s.ident16)
                m.then_inc(sem["s2Tp"], 1)
            eng.wait_ge(sem["q2T"], (b + 1) * TT)
            eng.wait_ge(sem["mx"], (b + 1) * TT * (H // 2))

            def scores(h):
                rows = slice((h % 2) * ST, (h % 2 + 1) * ST)
                if h >= 2:
                    eng.wait_ge(sem["exp"], b * H + h - 1)
                spot = lambda kt, n: ps[:, 3 * (h % 2) + at[kt] // 4, at[kt] % 4 * P:(at[kt] % 4 + n) * P]
                for kt in range(TT):
                    eng.matmul(spot(kt, TT - kt), kT[rows, h // 2, kt * P:(kt + 1) * P], qT[rows, h // 2, kt * P:T],
                               start=kt != 3, stop=True, skip_group_check=True)
                for kt in range(TT):
                    m = eng.matmul(spot(kt, 1), s.ident16, s.future_q, start=False, stop=True, skip_group_check=True)
                m.then_inc(sem["pp"], 1)

            def queries_back(quad):
                eng.wait_ge(sem["oq"], b * 4 + quad + 1)
                if quad:
                    eng.wait_ge(sem["on"], b * 4 + quad)
                for t in range(TT):
                    m = eng.transpose(ps[:, 7, t * P:(t + 1) * P], oq[:, t * P:(t + 1) * P], c("ident"))
                m.then_inc(sem["oqTp"], 1)

            scores(0)
            scores(1)
            for h in range(H):
                eng.wait_ge(sem["exp"], b * H + h + 1)
                if h % 4 == 0 and h:
                    eng.wait_ge(sem["oq"], b * 4 + h // 4)
                j = h % 4
                for kt in range(TT):
                    m = eng.matmul(ps[32 * j:32 * j + 32, 6, kt * P:T], va[:, kt, h * (HD + 1):h * (HD + 1) + 32],
                                   pT[:, h % 2, at[kt] * P:(at[kt] + TT - kt) * P],
                                   start=kt == 0, stop=True, skip_group_check=True)
                m.then_inc(sem["pv"], 1)
                if h + 2 < H:
                    scores(h + 2)
                if j == 0 and h:
                    queries_back(h // 4 - 1)
            queries_back(3)
            eng.wait_ge(sem["on"], (b + 1) * 4)
            for k in range(KC):
                for t in range(TT):
                    m = eng.transpose(ps[:, k, t * P:(t + 1) * P], heads[:, t, k * P:(k + 1) * P], c("ident"))
                m.then_inc(sem["oTp"], 1)
            eng.wait_ge(sem["oT"], (b + 1) * KC)
            for t in range(TT):
                for k in range(KC):
                    m = eng.matmul(ps[:, 2 + t // 2, (t % 2) * D:(t % 2 + 1) * D], oT[:, k, t * P:(t + 1) * P],
                                   s.wo[:, k, :], start=k == 0, stop=k == KC - 1)
                if t % 2:
                    m.then_inc(sem["yp"], 1)
            for k in range(KC):
                for t in range(TT):
                    if k == 0:
                        eng.wait_ge(sem["n2"], b * TT + t + 1)
                    m = eng.transpose(ps[:, 4 + k, t * P:(t + 1) * P],
                                      s.n2[:, nds(b * TT + t), k * P:(k + 1) * P].rearrange("p a d -> p (a d)"),
                                      c("ident"))
                m.then_inc(sem["nTp"], 1)
            eng.wait_ge(sem["nT"], (b + 1) * KC)
            for t in range(TT):
                for k in range(KC):
                    m = eng.matmul(ps[:, 6, t * X:(t + 1) * X], nT[:, k, t * P:(t + 1) * P], s.wr[:, k, :],
                                   start=k == 0, stop=k == KC - 1)
            m.then_inc(sem["lp"], 1)
            eng.wait_ge(sem["lg"], b + 1)

        repeat(eng, B, sequence)

    @block.vector
    def _(eng):
        eng.wait_ge(s.att_w_in, s.att_w_n - 1)
        o = Order(eng, sem["dve"])
        for k in range(KC):
            m = eng.tensor_scalar(s.wqkv[:, k, :], s.wqkv[:, k, :], s.g1[:, k:k + 1], None, ALU.mult)
            if k < KC - 1:
                o.after(m)
        m.then_inc(s.att_w_in, 1)
        o.after(eng.memset(sq[:, :, :, 3 * HD:ST], 0.0))
        o.after(eng.memset(sk[:, :, :, 3 * HD:ST], 0.0))
        o.after(eng.memset(sk[:, :, :, 3 * HD:3 * HD + 1], 1.0))
        o.after(eng.memset(va[:, :, H * (HD + 1):VW], 0.0))
        o.after(eng.memset(vh[:, :, :, HD:HD + 1], 1.0))

        def sequence(b):
            row = lambda t: s.h[:, nds(b * TT + t), :].rearrange("p a d -> p (a d)")
            for t in range(TT):
                eng.bn_stats(stats[:, t, :], row(t)).then_inc(sem["dve"], 1)
            o.n += TT
            eng.wait_ge(sem["dve"], o.base + o.n)
            for t in range(TT):
                m = eng.bn_aggr(mv[:, t, :], stats[:, t, :])
                if t < TT - 1:
                    m.then_inc(sem["dve"], 1)
            o.n += TT - 1
            m.then_inc(sem["mv"], 1)
            eng.wait_ge(sem["mv"], b + 1)
            eng.wait_ge(sem["dve"], o.base + o.n)
            eng.wait_ge(sem["rn"], b + 1)
            for t in range(TT):
                o.after(eng.tensor_scalar(x[:, t, :], row(t), mv[:, t, 0:1], rn[:, 0, t:t + 1], ALU.subtract, ALU.mult))
                eng.tensor_scalar(n1[:, t, :], row(t), mv[:, t, 0:1], rn[:, 1, t:t + 1], ALU.subtract, ALU.mult)\
                   .then_inc(sem["n1"], 1)
            v3 = lambda a: a.rearrange("p (h d) -> p h d", d=HD)
            half = HD // 2
            for t in range(TT):
                eng.wait_ge(sem["qkp"], b * TT + t + 1)
                if t:
                    eng.wait_ge(sem["hi"], b * TT * 2 + 2 * t)
                else:
                    eng.wait_ge(sem["hi"], b * TT * 2)
                qkp = v3(ps[:, 2 + t % 2, :])
                cos, sin = (c(n)[:, t * HD:(t + 1) * HD] for n in ("cos", "sin"))
                o.after(eng.tensor_tensor(v3(qk), qkp, spread(cos, 1, 2 * H), ALU.mult))
                o.after(eng.tensor_tensor(v3(rot)[:, :, 0:half], qkp[:, :, half:HD], spread(sin[:, 0:half], 1, 2 * H),
                                          ALU.mult))
                eng.tensor_tensor(v3(rot)[:, :, half:HD], qkp[:, :, 0:half], spread(sin[:, half:HD], 1, 2 * H),
                                  ALU.mult).then_inc(sem["qkr"], 1)
                eng.wait_ge(sem["qkr"], b * TT + t + 1)
                eng.tensor_tensor(qk, qk, rot, ALU.add).then_inc(sem["rope"], 1)
                eng.wait_ge(sem["rope"], b * TT + t + 1)
                o.after(eng.memset(sq[:, t, :, 3 * HD:3 * HD + 1], 0.0))
                eng.wait_ge(sem["hi"], (b * TT + t) * 2 + 2)
                o.after(eng.scalar_tensor_tensor(sq[:, t, :, 2 * HD:3 * HD], v3(qk[:, 0:D]), HD ** -0.5,
                                                 sq[:, t, :, 0:HD], ALU.mult, ALU.subtract))
                eng.tensor_tensor(sk[:, t, :, HD:2 * HD], v3(qk[:, D:2 * D]), sk[:, t, :, 0:HD], ALU.subtract)\
                   .then_inc(sem["stk"], 1)
                eng.wait_ge(sem["stk"], b * TT + t + 1)
                eng.wait_ge(sem["sTp"], b * TT + t + 1)
                eng.tensor_copy(kT[:, :, t * P:(t + 1) * P],
                                ps[:, 7, :].bitcast(F16).rearrange("p (a n) -> p a n", n=P)).then_inc(sem["kT"], 1)
            for t in range(TT):
                for a in range(H // 2):
                    n = t * (H // 2) + a
                    eng.wait_ge(sem["mp"], b * TT * (H // 2) + n + 1)
                    eng.tensor_reduce(mx[:, t, 2 * a:2 * a + 2], ps[:, 2 * (n % 3):2 * (n % 3) + 2, 0:(t + 1) * P], AX.X,
                                      ALU.max).then_inc(sem["mx"], 1)
                eng.wait_ge(sem["mx"], b * TT * (H // 2) + (t + 1) * (H // 2))
                eng.tensor_scalar(sq[:, t, :, 3 * HD:3 * HD + 1], mx[:, t, :].unsqueeze(2), -1.0, None, ALU.mult)\
                   .then_inc(sem["neg"], 1)
            for quad in range(4):
                eng.wait_ge(sem["pv"], b * H + 4 * quad + 4)
                eng.tensor_copy(oq, ps[:, 6, :]).then_inc(sem["oq"], 1)
                eng.wait_ge(sem["oqTp"], b * 4 + quad + 1)
                out = ps[:, 7, :].rearrange("p (t h d) -> p t h d", t=TT, h=4)
                o.after(eng.reciprocal(rden.unsqueeze(3), out[:, :, :, HD:HD + 1]))
                hq = heads[:, :, quad * 4 * HD:(quad + 1) * 4 * HD].rearrange("p t (h d) -> p t h d", h=4)
                for t in range(TT):
                    m = eng.tensor_tensor(hq[:, t], out[:, t, :, 0:HD], spread(rden[:, t, :], 2, HD), ALU.mult)
                    if t < TT - 1:
                        o.after(m)
                m.then_inc(sem["on"], 1)
                eng.wait_ge(sem["on"], b * 4 + quad + 1)
            for i in range(2):
                eng.wait_ge(sem["yp"], b * 2 + i + 1)
                eng.tensor_tensor(x[:, 2 * i:2 * i + 2, :], x[:, 2 * i:2 * i + 2, :],
                                  ps[:, 2 + i, :].rearrange("p (t d) -> p t d", t=2), ALU.add).then_inc(sem["g"], 1)
            hb = s.h[:, bass.ds(b * TT, TT), :]
            eng.wait_ge(sem["g"], (b + 1) * 2)
            o.after(eng.tensor_tensor(hb, hb, x, ALU.add))
            eng.wait_ge(sem["r2"], b + 1)
            eng.wait_ge(s.rows_zeroed, 16)
            for t in range(TT):
                eng.scalar_tensor_tensor(s.n2[:, nds(b * TT + t), :].rearrange("p a d -> p (a d)"), x[:, t, :],
                                         r2[:, t:t + 1], s.g2, ALU.mult, ALU.mult).then_inc(sem["n2"], 1)
            eng.wait_ge(sem["lp"], b + 1)
            eng.tensor_copy(s.logits[:, bass.ds(b * TT, TT), :],
                            ps[:, 6, 0:TT * X].rearrange("p (t e) -> p t e", e=X)).then_inc(sem["lg"], 1)

        repeat(eng, B, sequence)


def routing(nc, ctx, s):
    ar = Arena(s.scratch, s.scratch_words)
    ar.at = s.wd_words
    stage = ar.take(DQ, DC, D)
    tx = lambda: ar.take(NT, X)
    eq, one1, one2, lg2, both, pref, tot = (tx() for _ in range(7))
    m1, m2, pick, w1s, w2s = (ar.take(NT) for _ in range(5))
    incl, excl, tot_e = ar.take(X, NT), ar.take(X, NT), ar.take(X, NT)
    n_t, end_t = ar.take(X), ar.take(X)
    slot = ar.take(2, NT)
    cmp_t, own = ar.take(XT, X), ar.take(XT)
    tiles_i = ar.tensor[:, ar.at:ar.at + X].bitcast(I32)
    ps, c = s.psum, s.const
    names = ["both", "cnt", "slots", "e", "we", "dve", "pad", "wd0", "wd1", "wd2", "hi", "lo"]
    sem = {n: ctx.enter_context(nc.semaphore("route_" + n)) for n in names}
    block = ctx.enter_context(nc.Block())

    @block.vector
    def _(eng):
        o = Order(eng, sem["dve"])
        eng.memset(stage[HC[-1][1]:P, DQ - 1, DC - 1, :], 0.0).then_inc(sem["pad"], 1)

        def first_of_the_largest(values, top, onehot):
            o.after(eng.tensor_reduce(top, values, AX.X, ALU.max))
            o.after(eng.tensor_tensor(eq, values, spread(top, 2, X), ALU.is_equal))
            o.after(eng.tensor_tensor(eq, eq, spread(c("rank8"), 1, NT), ALU.mult))
            o.after(eng.tensor_reduce(pick, eq, AX.X, ALU.max))
            o.after(eng.tensor_tensor(onehot, eq, spread(pick, 2, X), ALU.is_equal))

        lg = s.logits[:, :, :]
        first_of_the_largest(lg, m1, one1)
        o.after(eng.scalar_tensor_tensor(lg2, one1, -3e38, lg, ALU.mult, ALU.add))
        first_of_the_largest(lg2, m2, one2)
        eng.tensor_tensor(both, one1, one2, ALU.add).then_inc(sem["both"], 1)
        eng.tensor_tensor(w2s, m2, m1, ALU.subtract).then_inc(sem["e"], 1)
        eng.wait_ge(sem["we"], 1)
        o.after(eng.tensor_scalar(w1s, w2s, 1.0, None, ALU.add))
        o.after(eng.reciprocal(s.w[:, 0, :], w1s))
        o.after(eng.tensor_tensor(s.w[:, 1, :], w2s, s.w[:, 0, :], ALU.mult))
        eng.wait_ge(sem["cnt"], 1)
        o.after(eng.tensor_copy(pref, ps[:, 0, 0:NT * X].rearrange("p (t e) -> p t e", e=X)))
        o.after(eng.tensor_copy(tot_e, ps[:, 1, 0:NT * X].rearrange("p (t e) -> p e t", e=X)))
        o.after(eng.tensor_tensor_scan(incl.rearrange("p e t -> p (e t)"), c("ereset"),
                                       tot_e.rearrange("p e t -> p (e t)"), 0.0, ALU.mult, ALU.add))
        o.after(eng.tensor_tensor(excl, incl, tot_e, ALU.subtract))
        o.after(eng.tensor_scalar(tiles_i, incl[:, :, NT - 1], P - 1.0, None, ALU.add))
        o.after(eng.tensor_scalar(tiles_i, tiles_i, 7, None, ALU.arith_shift_right))
        o.after(eng.tensor_copy(n_t, tiles_i))
        o.after(eng.tensor_tensor_scan(end_t, c("ones")[:, 0:X], n_t, 0.0, ALU.mult, ALU.add))
        o.after(eng.tensor_tensor(cmp_t, spread(end_t, 1, XT), spread(c("tileno"), 2, X), ALU.is_le))
        o.after(eng.tensor_reduce(own, cmp_t, AX.X, ALU.add))
        o.after(eng.tensor_scalar(s.expert[:, :], own, X - 1.0, None, ALU.min))
        o.after(eng.tensor_tensor(n_t, end_t, n_t, ALU.subtract))
        o.after(eng.tensor_scalar(n_t, n_t, float(P), None, ALU.mult))
        o.after(eng.tensor_tensor(excl, excl, spread(n_t, 2, NT), ALU.add))
        o.after(eng.tensor_tensor(pref, pref, excl.rearrange("p e t -> p t e"), ALU.add))
        for i, onehot in enumerate((one1, one2)):
            o.after(eng.tensor_tensor(lg2, onehot, pref, ALU.mult))
            o.after(eng.tensor_reduce(slot[:, i, :], lg2, AX.X, ALU.add))
        eng.tensor_copy(s.slots[:, :, :], slot).then_inc(sem["slots"], 1)
        for n in range(X * DQ):
            eng.wait_ge(sem["hi"], n + 1)
            eng.scalar_tensor_tensor(s.wd[:, n * DC:(n + 1) * DC, 1, :], stage[:, n % DQ, :, :], W_SCALE,
                                     s.wd[:, n * DC:(n + 1) * DC, 0, :], ALU.mult, ALU.subtract).then_inc(sem["lo"], 1)

    @block.scalar
    def _(eng):
        eng.wait_ge(sem["e"], 1)
        eng.activation(w2s, w2s, ACT.Exp).then_inc(sem["we"], 1)
        for n in range(X * DQ):
            eng.wait_ge(sem[f"wd{n % DQ}"], 16 * DC * (n // DQ + 1))
            eng.activation(s.wd[:, n * DC:(n + 1) * DC, 0, :], stage[:, n % DQ, :, :], ACT.Copy, scale=W_SCALE)\
               .then_inc(sem["hi"], 1)

    @block.tensor
    def _(eng):
        eng.wait_ge(sem["both"], 1)
        rhs = both.rearrange("p t e -> p (t e)")
        eng.matmul(ps[:, 0, 0:NT * X], c("before"), rhs, start=True, stop=True)
        eng.matmul(ps[:, 1, 0:NT * X], c("ones"), rhs, start=True, stop=True).then_inc(sem["cnt"], 1)

    @block.sync
    def _(eng):
        eng.wait_ge(sem["pad"], 1)
        for n in range(X * DQ):
            x, q = divmod(n, DQ)
            if n >= DQ:
                eng.wait_ge(sem["lo"], n - DQ + 1)
            for i in range(DC):
                h0, size = HC[q * DC + i]
                eng.dma_start(stage[0:size, q, i, :], s.wd_dram[x, h0:h0 + size, :]).then_inc(sem[f"wd{q}"], 16)

    @block.gpsimd
    def _(eng):
        eng.wait_ge(s.rows_zeroed, 16)
        eng.wait_ge(sem["slots"], 1)
        for t in range(NT):
            for i in range(TOP):
                eng.indirect_dma_start(
                    out=s.rows, out_offset=bass.IndirectOffsetOnAxis(ap=s.slots[:, i, t:t + 1], axis=0),
                    in_=s.n2[:, t, :], in_offset=None).then_inc(s.rows_out, 16)
        eng.wait_ge(s.rows_out, 16 * NT * TOP)


def experts(nc, ctx, s):
    ar = Arena(s.scratch, s.scratch_words)
    ar.at = s.wd_words
    xin = ar.take(2, D)
    hid = ar.take(2, HID)
    y = ar.take(2, D)
    xT = ar.take(2, 2, KC, P, dtype=F16)
    hT = ar.take(2, len(HC), P, dtype=F16)
    HH = HID // 2
    PRODUCTS = ((0, 0), (0, 1), (1, 0))
    ps, c = s.psum, s.const
    names = ["x0", "x1", "xTp", "xTh", "xT", "gp", "sil", "hid", "hTp", "hTh", "lo4", "hT", "yp", "y", "out0", "out1"]
    sem = {n: ctx.enter_context(nc.semaphore("exp_" + n)) for n in names}
    block = ctx.enter_context(nc.Block())
    rows = lambda dram, j: dram[bass.ds(j * P, P), :]

    def turns(tile, eng):
        for j in range(3):
            tile(j, j % 2, (j + 1) // 2 + 1, first=j == 0)
        pairs = (XT - 5) // 2
        with eng.Fori(0, pairs) as i:
            tile(2 * i + 3, 1, i + 3)
            tile(2 * i + 4, 0, i + 3)
        for j in range(2 * pairs + 3, XT):
            tile(j, j % 2, (j + 1) // 2 + 1, last=j == XT - 1)

    @block.sync
    def _(eng):
        for r in range(2):
            eng.dma_start(xin[:, r, :], rows(s.rows, r)).then_inc(sem[f"x{r}"], 16)

        def tile(j, r, nth, first=False, last=False):
            if not (isinstance(j, int) and j + 2 >= XT):
                eng.wait_ge(sem["xTp"], j + 1)
                eng.dma_start(xin[:, r, :], rows(s.rows, j + 2)).then_inc(sem[f"x{r}"], 16)
            eng.wait_ge(sem["y"], j + 1)
            eng.dma_start(rows(s.results, j), y[:, r, :]).then_inc(sem[f"out{r}"], 16)

        turns(tile, eng)
        for r in range(2):
            eng.wait_ge(sem[f"out{r}"], 16 * ((XT + 1 - r) // 2))

    @block.tensor
    def _(eng):
        def load(r, nth):
            eng.wait_ge(sem[f"x{r}"], 16 * nth)
            for k in range(KC):
                m = eng.transpose(ps[:, 6, k * P:(k + 1) * P], xin[:, r, k * P:(k + 1) * P], c("ident"))
            m.then_inc(sem["xTp"], 1)

        def down(j, e, first=False):
            eng.wait_ge(sem["hT"], j + 1)
            if not first:
                eng.wait_ge(sem["y"], j)
            n = 0
            for q, (_, size) in enumerate(HC):
                for a, b in PRODUCTS:
                    n += 1
                    m = eng.matmul(ps[:, 7, 0:D], hT[0:size, a, q, :],
                                   s.wd[0:size, bass.ds(e * len(HC) + q, 1), b, :].rearrange("p a n -> p (a n)"),
                                   start=n == 1, stop=n == 3 * len(HC))
            m.then_inc(sem["yp"], 1)

        def expert(j):
            return eng.value_load(s.expert[0:1, bass.ds(j, 1)], min_val=0, max_val=X - 1)

        def tile(j, r, nth, first=False, last=False):
            e = expert(j)
            if first:
                load(0, 1)
            eng.wait_ge(sem["xT"], j + 1)
            for u in range(2):
                if not first:
                    eng.wait_ge(sem["hid"], 2 * j - 1 + u)
                for which, w in enumerate((s.wg, s.wu)):
                    n = 0
                    for k in range(KC):
                        for a, b in PRODUCTS:
                            n += 1
                            m = eng.matmul(ps[:, 2 * u + which, 0:HH], xT[:, r, a, k, :],
                                           w[:, bass.ds(e * KC + k, 1), b, u * HH:(u + 1) * HH]
                                           .rearrange("p a n -> p (a n)"), start=n == 1, stop=n == 3 * KC)
                m.then_inc(sem["gp"], 1)
            if not last:
                load(1 - r, nth)
            if not first:
                down(j - 1, expert(j - 1), first=isinstance(j, int) and j == 1)
            eng.wait_ge(sem["hid"], 2 * j + 2)
            for q, (h0, n) in enumerate(HC):
                m = eng.transpose(ps[0:n, 4 + q // 4, (q % 4) * P:(q % 4 + 1) * P], hid[:, r, h0:h0 + n], c("ident"))
            m.then_inc(sem["hTp"], 1)
            if last:
                down(j, e)

        turns(tile, eng)

    full = HID // P
    rest = HC[-1][1]
    chunk = lambda n: ps[:, 4:6, :].rearrange("p a (q n) -> p (a q) n", n=P)[:, 0:n, :]

    @block.scalar
    def _(eng):
        def x_high(j, r):
            eng.wait_ge(sem["xTp"], j + 1)
            eng.activation(xT[:, r, 0, :, :], ps[:, 6, 0:D].rearrange("p (k n) -> p k n", k=KC), ACT.Copy)\
               .then_inc(sem["xTh"], 1)

        def tile(j, r, nth, first=False, last=False):
            if first:
                x_high(0, 0)
            for u in range(2):
                eng.wait_ge(sem["gp"], 2 * j + u + 1)
                eng.activation(hid[:, r, u * HH:(u + 1) * HH], ps[:, 2 * u, 0:HH], ACT.Silu, scale=1 / W_SCALE)\
                   .then_inc(sem["sil"], 1)
            if not last:
                x_high(j + 1, 1 - r)
            eng.wait_ge(sem["hTp"], j + 1)
            if not first:
                eng.wait_ge(sem["yp"], j)
            eng.activation(hT[:, 0, 0:full, :], chunk(full), ACT.Copy).then_inc(sem["hTh"], 1)
            eng.activation(hT[0:rest, 0, full, :], chunk(full + 1)[0:rest, full, :], ACT.Copy).then_inc(sem["hTh"], 1)

        turns(tile, eng)

    @block.vector
    def _(eng):
        def x_low(j, r):
            eng.wait_ge(sem["xTh"], j + 1)
            eng.tensor_tensor(xT[:, r, 1, :, :], ps[:, 6, 0:D].rearrange("p (k n) -> p k n", k=KC), xT[:, r, 0, :, :],
                              ALU.subtract).then_inc(sem["xT"], 1)

        def result(j, r, stored):
            eng.wait_ge(sem["yp"], j + 1)
            if not isinstance(stored, int) or stored > 0:
                eng.wait_ge(sem[f"out{r}"], 16 * stored)
            eng.tensor_scalar(y[:, r, :], ps[:, 7, 0:D], 1 / W_SCALE, None, ALU.mult).then_inc(sem["y"], 1)

        def tile(j, r, nth, first=False, last=False):
            if first:
                x_low(0, 0)
            for u in range(2):
                eng.wait_ge(sem["sil"], 2 * j + u + 1)
                half = hid[:, r, u * HH:(u + 1) * HH]
                eng.scalar_tensor_tensor(half, ps[:, 2 * u + 1, 0:HH], 1 / W_SCALE, half, ALU.mult, ALU.mult)\
                   .then_inc(sem["hid"], 1)
            if not last:
                x_low(j + 1, 1 - r)
            if not first:
                result(j - 1, 1 - r, nth - 2)
            eng.wait_ge(sem["hTh"], 2 * j + 2)
            eng.tensor_tensor(hT[:, 1, 0:full, :], chunk(full), hT[:, 0, 0:full, :], ALU.subtract)\
               .then_inc(sem["lo4"], 1)
            eng.tensor_tensor(hT[0:rest, 1, full, :], chunk(full + 1)[0:rest, full, :], hT[0:rest, 0, full, :],
                              ALU.subtract).then_inc(sem["hT"], 1)
            if last:
                result(j, r, j // 2)

        turns(tile, eng)


def combine(nc, ctx, s, out):
    ar = Arena(s.scratch, s.scratch_words)
    got = ar.take(NT * TOP, D)
    names = ["y"]
    sem = {n: ctx.enter_context(nc.semaphore("comb_" + n)) for n in names}
    back = [ctx.enter_context(nc.semaphore(f"comb_back{i}")) for i in range(NT)]
    done = ctx.enter_context(nc.semaphore("comb_done"))
    block = ctx.enter_context(nc.Block())
    out_t = out.rearrange("(t p) d -> p t d", p=P)

    @block.gpsimd
    def _(eng):
        for t in range(NT):
            for i in range(TOP):
                eng.indirect_dma_start(
                    out=got[:, t * TOP + i, :], out_offset=None, in_=s.results,
                    in_offset=bass.IndirectOffsetOnAxis(ap=s.slots[:, i, t:t + 1], axis=0)).then_inc(back[t], 16)

    @block.vector
    def _(eng):
        for t in range(NT):
            eng.wait_ge(back[t], 16 * TOP)
            for i in range(TOP):
                m = eng.scalar_tensor_tensor(s.h[:, t, :], got[:, t * TOP + i, :], s.w[:, i, t:t + 1], s.h[:, t, :],
                                             ALU.mult, ALU.add)
                m.then_inc(sem["y"], 1)
                eng.wait_ge(sem["y"], t * TOP + i + 1)

    @block.sync
    def _(eng):
        for t in range(0, NT, 2):
            eng.wait_ge(sem["y"], (t + 2) * TOP)
            eng.dma_start(out_t[:, t:t + 2, :], s.h[:, t:t + 2, :]).then_inc(done, 16)
        eng.wait_ge(done, 16 * NT // 2)


class Shared:
    pass


def build(nc, a, out):
    s = Shared()
    with ExitStack() as ctx:
        sb = lambda name, shape, dt=F32: ctx.enter_context(nc.sbuf_tensor(name, shape, dt))
        sem = lambda name: ctx.enter_context(nc.semaphore(name))
        s.psum = ctx.enter_context(nc.psum_tensor("psum", [P, 8, 512], F32))
        s.h = sb("h", [P, NT, D])
        s.scratch_words = 17536
        s.scratch = sb("scratch", [P, s.scratch_words])
        s.junk = sb("junk", [P, 4])
        tables = {}

        def table_views(tile, packed_tables):
            for name, (at, n) in packed_tables[1].items():
                tables[name] = tile[:, at:at + n]

        const = sb("const", [P, CONST[0].shape[1]])
        const_half = sb("const_half", [P, CONST_HALF[0].shape[1]], F16)
        table_views(const, CONST)
        table_views(const_half, CONST_HALF)
        s.const = lambda name: tables[name]
        s.ids = sb("ids", [P, NT], I32)
        s.table = a["table"]
        s.n2 = sb("n2", [P, NT, D])
        w3 = lambda name, n: sb(name, [P, KC, n])
        early = Arena(s.n2[:, :, :].rearrange("p t d -> p (t d)"), NT * D)
        s.gwq, s.gwk, s.wgk1, s.wvg, s.gwo = (early.take(KC, n) for n in (P, P, LOW, 2 * D, D))
        s.wgk2 = early.take(P)
        s.wg, s.wu = (sb(n, [P, X * KC, 2, HID], F16) for n in ("w_gate", "w_up"))
        s.wd_words = X * len(HC) * D
        s.wd = s.scratch[:, 0:s.wd_words].bitcast(F16).rearrange("p (q a n) -> p q a n", a=2, n=D)
        s.wgu_dram = [a[n].rearrange("x (k p) n -> (x k) p n", p=P) for n in ("wg", "wu")]
        s.wd_dram = a["wd"]
        sem_zero = sem("zero_set")
        s.rows = nc.dram_tensor("rows", [ROWS, D], F32).ap()
        s.results = nc.dram_tensor("results", [ROWS, D], F32).ap()
        s.slots, s.expert = sb("slots", [P, TOP, NT], I32), sb("expert", [P, XT], I32)
        w_choice = sb("w_choice", [P, TOP, NT]); s.w = w_choice[:, :, :]
        s.rows_out, s.rows_zeroed = sem("rows_out"), sem("rows_zeroed")
        s.tok_bias, zero = (early.take(D) for _ in range(2))
        const_first = early.take(CONST_FIRST[0].shape[1])
        table_views(const_first, CONST_FIRST)
        s.bgk2_t = sb("bgk2", [P, 1]); s.bgk2 = s.bgk2_t[:, :]
        s.gnw_t = sb("gnw", [P, 1]); s.gnw_half = s.gnw_t[:, :]
        s.ids_in, s.const_in, s.gla_w_in, s.vec_in = sem("ids_in"), sem("const_in"), sem("gla_w_in"), sem("vec_in")
        s.rows_in = [sem(f"rows_in{b}") for b in range(B)]
        s.gla_w_n, s.vec_n = 16 * 7, 16 * 3 + 1
        s.logits = sb("logits", [P, NT, X])
        s.wqkv, s.wo, s.wr = w3("wqkv", 3 * D), w3("wo", D), w3("wr", X)
        s.g1_t = sb("g1", [P, KC]); s.g1 = s.g1_t[:, :]
        s.g2_t = sb("g2", [P, D]); s.g2 = s.g2_t[:, :]
        s.ident16, s.future_k, s.future_q = (tables[n] for n in ("ident16", "future_k", "future_q"))
        s.att_w_in = sem("att_w_in")
        s.att_w_n = 16 * 7 + 1
        block = nc.Block()
        with block:
            @block.sync
            def _(eng):
                eng.dma_start(s.ids[:, :], a["ids"]).then_inc(s.ids_in, 16)
                for tile, name in ((const[:, :], "const"), (const_first, "const_first"), (const_half[:, :], "const_half")):
                    eng.dma_start(tile, a[name]).then_inc(s.const_in, 16)
                eng.dma_start(s.tok_bias, a["tok_bias"].partition_broadcast(P)).then_inc(s.vec_in, 16)
                kc = lambda name: a[name].rearrange("(k p) n -> p k n", p=P)
                eng.dma_start(s.gwq[:, :, :], kc("Wq")).then_inc(s.gla_w_in, 16)
                eng.dma_start(s.gwk[:, :, :], kc("Wk")).then_inc(s.gla_w_in, 16)
                eng.dma_start(s.wgk1[:, :, :], kc("Wgk1")).then_inc(s.gla_w_in, 16)
                eng.dma_start(s.wgk2[0:LOW, :], a["Wgk2"]).then_inc(s.gla_w_in, 16)
                eng.dma_start(s.wvg[:, :, 0:D], kc("Wv")).then_inc(s.gla_w_in, 16)
                eng.dma_start(s.wvg[:, :, D:2 * D], kc("Wg")).then_inc(s.gla_w_in, 16)
                eng.dma_start(s.gwo[:, :, :], kc("Wo")).then_inc(s.gla_w_in, 16)
                for i, name in enumerate(("wq", "wk", "wv")):
                    eng.dma_start(s.wqkv[:, :, i * D:(i + 1) * D], kc(name)).then_inc(s.att_w_in, 16)
                eng.dma_start(s.wo[:, :, :], kc("wo")).then_inc(s.att_w_in, 16)
                eng.dma_start(s.wr[:, :, :], kc("w_router")).then_inc(s.att_w_in, 16)
                eng.dma_start(s.g1, a["g1"]).then_inc(s.att_w_in, 16)
                eng.dma_start(s.g2, a["g2"].partition_broadcast(P)).then_inc(s.att_w_in, 16)
                eng.dma_start(s.bgk2, a["bgk2"]).then_inc(s.vec_in, 16)
                eng.dma_start(s.gnw_half, a["gnw"]).then_inc(s.vec_in, 16)

                eng.wait_ge(sem_zero, 1)
                eng.dma_start(s.rows.rearrange("(j p) d -> p j d", p=P), spread(zero, 1, XT)).then_inc(s.rows_zeroed, 16)

            @block.vector
            def _(eng):
                eng.memset(s.junk[:, :], 0.0)
                eng.memset(zero, 0.0).then_inc(sem_zero, 1)
                eng.wait_ge(s.vec_in, 48)
                eng.tensor_scalar(s.gnw_half, s.gnw_half, 0.5, None, ALU.mult).then_inc(s.vec_in, 1)
        with ExitStack() as stage:
            linear_attention(nc, stage, s)
        with ExitStack() as stage:
            softmax_attention(nc, stage, s)
        with ExitStack() as stage:
            routing(nc, stage, s)
        with ExitStack() as stage:
            experts(nc, stage, s)
        with ExitStack() as stage:
            combine(nc, stage, s, out)


def kernel(**inputs):
    import concourse.bacc as bacc
    from concourse.bass_utils import run_bass_kernel_spmd as run

    src = {
        "ids": inputs["x"].reshape(NT, P).T,
        "table": inputs["L0_tok_weight"].T,
        "tok_bias": inputs["L0_tok_bias"],
        "const": CONST[0],
        "const_first": CONST_FIRST[0],
        "const_half": CONST_HALF[0],
    }
    for n in ("Wq", "Wk", "Wv", "Wgk1", "Wgk2", "bgk2", "Wg", "gnw", "Wo"):
        src[n] = inputs["L0_attn_" + n]
    for n in ("wq", "wk", "wv", "wo", "w_router", "g1", "g2", "wg", "wu", "wd"):
        src[n] = inputs["L0_ffn_" + n]
    src["g1"] = src["g1"].reshape(KC, P).T
    src["gnw"] = np.tile(src["gnw"], P // DV).reshape(P, 1)
    src["bgk2"] = src["bgk2"].reshape(P, 1)
    nc = bacc.Bacc("TRN2", target_bir_lowering=False, num_devices=1)
    arrays, aps = {}, {}
    for name, v in src.items():
        v = np.ascontiguousarray(v)
        arrays["in_" + name] = v
        aps[name] = nc.dram_tensor("in_" + name, list(v.shape), mybir.dt.from_np(v.dtype), kind="ExternalInput").ap()
    out = nc.dram_tensor("out_y", [NT * P, D], F32, kind="ExternalOutput").ap()
    build(nc, aps, out)
    r = run(nc, [arrays], core_ids=[0])
    return r.results[0]["out_y"].reshape(B, T, D)
```

```python
from contextlib import ExitStack

import numpy as np

import concourse.bass as bass
from concourse import mybir

ALU = mybir.AluOpType
ACT = mybir.ActivationFunctionType
AX = mybir.AxisListType
F32 = mybir.dt.float32
F16 = mybir.dt.float16
I32 = mybir.dt.int32

P = 128
B, T, D = 4, 512, 256
KC = D // P
TT = T // P
NT = B * TT
H = 16
DK, DV = 8, 16
HPG, G = 4, 4
LOW = 16
SUB = 64
HD = 16
UH = 8
U = B * H // UH
VW = UH * (HD + 1) + 32 - (HD + 1)
ST = 64
X, HID, TOP = 8, 704, 2
HC = [(c * P, min(P, HID - c * P)) for c in range(-(-HID // P))]
XT = (NT * P * TOP + X * (P - 1)) // P
W_SCALE = 256.0
STAGES = 6
DC, DQ = 2, len(HC) // 2
NEVER = -60000.0


def shape_constants():
    i = np.arange(P)
    inv = 1.0 / 10000.0 ** (np.arange(0, HD, 2, dtype=np.float32) / HD)
    ang = np.einsum("i,j->ij", np.arange(T, dtype=np.float32), inv)
    cos = np.cos(np.concatenate([ang, ang], -1)).astype(np.float32)
    sin = np.sin(np.concatenate([ang, ang], -1)).astype(np.float32)
    sin[:, :HD // 2] *= -1
    tile = lambda a: np.ascontiguousarray(a.reshape(TT, P, HD).transpose(1, 0, 2).reshape(P, -1))
    gate = np.ones(T, np.float32)
    gate[::SUB] = 0
    rows = H * DK
    e_reset = np.ones((X, NT), np.float32)
    e_reset[:, 0] = 0
    f = lambda a: np.ascontiguousarray(a, np.float32)
    parts = [
        ("ident", f(np.eye(P))),
        ("upto", f(i[:, None] <= i[None, :])),
        ("before", f(i[:, None] < i[None, :])),
        ("ones", f(np.ones((P, P)))),
        ("cos", tile(cos)), ("sin", tile(sin)),
        ("powers", f(np.broadcast_to(np.float32(-0.5), (P, 2 * TT)))),
        ("rank8", f(np.broadcast_to(X - np.arange(X), (P, X)))),
        ("ereset", f(np.broadcast_to(e_reset.reshape(-1), (P, X * NT)))),
        ("eps", f(np.full((P, 1), 1e-5))),
        ("count", f(np.broadcast_to(i, (P, P)))),
        ("token1", f(i[:, None] + P * np.arange(NT)[None, :] + 1)),
        ("spare1", f(i[:, None] + P * (TOP * NT + np.arange(XT)[None, :]) + 1)),
    ]
    heads = i // DV
    first = [
        ("subreset", f(np.broadcast_to(gate, (P, T)))),
        ("headblock", f(np.arange(rows)[:, None] // DK == np.arange(H * DV)[None, :] // DV)),
        ("headmean", f((heads[:, None] == heads[None, :]) / DV)),
        ("headmask", f((np.arange(rows)[:, None] // DK) % HPG == np.arange(HPG)[None, :])),
    ]
    half = [
        ("ident16", np.eye(P)),
        ("future_k", np.where(i[None, :] > i[:, None], NEVER, 0)),
        ("future_q", np.where(i[:, None] > i[None, :], NEVER, 0)),
    ]
    return packed(parts), packed(first), packed([(n, a.astype(np.float16)) for n, a in half])


def packed(parts):
    at, where = 0, {}
    for name, a in parts:
        where[name] = (at, a.shape[1])
        at += a.shape[1]
    return np.ascontiguousarray(np.concatenate([a for _, a in parts], 1)), where


CONST, CONST_FIRST, CONST_HALF = shape_constants()


class Arena:

    def __init__(self, tensor, words):
        self.tensor, self.words, self.at = tensor, words, 0

    def take(self, *shape, dtype=F32):
        n = int(np.prod(shape))
        words = n if dtype != F16 else n // 2
        assert self.at + words <= self.words, (self.at, words, self.words)
        ap = self.tensor[:, self.at:self.at + words]
        self.at += words
        if dtype != F32:
            ap = ap.bitcast(dtype)
        if len(shape) > 1:
            names = "abcd"[:len(shape)]
            ap = ap.rearrange(f"p ({' '.join(names)}) -> p {' '.join(names)}",
                              **{k: v for k, v in zip(names, shape)})
        return ap


def spread(ap, axis, n):
    ap = ap.unsqueeze(axis)
    shape = list(ap.shape)
    shape[axis] = n
    return ap.broadcast_to(shape)


class Order:

    def __init__(self, eng, sem):
        self.eng, self.sem, self.n = eng, sem, 0

    def after(self, ins):
        self.n += 1
        ins.then_inc(self.sem, 1)
        self.eng.wait_ge(self.sem, self.n)


def linear_attention(nc, ctx, s):
    ar = Arena(s.scratch, s.scratch_words)
    xn = ar.take(TT, D)
    xT = ar.take(KC, T)
    z1T = ar.take(T)
    zb = ar.take(T)
    e1 = ar.take(T)
    ls = ar.take(T)
    e_in = ar.take(T)
    e_inv = ar.take(T)
    e_out = ar.take(T)
    qd = ar.take(TT, P)
    qi = ar.take(TT, P)
    qx = ar.take(HPG, TT, P)
    ka = ar.take(TT, P)
    kb = ar.take(TT, P)
    ks = ar.take(TT, P)
    ksT = ar.take(TT, P)
    vz = ar.take(TT, H // 2, 4, DV)
    att = ar.take(G, HPG, P)
    state = ar.take(2, D)
    dstate = zb[:, 0:D]
    dec = ar.take(TT)
    th = ls, zb
    sg = ar.take(KC, T)
    ogT = ar.take(KC, T)
    stats = ar.take(TT, 6)
    mv = ar.take(TT, 2)
    rstd = ar.take(TT)
    ps, c = s.psum, s.const
    oT = lambda k: ps[:, 4 + k, :]
    v_of = lambda t: vz[:, t, :, 0:4:3, :]
    names = ["h", "mv", "rstd", "xn", "xTp", "xT", "z1p", "z1", "gkp", "qp", "kp", "vp", "v", "gp", "th", "sg",
             "zb", "lsig", "ls", "dout", "exps", "kst", "qx", "ksTp", "ksT", "ap", "att", "used", "sp", "sadd",
             "oT", "sq", "msp", "ln", "rinv", "og", "yp", "dve", "act", "pool"]
    sem = {n: ctx.enter_context(nc.semaphore("gla_" + n)) for n in names}
    block = ctx.enter_context(nc.Block())

    @block.gpsimd
    def _(eng):
        eng.wait_ge(s.const_in, 32)
        o = Order(eng, sem["pool"])
        for b in range(B):
            eng.wait_ge(sem["mv"], b + 1)
            if b:
                eng.wait_ge(sem["xn"], b * TT)
            o.after(eng.tensor_scalar(rstd, mv[:, :, 1], 1e-5, None, ALU.add))
            eng.tensor_tensor(rstd, rstd, c("powers")[:, 0:TT], ALU.pow).then_inc(sem["rstd"], 1)
            if b == 0:
                s.gather_tokens(eng, range(TT, NT))

    @block.sync
    def _(eng):
        s.load_attention_weights(eng)

    @block.scalar
    def _(eng):
        eng.wait_ge(s.const_in, 32)
        o = Order(eng, sem["act"])

        def x_and_low_rank(b):
            for k in range(KC):
                eng.wait_ge(sem["xTp"], b * KC + k + 1)
                eng.activation(xT[:, k, :], ps[:, k, :], ACT.Copy).then_inc(sem["xT"], 1)
            eng.wait_ge(sem["z1p"], b + 1)
            eng.activation(z1T[0:LOW, :], ps[0:LOW, 6, :], ACT.Copy).then_inc(sem["z1"], 1)

        def decays(b):
            eng.wait_ge(sem["zb"], b + 1)
            o.after(eng.activation(e1, zb, ACT.Abs))
            o.after(eng.activation(e1, e1, ACT.Exp, scale=-1.0))
            eng.activation(e1, e1, ACT.Ln, bias=1.0).then_inc(sem["lsig"], 1)
            for t in range(TT):
                eng.wait_ge(sem["vp"], b * 2 + t // 2 + 1)
                eng.activation(v_of(t), ps[:, t // 2, t % 2 * D:(t % 2 + 1) * D].rearrange(
                    "p (a j d) -> p a j d", j=2, d=DV), ACT.Copy).then_inc(sem["v"], 1)
            eng.wait_ge(sem["ls"], b + 1)
            eng.activation(e_in, ls, ACT.Exp, scale=1.0 / 16).then_inc(sem["exps"], 1)
            eng.activation(e_inv, ls, ACT.Exp, scale=-1.0 / 16).then_inc(sem["exps"], 1)
            eng.wait_ge(sem["dout"], b + 1)
            eng.activation(e_out, e_out, ACT.Exp, scale=1.0 / 16).then_inc(sem["exps"], 1)
            for k in range(KC):
                eng.wait_ge(sem["gp"], b * KC + k + 1)
                if k == 0:
                    eng.wait_ge(sem["exps"], b * 3 + 3)
                eng.activation(th[k], ps[:, 6 + k, :], ACT.Tanh, scale=0.5).then_inc(sem["th"], 1)
            eng.wait_ge(sem["ksTp"], b + 1)
            eng.activation(ksT, ps[:, 4, :].rearrange("p (t n) -> p t n", t=TT), ACT.Copy).then_inc(sem["ksT"], 1)
        def one_over_rms(b):
            for k in range(KC):
                eng.wait_ge(sem["msp"], b * KC + k + 1)
                eng.activation(ogT[:, k, :], ps[:, 2 + k, :], ACT.Ln, bias=c("eps")).then_inc(sem["ln"], 1)
            for k in range(KC):
                eng.wait_ge(sem["ln"], b * KC + k + 1)
                eng.activation(ogT[:, k, :], ogT[:, k, :], ACT.Exp, scale=-0.5).then_inc(sem["rinv"], 1)

        x_and_low_rank(0)
        for b in range(B):
            decays(b)
            for k in range(KC):
                eng.wait_ge(sem["oT"], b + 1)
                if b:
                    eng.wait_ge(sem["yp"], b * 2)
                eng.activation(ogT[:, k, :], oT(k), ACT.Square).then_inc(sem["sq"], 1)
            if b + 1 < B:
                x_and_low_rank(b + 1)
            one_over_rms(b)

    @block.tensor
    def _(eng):
        eng.wait_ge(s.const_in, 32)

        def transposes(b):
            for k in range(KC):
                for t in range(TT):
                    if k == 0:
                        eng.wait_ge(sem["xn"], b * TT + t + 1)
                    m = eng.transpose(ps[:, k, t * P:(t + 1) * P], xn[:, t, k * P:(k + 1) * P], c("ident"))
                m.then_inc(sem["xTp"], 1)

        def project(bank, w, n, name):
            for k in range(KC):
                m = eng.matmul(ps[0:n, bank, :], w[:, k, :], xT[:, k, :], start=k == 0, stop=k == KC - 1)
            m.then_inc(sem[name], 1)

        def gate_projections(b):
            eng.wait_ge(s.gla_w_in, s.gla_w_n)
            eng.wait_ge(sem["xT"], (b + 1) * KC)
            project(6, s.wgk1, LOW, "z1p")

        def projections(b):
            eng.wait_ge(sem["z1"], b + 1)
            eng.matmul(ps[:, 7, :], s.wgk2[0:LOW, :], z1T[0:LOW, :], start=True, stop=True).then_inc(sem["gkp"], 1)
            if b:
                eng.wait_ge(sem["ln"], b * KC)
            project(2, s.gwq, P, "qp")
            project(3, s.gwk, P, "kp")
            for t in range(TT):
                for k in range(KC):
                    m = eng.matmul(ps[:, t // 2, t % 2 * D:(t % 2 + 1) * D], xT[:, k, t * P:(t + 1) * P],
                                   s.wvg[:, k, 0:D], start=k == 0, stop=k == KC - 1)
                if t % 2:
                    m.then_inc(sem["vp"], 1)
            project(6, s.wvg[:, :, D:D + P], P, "gp")
            eng.wait_ge(sem["zb"], b + 1)
            project(7, s.wvg[:, :, D + P:2 * D], P, "gp")

        def chunks(b):
            eng.wait_ge(sem["v"], (b + 1) * TT)
            eng.wait_ge(sem["qx"], b + 1)
            def scores(t):
                for i, k in enumerate((ka, kb)):
                    for g in range(G):
                        if t and i == 0:
                            eng.wait_ge(sem["att"], b * TT * G + (t - 1) * G + g + 1)
                        m = eng.matmul(
                            ps[:, g, :].rearrange("p (j n) -> p j n", j=HPG)[:, :, i * SUB:(i + 1) * SUB],
                            k[32 * g:32 * g + 32, t, :], qx[32 * g:32 * g + 32, :, t, i * SUB:(i + 1) * SUB],
                            start=True, stop=True)
                        if i:
                            m.then_inc(sem["ap"], 1)

            scores(0)
            eng.wait_ge(sem["kst"], b + 1)
            if b:
                eng.wait_ge(sem["h"], b * 2)
            for t in range(TT):
                m = eng.transpose(ps[:, 4, t * P:(t + 1) * P], ks[:, t, :], c("ident"))
            m.then_inc(sem["ksTp"], 1)
            for t in range(TT):
                if t < TT - 1:
                    if t == 0:
                        eng.wait_ge(sem["ksT"], b + 1)
                        eng.wait_ge(sem["sg"], (b + 1) * KC)
                    eng.matmul(ps[:, 7, 0:D], ksT[:, t, :], v_of(t), start=True, stop=True).then_inc(sem["sp"], 1)
                    scores(t + 1)
                cols = slice(t * P, (t + 1) * P)
                for g in range(G):
                    eng.wait_ge(sem["att"], b * TT * G + t * G + g + 1)
                    for j in (0, 2, 1, 3):
                        pair = (g * HPG + j) // 2
                        rows = slice(32 * (pair % 4), 32 * (pair % 4) + 32)
                        m = eng.matmul(ps[rows, 4 + pair // 4, cols],
                                       vz[:, t, pair, 2 * (j % 2):2 * (j % 2) + 2, :].rearrange("p a d -> p (a d)"),
                                       att[:, g, j, :], start=j % 2 == 0, stop=True, skip_group_check=True)
                    m.then_inc(sem["used"], 1)
                if t:
                    eng.wait_ge(sem["sadd"], b * (TT - 1) + t)
                    for k in range(KC):
                        m = eng.matmul(ps[:, 4 + k, cols], state[:, t % 2, k * P:(k + 1) * P], qi[:, t, :],
                                       start=False, stop=True, skip_group_check=True)
            m.then_inc(sem["oT"], 1)

        def mean_squares(b):
            for k in range(KC):
                eng.wait_ge(sem["sq"], b * KC + k + 1)
                eng.matmul(ps[:, 2 + k, :], c("headmean"), ogT[:, k, :], start=True, stop=True)\
                   .then_inc(sem["msp"], 1)

        def outputs(b):
            eng.wait_ge(sem["og"], (b + 1) * KC)
            for t in range(TT):
                for k in range(KC):
                    m = eng.matmul(ps[:, 4 + t // 2, (t % 2) * D:(t % 2 + 1) * D], ogT[:, k, t * P:(t + 1) * P],
                                   s.gwo[:, k, :], start=k == 0, stop=k == KC - 1)
                if t % 2:
                    m.then_inc(sem["yp"], 1)

        transposes(0)
        gate_projections(0)
        projections(0)
        for b in range(B):
            chunks(b)
            eng.wait_ge(sem["att"], (b + 1) * TT * G)
            if b + 1 < B:
                transposes(b + 1)
            mean_squares(b)
            if b + 1 < B:
                gate_projections(b + 1)
                projections(b + 1)
            outputs(b)

    @block.vector
    def _(eng):
        eng.wait_ge(s.const_in, 32)
        o = Order(eng, sem["dve"])
        o.after(eng.memset(ka[:, :, SUB:P], 0.0))
        o.after(eng.memset(vz[:, :, :, 1:3, :], 0.0))
        eng.wait_ge(s.vec_in, s.vec_n)

        def moments(b):
            hb = s.h[:, b * TT:(b + 1) * TT, :]
            eng.wait_ge(s.rows_in[b], 16 * TT)
            o.after(eng.tensor_tensor(hb, hb, spread(s.tok_bias, 1, TT), ALU.add))
            for t in range(TT):
                eng.bn_stats(stats[:, t, :], s.h[:, b * TT + t, :]).then_inc(sem["dve"], 1)
            o.n += TT
            eng.wait_ge(sem["dve"], o.n)
            for t in range(TT):
                m = eng.bn_aggr(mv[:, t, :], stats[:, t, :])
                if t < TT - 1:
                    m.then_inc(sem["dve"], 1)
            o.n += TT - 1
            eng.wait_ge(sem["dve"], o.n)
            m.then_inc(sem["mv"], 1)

        def layernorm(b):
            eng.wait_ge(sem["mv"], b + 1)
            eng.wait_ge(sem["rstd"], b + 1)
            if b:
                eng.wait_ge(sem["xTp"], b * KC)
            for t in range(TT):
                eng.tensor_scalar(xn[:, t, :], s.h[:, b * TT + t, :], mv[:, t, 0:1], rstd[:, t:t + 1],
                                  ALU.subtract, ALU.mult).then_inc(sem["xn"], 1)

        def gate_bias(b):
            eng.wait_ge(sem["gkp"], b + 1)
            eng.tensor_scalar(zb, ps[:, 7, :], s.bgk2, None, ALU.add).then_inc(sem["zb"], 1)

        def queries_and_keys(b):
            eng.wait_ge(sem["zb"], b + 1)
            eng.wait_ge(sem["lsig"], b + 1)
            o.after(eng.scalar_tensor_tensor(zb, zb, 0.0, e1, ALU.min, ALU.subtract))
            eng.tensor_tensor_scan(ls, c("subreset"), zb, 0.0, ALU.mult, ALU.add).then_inc(sem["ls"], 1)
            eng.wait_ge(sem["ls"], b + 1)
            ls_s = ls.rearrange("p (a n) -> p a n", n=SUB)
            eng.tensor_tensor(e_out.rearrange("p (a n) -> p a n", n=SUB),
                              ls_s[:, :, SUB - 1:SUB].broadcast_to([P, T // SUB, SUB]), ls_s,
                              ALU.subtract).then_inc(sem["dout"], 1)
            ei, ev, eo = (x.rearrange("p (t n) -> p t n", n=P) for x in (e_in, e_inv, e_out))
            eng.wait_ge(sem["exps"], b * 3 + 2)
            eng.wait_ge(sem["qp"], b + 1)
            o.after(eng.scalar_tensor_tensor(qd, ps[:, 2, :].rearrange("p (t n) -> p t n", n=P), DK ** -0.5, ei,
                                             ALU.mult, ALU.mult))
            kp = ps[:, 3, :].rearrange("p (t n) -> p t n", n=P)
            lo, hi = slice(0, SUB), slice(SUB, P)
            eng.wait_ge(sem["kp"], b + 1)
            o.after(eng.tensor_tensor(ka[:, :, lo], kp[:, :, lo], ev[:, :, lo], ALU.mult))
            o.after(eng.tensor_tensor(kb[:, :, hi], kp[:, :, hi], ev[:, :, hi], ALU.mult))
            eng.wait_ge(sem["exps"], (b + 1) * 3)
            o.after(eng.tensor_tensor(kb[:, :, lo], kp[:, :, lo], eo[:, :, lo], ALU.mult))
            o.after(eng.tensor_tensor(ks[:, :, hi], kp[:, :, hi], eo[:, :, hi], ALU.mult))
            for j in range(HPG):
                m = eng.tensor_scalar(qx[:, j, :, :], qd, c("headmask")[:, j:j + 1], None, ALU.mult)
                if j < HPG - 1:
                    o.after(m)
            m.then_inc(sem["qx"], 1)
            eng.tensor_tensor(ks[:, :, lo], kb[:, :, lo], ei[:, :, P - 1:P].broadcast_to([P, TT, SUB]),
                              ALU.mult).then_inc(sem["kst"], 1)
            eng.wait_ge(sem["kst"], b + 1)
            o.after(eng.tensor_copy(qi[:, :, lo], qd[:, :, lo]))
            o.after(eng.tensor_tensor(qi[:, :, hi], qd[:, :, hi], ei[:, :, SUB - 1:SUB].broadcast_to([P, TT, SUB]),
                                      ALU.mult))
            o.after(eng.tensor_tensor(dec.unsqueeze(2), ei[:, :, SUB - 1:SUB], ei[:, :, P - 1:P], ALU.mult))

        def gate(b):
            for k in range(KC):
                eng.wait_ge(sem["th"], b * KC + k + 1)
                eng.scalar_tensor_tensor(sg[:, k, :], th[k], 1.0, ps[:, 6 + k, :], ALU.add, ALU.mult)\
                   .then_inc(sem["sg"], 1)
                eng.wait_ge(sem["sg"], b * KC + k + 1)

        def chunks(b):
            for t in range(TT):
                for g in range(G):
                    n = t * G + g
                    eng.wait_ge(sem["ap"], b * TT * G + n + 1)
                    if t:
                        eng.wait_ge(sem["used"], b * TT * G + n - G + 1)
                    eng.tensor_tensor(att[:, g, :, :], ps[:, g, :].rearrange("p (j n) -> p j n", j=HPG),
                                      spread(c("upto"), 1, HPG), ALU.mult).then_inc(sem["att"], 1)
                    if g == 1 and t < TT - 1:
                        eng.wait_ge(sem["sp"], b * (TT - 1) + t + 1)
                        own = dstate if t else state[:, 1, :]
                        m = eng.tensor_tensor(own, ps[:, 7, 0:D], c("headblock"), ALU.mult)
                        if t:
                            o.after(m)
                            m = eng.scalar_tensor_tensor(state[:, (t + 1) % 2, :], state[:, t % 2, :],
                                                         dec[:, t:t + 1], dstate, ALU.mult, ALU.add)
                        m.then_inc(sem["sadd"], 1)
                        eng.wait_ge(sem["sadd"], b * (TT - 1) + t + 1)
                if b + 1 < B and t == 1:
                    moments(b + 1)
                if b + 1 < B and t == 2:
                    layernorm(b + 1)

        def normalise(b):
            for k in range(KC):
                eng.wait_ge(sem["rinv"], b * KC + k + 1)
                o.after(eng.scalar_tensor_tensor(ogT[:, k, :], oT(k), s.gnw_half, ogT[:, k, :], ALU.mult, ALU.mult))
                eng.tensor_tensor(ogT[:, k, :], ogT[:, k, :], sg[:, k, :], ALU.mult).then_inc(sem["og"], 1)

        def add_outputs(b):
            for i in range(2):
                eng.wait_ge(sem["yp"], b * 2 + i + 1)
                hh = s.h[:, b * TT + 2 * i:b * TT + 2 * i + 2, :]
                eng.tensor_tensor(hh, hh, ps[:, 4 + i, :].rearrange("p (t d) -> p t d", t=2),
                                  ALU.add).then_inc(sem["h"], 1)

        moments(0)
        layernorm(0)
        gate_bias(0)
        for b in range(B):
            queries_and_keys(b)
            if b:
                add_outputs(b - 1)
            gate(b)
            chunks(b)
            if b + 1 < B:
                gate_bias(b + 1)
            normalise(b)
        add_outputs(B - 1)


def softmax_attention(nc, ctx, s):
    ar = Arena(s.scratch, s.scratch_words)
    x = ar.take(TT, D)
    heads = ar.take(TT, D)
    n1T = ar.take(KC, T)
    oT = ar.take(KC, T)
    nT = oT
    qk = ar.take(2, 2 * UH * HD)
    rot = ar.take(2 * UH * HD)
    sq = ar.take(TT, UH, ST, dtype=F16)
    sk = ar.take(TT, UH, ST, dtype=F16)
    qT = ar.take(2, UH // 2, T, dtype=F16)
    kT = ar.take(2, UH // 2, T, dtype=F16)
    va = ar.take(2, TT, VW)
    vh = va[:, :, :, 0:UH * (HD + 1)].rearrange("p u t (h d) -> p u t h d", h=UH)
    pT = ar.take(2, 10 * P)
    oq = ar.take(T)
    mx = ar.take(TT, UH)
    rden = ar.take(TT, 4)
    stats, mv, rn = ar.take(TT, 6), ar.take(B, TT, 2), ar.take(B, 2, TT)
    ssq, r2 = ar.take(TT), ar.take(TT)
    junk = ar.take(D)
    stage = ar.take(2, HID)
    ps, c = s.psum, s.const
    OUT, TAIL, MAXB, STK = 3, 4, 5, 7
    FILLS = []
    for t in range(TT):
        n = min(UH // 2, TT // (t + 1))
        FILLS.append([range(h + odd, h + 2 * n, 2) for h in range(0, UH, 2 * n) for odd in range(2)])
    BEFORE = [sum(len(f) for f in FILLS[:t]) for t in range(TT + 1)]
    filling = lambda u, t, k: u * BEFORE[TT] + BEFORE[t] + k
    half_of = lambda t, i: range(i * len(FILLS[t]) // 2, (i + 1) * len(FILLS[t]) // 2)
    at = {0: 0, 1: 4, 3: 7, 2: 8}
    names = ["mv", "rn", "n1", "n1Tp", "n1T", "pj", "va", "qkr", "rope", "hi", "stk", "sTp", "stT", "mp", "mx",
             "neg", "s2Tp", "q2T", "pp", "exp", "pv", "oq", "oqTp", "on", "oTp", "oT", "yp", "x", "g", "ssq",
             "r2", "n2", "nTp", "nT", "lp", "lg", "split", "w0", "w1", "dve", "act", "pool"]
    sem = {n: ctx.enter_context(nc.semaphore("att_" + n)) for n in names}
    block = ctx.enter_context(nc.Block())
    has_next = lambda u: u + 1 < U
    new_sequence = lambda u: u >= 0 and u % 2 == 0 and u // 2 + 1 < B
    closing = lambda u: u >= 2 and u % 2 == 0
    routing_turn = lambda u: u >= 3 and u % 2

    @block.gpsimd
    def _(eng):
        o = Order(eng, sem["pool"])

        def split(n):
            eng.wait_ge(sem[f"w{n % 2}"], 16 * (n // 2 + 1))
            w, w16 = stage[:, n % 2, :], (s.wg, s.wu)[n % 2]
            o.after(eng.tensor_scalar(w, w, W_SCALE, None, ALU.mult))
            o.after(eng.tensor_copy(w16[:, n // 2, 0, :], w))
            eng.tensor_tensor(w16[:, n // 2, 1, :], w, w16[:, n // 2, 0, :], ALU.subtract).then_inc(sem["split"], 1)

        def norm_factors(b):
            eng.wait_ge(sem["mv"], b + 1)
            eng.tensor_scalar(rn[:, b, 0, :], mv[:, b, :, 1], 1e-5, None, ALU.add).then_inc(sem["pool"], 1)
            eng.tensor_scalar(rn[:, b, 1, :], mv[:, b, :, 1], 1.0 + 1e-6, 1e-11, ALU.mult, ALU.add)\
               .then_inc(sem["pool"], 1)
            o.n += 2
            eng.wait_ge(sem["pool"], o.n)
            r = rn[:, b].rearrange("p a t -> p (a t)")
            eng.tensor_tensor(r, r, c("powers")[:, 0:2 * TT], ALU.pow).then_inc(sem["rn"], 1)

        def rms_factors(b):
            eng.wait_ge(sem["ssq"], (b + 1) * TT)
            o.after(eng.tensor_scalar(r2, ssq, 1.0 / D, 1e-6, ALU.mult, ALU.add))
            eng.tensor_tensor(r2, r2, c("powers")[:, 0:TT], ALU.pow).then_inc(sem["r2"], 1)

        chunks = iter(range(2 * X * KC))

        def splits(n):
            for _ in range(n):
                split(next(chunks))

        norm_factors(0)
        for u in range(-1, U):
            splits(1 if u in (-1, U - 1) else 2)
            if new_sequence(u):
                norm_factors(u // 2 + 1)
            splits(1 if u in (-1, U - 1) else 2)
            if closing(u):
                rms_factors(u // 2 - 1)
        rms_factors(B - 1)

    @block.sync
    def _(eng):
        def store_tokens(b):
            eng.wait_ge(sem["n2"], (b + 1) * TT)
            eng.dma_start(s.tokens[b * TT * P:(b + 1) * TT * P, :].rearrange("(t p) d -> p t d", p=P),
                          s.n2[:, b * TT:(b + 1) * TT, :]).then_inc(s.tokens_out, 16)

        for n in range(2 * X * KC):
            if n >= 2:
                eng.wait_ge(sem["split"], n - 1)
            eng.dma_start(stage[:, n % 2, :], s.wgu_dram[n % 2][n // 2]).then_inc(sem[f"w{n % 2}"], 16)
            if n in (18, 26):
                store_tokens((n - 18) // 8)
        store_tokens(2)
        for b in range(3):
            eng.wait_ge(s.tokens_out, 16 * (b + 1))
            eng.wait_ge(sem["nTp"], (b + 1) * KC)
            for n in (2 * b, 2 * b + 1):
                s.load_down(eng, n)
        store_tokens(3)

    @block.scalar
    def _(eng):
        def n1_out(b, k):
            eng.wait_ge(sem["n1Tp"], b * KC + k + 1)
            eng.activation(n1T[:, k, :], ps[:, STK, :], ACT.Copy).then_inc(sem["n1T"], 1)

        def v_and_high(u, t):
            n = u * TT + t
            eng.wait_ge(sem["qkr"], n + 1)
            if u >= 2:
                eng.wait_ge(sem["pv"], (u - 1) * UH)
            hv = lambda a: a.rearrange("p (h d) -> p h d", d=HD)
            eng.activation(vh[:, u % 2, t, :, 0:HD], hv(ps[:, MAXB + t % 2, 2 * UH * HD:3 * UH * HD]), ACT.Copy)\
               .then_inc(sem["va"], 1)
            eng.wait_ge(sem["rope"], n + 1)
            if u:
                eng.wait_ge(sem["s2Tp"], u * 2)
            two = lambda a: a.rearrange("p h (j d) -> p h j d", d=HD)
            q, k = hv(qk[:, t % 2, 0:UH * HD]), hv(qk[:, t % 2, UH * HD:2 * UH * HD])
            eng.activation(two(sq[:, t, :, 0:2 * HD]), spread(q, 2, 2), ACT.Copy, scale=HD ** -0.5)\
               .then_inc(sem["hi"], 1)
            eng.activation(two(sk[:, t, :, 0:3 * HD])[:, :, 0:3:2, :], spread(k, 2, 2), ACT.Copy)\
               .then_inc(sem["hi"], 1)

        def stacks_out(u, t):
            eng.wait_ge(sem["sTp"], u * TT + t + 1)
            both = ps[:, STK, :].bitcast(F16).rearrange("p (s a n) -> p s a n", s=2, n=P)
            for i, dst in enumerate((qT, kT)):
                eng.activation(dst[:, u % 2, :, t * P:(t + 1) * P], both[:, i], ACT.Copy).then_inc(sem["stT"], 1)

        def shifted_q_out(u, ts):
            for t in ts:
                eng.wait_ge(sem["s2Tp"], u * 2 + t // 2 + 1)
                two = ps[:, (TAIL, STK)[t // 2], :].bitcast(F16).rearrange("p (s a n) -> p s a n", s=2, n=P)
                eng.activation(qT[:, u % 2, :, t * P:(t + 1) * P], two[:, t % 2], ACT.Copy).then_inc(sem["q2T"], 1)

        def exponentials(u, h):
            n = u * UH + h
            eng.wait_ge(sem["pp"], n + 1)
            if n >= 2:
                eng.wait_ge(sem["pv"], n - 1)
            src = ps[:, 0:3, :].rearrange("p a n -> p (a n)")[:, 0:10 * P]
            eng.activation(pT[:, n % 2, :], src, ACT.Exp).then_inc(sem["exp"], 1)

        def quad_out(quad):
            eng.wait_ge(sem["pv"], 4 * (quad + 1))
            if quad:
                eng.wait_ge(sem["oqTp"], quad)
            eng.activation(oq, ps[:, OUT, :], ACT.Copy).then_inc(sem["oq"], 1)

        def tail_out(name, b, k):
            eng.wait_ge(sem[name + "p"], b * KC + k + 1)
            if name == "oT" and b:
                eng.wait_ge(sem["lp"], b)
            if name == "nT":
                eng.wait_ge(sem["yp"], (b + 1) * 2)
            eng.activation(oT[:, k, :], ps[:, TAIL, :], ACT.Copy).then_inc(sem[name], 1)

        def squares(b):
            eng.wait_ge(sem["g"], (b + 1) * 2)
            for t in range(TT):
                eng.activation(junk, x[:, t, :], ACT.Square, accum_out=ssq[:, t:t + 1]).then_inc(sem["ssq"], 1)
                eng.wait_ge(sem["ssq"], b * TT + t + 1)

        def turn(u):
            def step(h):
                if u >= 0:
                    exponentials(u, h)

            step(0)
            if u >= 1:
                quad_out(2 * u - 1)
            step(1)
            if has_next(u):
                v_and_high(u + 1, 0)
                v_and_high(u + 1, 1)
            step(2)
            if has_next(u):
                stacks_out(u + 1, 0)
            if closing(u):
                tail_out("oT", u // 2 - 1, 0)
            step(3)
            if has_next(u):
                stacks_out(u + 1, 1)
            if closing(u):
                tail_out("oT", u // 2 - 1, 1)
            if routing_turn(u):
                tail_out("nT", (u - 3) // 2, 0)
            step(4)
            if u >= 0:
                quad_out(2 * u)
            if routing_turn(u):
                tail_out("nT", (u - 3) // 2, 1)
            if has_next(u):
                v_and_high(u + 1, 2)
                v_and_high(u + 1, 3)
            step(5)
            if has_next(u):
                stacks_out(u + 1, 2)
            step(6)
            if has_next(u):
                stacks_out(u + 1, 3)
            step(7)
            if new_sequence(u):
                n1_out(u // 2 + 1, 0)
            if closing(u):
                squares(u // 2 - 1)
            if new_sequence(u):
                n1_out(u // 2 + 1, 1)
            if has_next(u):
                shifted_q_out(u + 1, range(TT))
            else:
                tail_out("oT", B - 1, 0)

        for k in range(KC):
            n1_out(0, k)
        for u in range(-1, U):
            turn(u)
        quad_out(2 * U - 1)
        tail_out("oT", B - 1, 1)
        squares(B - 1)
        for k in range(KC):
            tail_out("nT", B - 1, k)

    @block.tensor
    def _(eng):
        eng.wait_ge(s.att_w_in, s.att_w_n - 1)

        def n1_up(b, k):
            eng.wait_ge(sem["n1"], (b + 1) * TT)
            if k:
                eng.wait_ge(sem["n1T"], b * KC + k)
            elif b:
                eng.wait_ge(sem["stT"], 2 * (2 * b) * TT)
            for t in range(TT):
                m = eng.transpose(ps[:, STK, t * P:(t + 1) * P], s.n2[:, b * TT + t, k * P:(k + 1) * P], c("ident"))
            m.then_inc(sem["n1Tp"], 1)

        def project(u, t):
            n = u * TT + t
            if t == 0:
                eng.wait_ge(sem["n1T"], (u // 2 + 1) * KC)
                if u:
                    eng.wait_ge(sem["mx"], filling(u, 0, 0))
            if t >= 2:
                eng.wait_ge(sem["va"], n - 1)
            w = s.wqkv.rearrange("p k (j g n) -> p k j g n", j=3, g=2)
            for k in range(KC):
                m = eng.matmul(ps[:, MAXB + t % 2, 0:3 * UH * HD], n1T[:, k, t * P:(t + 1) * P],
                               w[:, k, :, u % 2, :], start=k == 0, stop=k == KC - 1)
            m.then_inc(sem["pj"], 1)

        def stack_up(u, t):
            n = u * TT + t
            eng.wait_ge(sem["stk"], n + 1)
            if t:
                eng.wait_ge(sem["stT"], 2 * n)
            for i, stack in enumerate((sq, sk)):
                for a in range(UH // 2):
                    at_word = (i * UH // 2 + a) * P // 2
                    m = eng.transpose(ps[:, STK, at_word:at_word + P // 2].bitcast(F16),
                                      stack[:, t, 2 * a:2 * a + 2, :].rearrange("p h d -> p (h d)"), s.ident16)
            m.then_inc(sem["sTp"], 1)

        def max_scores(u, t, ks):
            eng.wait_ge(sem["stT"], 2 * (u * TT + t + 1))
            for k in ks:
                n, width = filling(u, t, k), (t + 1) * P
                if t == 0 and k < 2:
                    eng.wait_ge(sem["va"], (u + 1) * TT)
                else:
                    eng.wait_ge(sem["mx"], n - 1)
                for i, h in enumerate(FILLS[t][k]):
                    rows, out = slice(h % 2 * ST, (h % 2 + 1) * ST), ps[:, MAXB + k % 2, i * width:(i + 1) * width]
                    eng.matmul(out, qT[rows, u % 2, h // 2, t * P:(t + 1) * P], kT[rows, u % 2, h // 2, 0:width],
                               start=True, stop=True, skip_group_check=True)
                    m = eng.matmul(out[:, t * P:], s.ident16, s.future_k, start=False, stop=True,
                                   skip_group_check=True)
                m.then_inc(sem["mp"], 1)

        def shifted_q(u, ts):
            for t in ts:
                eng.wait_ge(sem["neg"], u * TT + t + 1)
                if t == 0:
                    eng.wait_ge(sem["stT"], 2 * (u + 1) * TT)
                    eng.wait_ge(sem["n1T"], min((u + 1) // 2 + 1, B) * KC)
                for a in range(UH // 2):
                    at_word = (t % 2 * UH // 2 + a) * P // 2
                    m = eng.transpose(ps[:, (TAIL, STK)[t // 2], at_word:at_word + P // 2].bitcast(F16),
                                      sq[:, t, 2 * a:2 * a + 2, :].rearrange("p h d -> p (h d)"), s.ident16)
                if t % 2:
                    m.then_inc(sem["s2Tp"], 1)

        def scores(u, h):
            n = u * UH + h
            rows = slice((h % 2) * ST, (h % 2 + 1) * ST)
            if n:
                eng.wait_ge(sem["exp"], n)
            spot = lambda kt, w: ps[:, at[kt] // 4, at[kt] % 4 * P:(at[kt] % 4 + w) * P]
            for kt in range(TT):
                eng.matmul(spot(kt, TT - kt), kT[rows, u % 2, h // 2, kt * P:(kt + 1) * P],
                           qT[rows, u % 2, h // 2, kt * P:T], start=kt != 3, stop=True, skip_group_check=True)
            for kt in range(TT):
                m = eng.matmul(spot(kt, 1), s.ident16, s.future_q, start=False, stop=True, skip_group_check=True)
            m.then_inc(sem["pp"], 1)

        def weighted_values(u, h):
            n, j = u * UH + h, h % 4
            eng.wait_ge(sem["exp"], n + 1)
            if j == 0 and n:
                eng.wait_ge(sem["oq"], n // 4)
            for kt in range(TT):
                m = eng.matmul(ps[32 * j:32 * j + 32, OUT, kt * P:T],
                               va[:, u % 2, kt, h * (HD + 1):h * (HD + 1) + 32],
                               pT[:, n % 2, at[kt] * P:(at[kt] + TT - kt) * P],
                               start=kt == 0, stop=True, skip_group_check=True)
            m.then_inc(sem["pv"], 1)

        def queries_back(quad):
            eng.wait_ge(sem["oq"], quad + 1)
            if quad:
                eng.wait_ge(sem["on"], quad)
            for t in range(TT):
                m = eng.transpose(ps[:, TAIL, t * P:(t + 1) * P], oq[:, t * P:(t + 1) * P], c("ident"))
            m.then_inc(sem["oqTp"], 1)

        def heads_up(b, k):
            eng.wait_ge(sem["on"], 4 * b + 2 * (k + 1))
            if k:
                eng.wait_ge(sem["oT"], b * KC + k)
            for t in range(TT):
                m = eng.transpose(ps[:, TAIL, t * P:(t + 1) * P], heads[:, t, k * P:(k + 1) * P], c("ident"))
            m.then_inc(sem["oTp"], 1)

        def output_projection(b, i):
            eng.wait_ge(sem["oT"], (b + 1) * KC)
            for t in (2 * i, 2 * i + 1):
                for k in range(KC):
                    m = eng.matmul(ps[:, TAIL, (t % 2) * D:(t % 2 + 1) * D], oT[:, k, t * P:(t + 1) * P],
                                   s.wo[:, k, :], start=k == 0, stop=k == KC - 1)
            m.then_inc(sem["yp"], 1)

        def n2_up(b, k):
            eng.wait_ge(sem["n2"], (b + 1) * TT)
            if k:
                eng.wait_ge(sem["nT"], b * KC + k)
            for t in range(TT):
                m = eng.transpose(ps[:, TAIL, t * P:(t + 1) * P], s.n2[:, b * TT + t, k * P:(k + 1) * P], c("ident"))
            m.then_inc(sem["nTp"], 1)

        def router(b):
            eng.wait_ge(sem["nT"], (b + 1) * KC)
            for t in range(TT):
                for k in range(KC):
                    m = eng.matmul(ps[:, TAIL, t * X:(t + 1) * X], nT[:, k, t * P:(t + 1) * P], s.wr[:, k, :],
                                   start=k == 0, stop=k == KC - 1)
            m.then_inc(sem["lp"], 1)

        def turn(u):
            last = (u - 3) // 2

            def step(h):
                if u >= 0:
                    if h < UH - 1:
                        scores(u, h + 1)
                    weighted_values(u, h)

            if has_next(u):
                project(u + 1, 0)
            if u >= 0:
                eng.wait_ge(sem["q2T"], (u + 1) * TT)
                scores(u, 0)
            if has_next(u):
                project(u + 1, 1)
            step(0)
            if u >= 1:
                queries_back(2 * u - 1)
            step(1)
            if closing(u):
                eng.wait_ge(sem["on"], 2 * u)
                heads_up(u // 2 - 1, 0)
            if has_next(u):
                stack_up(u + 1, 0)
                project(u + 1, 2)
                project(u + 1, 3)
            step(2)
            if closing(u):
                heads_up(u // 2 - 1, 1)
            if routing_turn(u):
                eng.wait_ge(sem["on"], 2 * u)
                n2_up(last, 0)
            if has_next(u):
                stack_up(u + 1, 1)
            step(3)
            if closing(u):
                output_projection(u // 2 - 1, 0)
            if routing_turn(u):
                n2_up(last, 1)
            if has_next(u):
                max_scores(u + 1, 0, half_of(0, 0))
            step(4)
            if has_next(u):
                max_scores(u + 1, 0, half_of(0, 1))
            if u >= 0:
                if closing(u):
                    eng.wait_ge(sem["g"], (u // 2 - 1) * 2 + 1)
                if routing_turn(u):
                    eng.wait_ge(sem["nT"], (last + 1) * KC)
                queries_back(2 * u)
            if has_next(u):
                stack_up(u + 1, 2)
                max_scores(u + 1, 1, half_of(1, 0))
            step(5)
            if has_next(u):
                max_scores(u + 1, 1, half_of(1, 1))
            if closing(u):
                eng.wait_ge(sem["on"], 2 * u + 1)
                output_projection(u // 2 - 1, 1)
            if routing_turn(u):
                eng.wait_ge(sem["on"], 2 * u + 1)
                router(last)
            if has_next(u):
                stack_up(u + 1, 3)
                max_scores(u + 1, 2, half_of(2, 0))
            step(6)
            if new_sequence(u):
                n1_up(u // 2 + 1, 0)
            if has_next(u):
                max_scores(u + 1, 2, half_of(2, 1))
            step(7)
            if has_next(u):
                max_scores(u + 1, 3, half_of(3, 0))
            if new_sequence(u):
                n1_up(u // 2 + 1, 1)
            if has_next(u):
                if u >= 0:
                    eng.wait_ge(sem["on"], 2 * u + 1)
                if closing(u):
                    eng.wait_ge(sem["g"], (u // 2) * 2)
                if routing_turn(u):
                    eng.wait_ge(sem["lg"], last + 1)
                shifted_q(u + 1, (0, 1))
                max_scores(u + 1, 3, half_of(3, 1))
                shifted_q(u + 1, (2, 3))
            else:
                eng.wait_ge(sem["lg"], last + 1)
                heads_up(B - 1, 0)

        for k in range(KC):
            n1_up(0, k)
        eng.wait_ge(s.att_w_in, s.att_w_n)
        for u in range(-1, U):
            turn(u)
        eng.wait_ge(sem["oT"], (B - 1) * KC + 1)
        queries_back(2 * U - 1)
        heads_up(B - 1, 1)
        for i in range(2):
            if i:
                eng.wait_ge(sem["g"], (B - 1) * 2 + 1)
            output_projection(B - 1, i)
        eng.wait_ge(sem["g"], B * 2)
        for k in range(KC):
            n2_up(B - 1, k)
        router(B - 1)

    @block.vector
    def _(eng):
        eng.wait_ge(s.att_w_in, s.att_w_n - 1)
        o = Order(eng, sem["dve"])
        v3 = lambda a: a.rearrange("p (h d) -> p h d", d=HD)
        half = HD // 2

        def moments(b):
            for t in range(TT):
                eng.bn_stats(stats[:, t, :], s.h[:, b * TT + t, :]).then_inc(sem["dve"], 1)
            o.n += TT
            eng.wait_ge(sem["dve"], o.n)
            for t in range(TT):
                m = eng.bn_aggr(mv[:, b, t, :], stats[:, t, :])
                if t < TT - 1:
                    m.then_inc(sem["dve"], 1)
            o.n += TT - 1
            m.then_inc(sem["mv"], 1)
            eng.wait_ge(sem["mv"], b + 1)
            eng.wait_ge(sem["dve"], o.n)

        def normalised(b, factor, out, done):
            for t in range(TT):
                eng.tensor_scalar(out[:, t, :], s.h[:, b * TT + t, :], mv[:, b, t, 0:1], rn[:, b, factor, t:t + 1],
                                  ALU.subtract, ALU.mult).then_inc(sem[done], 1)

        def rmsnormed(b):
            eng.wait_ge(sem["rn"], b + 1)
            normalised(b, 1, s.n2[:, b * TT:(b + 1) * TT, :], "n1")

        def rotate(u, t):
            n = u * TT + t
            eng.wait_ge(sem["pj"], n + 1)
            if n >= 2:
                eng.wait_ge(sem["hi"], 2 * (n - 1))
            qkp = v3(ps[:, MAXB + t % 2, 0:2 * UH * HD])
            cos, sin = (c(name)[:, t * HD:(t + 1) * HD] for name in ("cos", "sin"))
            o.after(eng.tensor_tensor(v3(qk[:, t % 2]), qkp, spread(cos, 1, 2 * UH), ALU.mult))
            o.after(eng.tensor_tensor(v3(rot)[:, :, 0:half], qkp[:, :, half:HD], spread(sin[:, 0:half], 1, 2 * UH),
                                      ALU.mult))
            eng.tensor_tensor(v3(rot)[:, :, half:HD], qkp[:, :, 0:half], spread(sin[:, half:HD], 1, 2 * UH),
                              ALU.mult).then_inc(sem["qkr"], 1)
            eng.wait_ge(sem["qkr"], n + 1)
            eng.tensor_tensor(qk[:, t % 2], qk[:, t % 2], rot, ALU.add).then_inc(sem["rope"], 1)
            eng.wait_ge(sem["rope"], n + 1)

        def low_halves(u, t):
            n = u * TT + t
            eng.wait_ge(sem["hi"], 2 * n + 2)
            o.after(eng.memset(sq[:, t, :, 3 * HD:3 * HD + 1], 0.0))
            o.after(eng.scalar_tensor_tensor(sq[:, t, :, 2 * HD:3 * HD], v3(qk[:, t % 2, 0:UH * HD]), HD ** -0.5,
                                             sq[:, t, :, 0:HD], ALU.mult, ALU.subtract))
            eng.tensor_tensor(sk[:, t, :, HD:2 * HD], v3(qk[:, t % 2, UH * HD:2 * UH * HD]), sk[:, t, :, 0:HD],
                              ALU.subtract).then_inc(sem["stk"], 1)
            eng.wait_ge(sem["stk"], n + 1)

        def maxima(u, t, ks):
            for k in ks:
                n, hs = filling(u, t, k), FILLS[t][k]
                eng.wait_ge(sem["mp"], n + 1)
                of_heads = ps[:, MAXB + k % 2, 0:len(hs) * (t + 1) * P].rearrange("p (h n) -> p h n", h=len(hs))
                eng.tensor_reduce(mx[:, t, hs.start:hs.stop:2], of_heads, AX.X, ALU.max).then_inc(sem["mx"], 1)
            if ks.stop == len(FILLS[t]):
                eng.wait_ge(sem["mx"], n + 1)
                eng.wait_ge(sem["sTp"], u * TT + t + 1)
                eng.tensor_scalar(sq[:, t, :, 3 * HD:3 * HD + 1], mx[:, t, :].unsqueeze(2), -1.0, None, ALU.mult)\
                   .then_inc(sem["neg"], 1)
                eng.wait_ge(sem["neg"], u * TT + t + 1)

        def divided(quad):
            eng.wait_ge(sem["oqTp"], quad + 1)
            out = ps[:, TAIL, :].rearrange("p (t h d) -> p t h d", t=TT, h=4)
            o.after(eng.reciprocal(rden.unsqueeze(3), out[:, :, :, HD:HD + 1]))
            if quad >= 4:
                eng.wait_ge(sem["oTp"], quad // 4 * KC)
            q = quad % 4
            hq = heads[:, :, q * 4 * HD:(q + 1) * 4 * HD].rearrange("p t (h d) -> p t h d", h=4)
            eng.tensor_tensor(hq, out[:, :, :, 0:HD], spread(rden, 3, HD), ALU.mult).then_inc(sem["on"], 1)
            eng.wait_ge(sem["on"], quad + 1)

        def layernormed(b):
            eng.wait_ge(sem["ssq"], b * TT)
            normalised(b, 0, x, "x")

        def add_attention(b, i):
            eng.wait_ge(sem["yp"], b * 2 + i + 1)
            eng.wait_ge(sem["x"], (b + 1) * TT)
            x2 = x[:, 2 * i:2 * i + 2, :]
            eng.tensor_tensor(x2, x2, ps[:, TAIL, :].rearrange("p (t d) -> p t d", t=2), ALU.add)\
               .then_inc(sem["g"], 1)
            eng.wait_ge(sem["g"], b * 2 + i + 1)

        def n2_and_h(b):
            hb = s.h[:, b * TT:(b + 1) * TT, :]
            o.after(eng.tensor_tensor(hb, hb, x, ALU.add))
            eng.wait_ge(sem["r2"], b + 1)
            for t in range(TT):
                eng.scalar_tensor_tensor(s.n2[:, b * TT + t, :], x[:, t, :], r2[:, t:t + 1], s.g2,
                                         ALU.mult, ALU.mult).then_inc(sem["n2"], 1)
            eng.wait_ge(sem["n2"], (b + 1) * TT)

        def logits(b):
            eng.wait_ge(sem["lp"], b + 1)
            eng.tensor_copy(s.logits[:, b * TT:(b + 1) * TT, :],
                            ps[:, TAIL, 0:TT * X].rearrange("p (t x) -> p t x", t=TT)).then_inc(sem["lg"], 1)

        def turn(u):
            if has_next(u):
                rotate(u + 1, 0)
                rotate(u + 1, 1)
            if u >= 1:
                divided(2 * u - 1)
            if has_next(u):
                low_halves(u + 1, 0)
                low_halves(u + 1, 1)
            if routing_turn(u):
                n2_and_h((u - 3) // 2)
            if new_sequence(u):
                moments(u // 2 + 1)
            if has_next(u):
                rotate(u + 1, 2)
                rotate(u + 1, 3)
            if closing(u):
                layernormed(u // 2 - 1)
            if closing(u):
                add_attention(u // 2 - 1, 0)
            if has_next(u):
                maxima(u + 1, 0, half_of(0, 0))
                low_halves(u + 1, 2)
                low_halves(u + 1, 3)
                maxima(u + 1, 0, half_of(0, 1))
            if new_sequence(u):
                rmsnormed(u // 2 + 1)
            if has_next(u):
                maxima(u + 1, 1, half_of(1, 0))
            if u >= 0:
                divided(2 * u)
            if has_next(u):
                maxima(u + 1, 1, half_of(1, 1))
                maxima(u + 1, 2, half_of(2, 0))
            if closing(u):
                add_attention(u // 2 - 1, 1)
            if has_next(u):
                maxima(u + 1, 2, half_of(2, 1))
                maxima(u + 1, 3, half_of(3, 0))
            if routing_turn(u):
                logits((u - 3) // 2)
            if has_next(u):
                maxima(u + 1, 3, half_of(3, 1))
            else:
                layernormed(B - 1)

        moments(0)
        rmsnormed(0)
        for k in range(KC):
            m = eng.tensor_scalar(s.wqkv[:, k, :], s.wqkv[:, k, :], s.g1[:, k:k + 1], None, ALU.mult)
            if k < KC - 1:
                o.after(m)
        m.then_inc(s.att_w_in, 1)
        o.after(eng.memset(sq[:, :, :, 3 * HD:ST], 0.0))
        o.after(eng.memset(sk[:, :, :, 3 * HD:ST], 0.0))
        o.after(eng.memset(sk[:, :, :, 3 * HD:3 * HD + 1], 1.0))
        for u in range(2):
            o.after(eng.memset(va[:, u, :, UH * (HD + 1):VW], 0.0))
            o.after(eng.memset(vh[:, u, :, :, HD:HD + 1], 1.0))
        for u in range(-1, U):
            turn(u)
        divided(2 * U - 1)
        for i in range(2):
            add_attention(B - 1, i)
        n2_and_h(B - 1)
        logits(B - 1)


def routing(nc, ctx, s):
    ar = Arena(s.scratch, s.scratch_words)
    ar.at = s.wd_words
    tx = lambda: ar.take(NT, X)
    eq, one1, one2, lg2, both, pref, tot = (tx() for _ in range(7))
    m1, m2, pick, w1s, w2s = (ar.take(NT) for _ in range(5))
    incl, excl, tot_e = ar.take(X, NT), ar.take(X, NT), ar.take(X, NT)
    n_t, end_t = ar.take(X), ar.take(X)
    free = Arena(s.wqkv[:, :, :].rearrange("p k n -> p (k n)"), KC * 3 * D)
    slot, col, row = ar.take(TOP, NT), ar.take(TOP, NT), ar.take(TOP, NT)
    slot_i, col_i = (ar.take(TOP * NT).bitcast(I32).rearrange("p (i t) -> p i t", i=TOP) for _ in range(2))
    in_row = ar.take(TOP * NT, P, dtype=F16)
    in_tile = free.take(TOP * NT, XT, dtype=F16)
    cmp_t, own = free.take(XT, X), free.take(XT)
    token1, second, spare = (free.take(XT) for _ in range(3))
    tiles_i = ar.tensor[:, ar.at:ar.at + X].bitcast(I32)
    ps, c = s.psum, s.const
    names = ["both", "cnt", "in", "src", "e", "we", "dve", "pad", "scaled", "hi", "lo_dve", "lo_pool"]
    sem = {n: ctx.enter_context(nc.semaphore("route_" + n)) for n in names}
    block = ctx.enter_context(nc.Block())

    @block.vector
    def _(eng):
        o = Order(eng, sem["dve"])
        eng.wait_ge(s.tokens_out, 16 * 3)
        for n in range(DQ - 1, STAGES, DQ):
            eng.memset(s.stage[HC[-1][1]:P, n, DC - 1, :], 0.0).then_inc(sem["pad"], 1)
        thirds = iter(range(DQ - 1, X * DQ, DQ))

        def low_parts(k):
            for _ in range(k):
                n = next(thirds)
                eng.wait_ge(sem["hi"], n + 1)
                eng.scalar_tensor_tensor(s.wd[:, n * DC:(n + 1) * DC, 1, :], s.stage[:, n % STAGES], W_SCALE,
                                         s.wd[:, n * DC:(n + 1) * DC, 0, :], ALU.mult, ALU.subtract)\
                   .then_inc(sem["lo_dve"], 1)

        def first_of_the_largest(values, top, onehot):
            o.after(eng.tensor_reduce(top, values, AX.X, ALU.max))
            o.after(eng.tensor_tensor(eq, values, spread(top, 2, X), ALU.is_equal))
            o.after(eng.tensor_tensor(eq, eq, spread(c("rank8"), 1, NT), ALU.mult))
            o.after(eng.tensor_reduce(pick, eq, AX.X, ALU.max))
            o.after(eng.tensor_tensor(onehot, eq, spread(pick, 2, X), ALU.is_equal))

        lg = s.logits[:, :, :]
        first_of_the_largest(lg, m1, one1)
        o.after(eng.scalar_tensor_tensor(lg2, one1, -3e38, lg, ALU.mult, ALU.add))
        first_of_the_largest(lg2, m2, one2)
        eng.tensor_tensor(both, one1, one2, ALU.add).then_inc(sem["both"], 1)
        eng.tensor_tensor(w2s, m2, m1, ALU.subtract).then_inc(sem["e"], 1)
        low_parts(2)
        eng.wait_ge(sem["we"], 1)
        o.after(eng.tensor_scalar(w1s, w2s, 1.0, None, ALU.add))
        o.after(eng.reciprocal(s.w[:, 0, :], w1s))
        o.after(eng.tensor_tensor(s.w[:, 1, :], w2s, s.w[:, 0, :], ALU.mult))
        eng.wait_ge(sem["cnt"], 1)
        o.after(eng.tensor_copy(pref, ps[:, 0, 0:NT * X].rearrange("p (t e) -> p t e", e=X)))
        o.after(eng.tensor_copy(tot_e, ps[:, 1, 0:NT * X].rearrange("p (t e) -> p e t", e=X)))
        o.after(eng.tensor_tensor_scan(incl.rearrange("p e t -> p (e t)"), c("ereset"),
                                       tot_e.rearrange("p e t -> p (e t)"), 0.0, ALU.mult, ALU.add))
        o.after(eng.tensor_tensor(excl, incl, tot_e, ALU.subtract))
        o.after(eng.tensor_scalar(tiles_i, incl[:, :, NT - 1], P - 1.0, None, ALU.add))
        o.after(eng.tensor_scalar(tiles_i, tiles_i, 7, None, ALU.arith_shift_right))
        o.after(eng.tensor_copy(n_t, tiles_i))
        low_parts(1)
        o.after(eng.tensor_tensor_scan(end_t, c("ones")[:, 0:X], n_t, 0.0, ALU.mult, ALU.add))
        o.after(eng.tensor_tensor(cmp_t, spread(end_t, 1, XT), spread(c("count")[:, 0:XT], 2, X), ALU.is_le))
        o.after(eng.tensor_reduce(own, cmp_t, AX.X, ALU.add))
        o.after(eng.tensor_scalar(s.expert[:, :], own, X - 1.0, None, ALU.min))
        o.after(eng.tensor_tensor(n_t, end_t, n_t, ALU.subtract))
        o.after(eng.tensor_scalar(n_t, n_t, float(P), None, ALU.mult))
        o.after(eng.tensor_tensor(excl, excl, spread(n_t, 2, NT), ALU.add))
        o.after(eng.tensor_tensor(pref, pref, excl.rearrange("p e t -> p t e"), ALU.add))
        low_parts(1)
        for i, onehot in enumerate((one1, one2)):
            o.after(eng.tensor_tensor(lg2, onehot, pref, ALU.mult))
            o.after(eng.tensor_reduce(slot[:, i, :], lg2, AX.X, ALU.add))
        o.after(eng.tensor_copy(slot_i, slot))
        o.after(eng.tensor_scalar(col_i, slot_i, 7, None, ALU.arith_shift_right))
        o.after(eng.tensor_copy(col, col_i))
        o.after(eng.scalar_tensor_tensor(row, col, -float(P), slot, ALU.mult, ALU.add))
        flat = lambda a: a.rearrange("p i t -> p (i t)")
        o.after(eng.tensor_tensor(in_tile, spread(c("count")[:, 0:XT], 1, TOP * NT), spread(flat(col), 2, XT),
                                  ALU.is_equal))
        for i in range(TOP):
            part = slice(i * NT, (i + 1) * NT)
            o.after(eng.tensor_tensor(in_tile[:, part], in_tile[:, part], spread(c("token1"), 2, XT), ALU.mult))
        for n in range(0, TOP * NT, 8):
            m = eng.tensor_tensor(in_row[:, n:n + 8, :], spread(c("count"), 1, 8), spread(flat(row)[:, n:n + 8], 2, P),
                                  ALU.is_equal)
            m.then_inc(sem["in"], 1)
            if n in (0, 16):
                low_parts(1)
        eng.wait_ge(sem["src"], 1)
        o.after(eng.tensor_copy(token1, ps[:, 2, 0:XT]))
        o.after(eng.tensor_tensor(token1, token1, ps[:, 3, 0:XT], ALU.add))
        o.after(eng.tensor_scalar(s.source[:, :], token1, -1.0, 0.0, ALU.add, ALU.max))
        o.after(eng.tensor_scalar(second, ps[:, 3, 0:XT], 0.0, float(NT * P), ALU.is_gt, ALU.mult))
        o.after(eng.scalar_tensor_tensor(second, token1, -1.0, second, ALU.add, ALU.add))
        o.after(eng.scalar_tensor_tensor(spare, token1, 0.0, c("spare1"), ALU.is_equal, ALU.mult))
        o.after(eng.tensor_tensor(s.target[:, :], second, spare, ALU.add))
        low_parts(X - 6)

    @block.scalar
    def _(eng):
        def high_parts(ns):
            for n in ns:
                eng.wait_ge(s.down_in[n % STAGES], 16 * DC * (n // STAGES + 1))
                if n % DQ == DQ - 1 and n < STAGES:
                    eng.wait_ge(sem["pad"], n // DQ + 1)
                st, hi = s.stage[:, n % STAGES], s.wd[:, n * DC:(n + 1) * DC, 0, :]
                if n % DQ < DQ - 1:
                    eng.activation(st, st, ACT.Copy, scale=W_SCALE).then_inc(sem["scaled"], 1)
                    eng.wait_ge(sem["scaled"], n // DQ * (DQ - 1) + n % DQ + 1)
                    eng.activation(hi, st, ACT.Copy).then_inc(sem["hi"], 1)
                else:
                    eng.activation(hi, st, ACT.Copy, scale=W_SCALE).then_inc(sem["hi"], 1)

        high_parts(range(4))
        eng.wait_ge(sem["e"], 1)
        eng.activation(w2s, w2s, ACT.Exp).then_inc(sem["we"], 1)
        high_parts(range(4, X * DQ))

    @block.gpsimd
    def _(eng):
        for n in range(X * DQ):
            if n % DQ < DQ - 1:
                eng.wait_ge(sem["hi"], n + 1)
                eng.tensor_tensor(s.wd[:, n * DC:(n + 1) * DC, 1, :], s.stage[:, n % STAGES],
                                  s.wd[:, n * DC:(n + 1) * DC, 0, :], ALU.subtract).then_inc(sem["lo_pool"], 1)

    @block.tensor
    def _(eng):
        eng.wait_ge(sem["both"], 1)
        rhs = both.rearrange("p t e -> p (t e)")
        eng.matmul(ps[:, 0, 0:NT * X], c("before"), rhs, start=True, stop=True)
        eng.matmul(ps[:, 1, 0:NT * X], c("ones"), rhs, start=True, stop=True).then_inc(sem["cnt"], 1)
        for n in range(TOP * NT):
            if n % 8 == 0:
                eng.wait_ge(sem["in"], n // 8 + 1)
            m = eng.matmul(ps[:, 2 + n // NT, 0:XT], in_row[:, n, :], in_tile[:, n, :],
                           start=n % NT == 0, stop=n % NT == NT - 1)
        m.then_inc(sem["src"], 1)

    @block.sync
    def _(eng):
        for n in range(STAGES, X * DQ):
            x, q = divmod(n - STAGES, DQ)
            if q == DQ - 1:
                eng.wait_ge(sem["lo_dve"], x + 1)
            else:
                eng.wait_ge(sem["lo_pool"], x * (DQ - 1) + q + 1)
            s.load_down(eng, n)


def experts(nc, ctx, s):
    ar = Arena(s.scratch, s.scratch_words)
    ar.at = s.wd_words
    xin = ar.take(2, D)
    hid = ar.take(2, HID)
    y = ar.take(2, D)
    xT = ar.take(2, 2, KC, P, dtype=F16)
    hT = ar.take(2, len(HC), P, dtype=F16)
    HH = HID // 2
    PRODUCTS = ((0, 0), (0, 1), (1, 0))
    ps, c = s.psum, s.const
    names = ["x0", "x1", "xTp", "xTh", "xT", "gp", "sil", "hid", "hTp", "hTh", "lo4", "hT", "yp", "y", "out0",
             "out1"]
    sem = {n: ctx.enter_context(nc.semaphore("exp_" + n)) for n in names}
    block = ctx.enter_context(nc.Block())

    def turns(tile, eng):
        for j in range(3):
            tile(j, j % 2, (j + 1) // 2 + 1, first=j == 0)
        pairs = (XT - 5) // 2
        with eng.Fori(0, pairs) as i:
            tile(2 * i + 3, 1, i + 3)
            tile(2 * i + 4, 0, i + 3)
        for j in range(2 * pairs + 3, XT):
            tile(j, j % 2, (j + 1) // 2 + 1, last=j == XT - 1)

    @block.gpsimd
    def _(eng):
        eng.wait_ge(s.tokens_out, 16 * B)

        def gather(j):
            eng.indirect_dma_start(out=xin[:, j % 2, :], out_offset=None, in_=s.tokens,
                                   in_offset=bass.IndirectOffsetOnAxis(ap=s.source[:, j:j + 1], axis=0))\
               .then_inc(sem[f"x{j % 2}"], 16)

        gather(0)
        gather(1)
        eng.wait_ge(sem["xTp"], 1)
        gather(2)
        for j in range(XT):
            if j + 3 < XT:
                eng.wait_ge(sem["xTp"], j + 2)
                gather(j + 3)
            eng.wait_ge(sem["y"], j + 1)
            eng.indirect_dma_start(out=s.results, out_offset=bass.IndirectOffsetOnAxis(ap=s.target[:, j:j + 1], axis=0),
                                   in_=y[:, j % 2, :], in_offset=None).then_inc(sem[f"out{j % 2}"], 16)
        for r in range(2):
            eng.wait_ge(sem[f"out{r}"], 16 * ((XT + 1 - r) // 2))

    @block.tensor
    def _(eng):
        def load(r, nth):
            eng.wait_ge(sem[f"x{r}"], 16 * nth)
            for k in range(KC):
                m = eng.transpose(ps[:, 6, k * P:(k + 1) * P], xin[:, r, k * P:(k + 1) * P], c("ident"))
            m.then_inc(sem["xTp"], 1)

        def down(j, e, first=False):
            eng.wait_ge(sem["hT"], j + 1)
            if not first:
                eng.wait_ge(sem["y"], j)
            n = 0
            for q, (_, size) in enumerate(HC):
                for a, b in PRODUCTS:
                    n += 1
                    m = eng.matmul(ps[:, 7, 0:D], hT[0:size, a, q, :],
                                   s.wd[0:size, bass.ds(e * len(HC) + q, 1), b, :].rearrange("p a n -> p (a n)"),
                                   start=n == 1, stop=n == 3 * len(HC))
            m.then_inc(sem["yp"], 1)

        def expert(j):
            return eng.value_load(s.expert[0:1, bass.ds(j, 1)], min_val=0, max_val=X - 1)

        def tile(j, r, nth, first=False, last=False):
            e = expert(j)
            if first:
                load(0, 1)
            eng.wait_ge(sem["xT"], j + 1)
            for u in range(2):
                if not first:
                    eng.wait_ge(sem["hid"], 2 * j - 1 + u)
                for which, w in enumerate((s.wg, s.wu)):
                    n = 0
                    for k in range(KC):
                        for a, b in PRODUCTS:
                            n += 1
                            m = eng.matmul(ps[:, 2 * u + which, 0:HH], xT[:, r, a, k, :],
                                           w[:, bass.ds(e * KC + k, 1), b, u * HH:(u + 1) * HH]
                                           .rearrange("p a n -> p (a n)"), start=n == 1, stop=n == 3 * KC)
                m.then_inc(sem["gp"], 1)
            if not last:
                load(1 - r, nth)
            if not first:
                down(j - 1, expert(j - 1), first=isinstance(j, int) and j == 1)
            eng.wait_ge(sem["hid"], 2 * j + 2)
            for q, (h0, n) in enumerate(HC):
                m = eng.transpose(ps[0:n, 4 + q // 4, (q % 4) * P:(q % 4 + 1) * P], hid[:, r, h0:h0 + n], c("ident"))
            m.then_inc(sem["hTp"], 1)
            if last:
                down(j, e)

        turns(tile, eng)

    full = HID // P
    rest = HC[-1][1]
    chunk = lambda n: ps[:, 4:6, :].rearrange("p a (q n) -> p (a q) n", n=P)[:, 0:n, :]

    @block.scalar
    def _(eng):
        def x_high(j, r):
            eng.wait_ge(sem["xTp"], j + 1)
            eng.activation(xT[:, r, 0, :, :], ps[:, 6, 0:D].rearrange("p (k n) -> p k n", k=KC), ACT.Copy)\
               .then_inc(sem["xTh"], 1)

        def tile(j, r, nth, first=False, last=False):
            if first:
                x_high(0, 0)
            for u in range(2):
                eng.wait_ge(sem["gp"], 2 * j + u + 1)
                eng.activation(hid[:, r, u * HH:(u + 1) * HH], ps[:, 2 * u, 0:HH], ACT.Silu, scale=1 / W_SCALE)\
                   .then_inc(sem["sil"], 1)
            if not last:
                x_high(j + 1, 1 - r)
            eng.wait_ge(sem["hTp"], j + 1)
            if not first:
                eng.wait_ge(sem["yp"], j)
            eng.activation(hT[:, 0, 0:full, :], chunk(full), ACT.Copy).then_inc(sem["hTh"], 1)
            eng.activation(hT[0:rest, 0, full, :], chunk(full + 1)[0:rest, full, :], ACT.Copy).then_inc(sem["hTh"], 1)

        turns(tile, eng)

    @block.vector
    def _(eng):
        def x_low(j, r):
            eng.wait_ge(sem["xTh"], j + 1)
            eng.tensor_tensor(xT[:, r, 1, :, :], ps[:, 6, 0:D].rearrange("p (k n) -> p k n", k=KC), xT[:, r, 0, :, :],
                              ALU.subtract).then_inc(sem["xT"], 1)

        def result(j, r, stored):
            eng.wait_ge(sem["yp"], j + 1)
            if not isinstance(stored, int) or stored > 0:
                eng.wait_ge(sem[f"out{r}"], 16 * stored)
            eng.tensor_scalar(y[:, r, :], ps[:, 7, 0:D], 1 / W_SCALE, None, ALU.mult).then_inc(sem["y"], 1)

        def tile(j, r, nth, first=False, last=False):
            if first:
                x_low(0, 0)
            for u in range(2):
                eng.wait_ge(sem["sil"], 2 * j + u + 1)
                half = hid[:, r, u * HH:(u + 1) * HH]
                eng.scalar_tensor_tensor(half, ps[:, 2 * u + 1, 0:HH], 1 / W_SCALE, half, ALU.mult, ALU.mult)\
                   .then_inc(sem["hid"], 1)
            if not last:
                x_low(j + 1, 1 - r)
            if not first:
                result(j - 1, 1 - r, nth - 2)
            eng.wait_ge(sem["hTh"], 2 * j + 2)
            eng.tensor_tensor(hT[:, 1, 0:full, :], chunk(full), hT[:, 0, 0:full, :], ALU.subtract)\
               .then_inc(sem["lo4"], 1)
            eng.tensor_tensor(hT[0:rest, 1, full, :], chunk(full + 1)[0:rest, full, :], hT[0:rest, 0, full, :],
                              ALU.subtract).then_inc(sem["hT"], 1)
            if last:
                result(j, r, j // 2)

        turns(tile, eng)


def combine(nc, ctx, s, out):
    ar = Arena(s.scratch, s.scratch_words)
    got = ar.take(NT * TOP, D)
    summed, done = (ctx.enter_context(nc.semaphore("comb_" + n)) for n in ("summed", "done"))
    back = [ctx.enter_context(nc.semaphore(f"comb_back{b}")) for b in range(B)]
    block = ctx.enter_context(nc.Block())
    out_t = out.rearrange("(t p) d -> p t d", p=P)
    results = s.results[0:TOP * NT * P, :].rearrange("(n p) d -> p n d", p=P)

    @block.vector
    def _(eng):
        for t in range(NT):
            if t % TT == 0:
                eng.wait_ge(back[t // TT], 16 * TOP)
            for i in range(TOP):
                eng.scalar_tensor_tensor(s.h[:, t, :], got[:, i * NT + t, :], s.w[:, i, t:t + 1], s.h[:, t, :],
                                         ALU.mult, ALU.add).then_inc(summed, 1)
                eng.wait_ge(summed, t * TOP + i + 1)

    @block.sync
    def _(eng):
        for b in range(B):
            for i in range(TOP):
                n = i * NT + b * TT
                eng.dma_start(got[:, n:n + TT, :], results[:, n:n + TT, :]).then_inc(back[b], 16)
        for t in range(0, NT, 2):
            eng.wait_ge(summed, (t + 2) * TOP)
            eng.dma_start(out_t[:, t:t + 2, :], s.h[:, t:t + 2, :]).then_inc(done, 16)
        eng.wait_ge(done, 16 * NT // 2)


class Shared:
    pass


def build(nc, a, out):
    s = Shared()
    with ExitStack() as ctx:
        sb = lambda name, shape, dt=F32: ctx.enter_context(nc.sbuf_tensor(name, shape, dt))
        sem = lambda name: ctx.enter_context(nc.semaphore(name))
        s.psum = ctx.enter_context(nc.psum_tensor("psum", [P, 8, 512], F32))
        s.h = sb("h", [P, NT, D])
        s.scratch_words = 17536
        s.scratch = sb("scratch", [P, s.scratch_words])
        tables = {}

        def table_views(tile, packed_tables):
            for name, (at, n) in packed_tables[1].items():
                tables[name] = tile[:, at:at + n]

        const = sb("const", [P, CONST[0].shape[1]])
        const_half = sb("const_half", [P, CONST_HALF[0].shape[1]], F16)
        table_views(const, CONST)
        table_views(const_half, CONST_HALF)
        s.const = lambda name: tables[name]
        s.ids = sb("ids", [P, NT], I32)
        s.table = a["table"]
        s.n2 = sb("n2", [P, NT, D])
        w3 = lambda name, n: sb(name, [P, KC, n])
        early = Arena(s.n2[:, :, :].rearrange("p t d -> p (t d)"), NT * D)
        s.gwq, s.gwk, s.wgk1, s.wvg, s.gwo = (early.take(KC, n) for n in (P, P, LOW, 2 * D, D))
        s.wgk2 = early.take(P)
        s.wg, s.wu = (sb(n, [P, X * KC, 2, HID], F16) for n in ("w_gate", "w_up"))
        s.wd_words = X * len(HC) * D
        s.wd = s.scratch[:, 0:s.wd_words].bitcast(F16).rearrange("p (q a n) -> p q a n", a=2, n=D)
        s.wgu_dram = [a[n].rearrange("x (k p) n -> (x k) p n", p=P) for n in ("wg", "wu")]
        s.stage = s.n2[:, 0:3 * TT, :].rearrange("p (n i) d -> p n i d", i=DC)
        s.down_in = [sem(f"down_in{n}") for n in range(STAGES)]

        def load_down(eng, n):
            x, q = divmod(n, DQ)
            for i in range(DC):
                h0, size = HC[q * DC + i]
                eng.dma_start(s.stage[0:size, n % STAGES, i, :], a["wd"][x, h0:h0 + size, :])\
                   .then_inc(s.down_in[n % STAGES], 16)

        s.load_down = load_down
        s.tokens = nc.dram_tensor("tokens", [NT * P, D], F32).ap()
        s.source, s.target = (sb(n, [P, XT], I32) for n in ("source", "target"))
        s.results = nc.dram_tensor("results", [(TOP * NT + XT) * P, D], F32).ap()
        s.expert = sb("expert", [P, XT], I32)
        w_choice = sb("w_choice", [P, TOP, NT]); s.w = w_choice[:, :, :]
        s.tokens_out = sem("tokens_out")
        s.tok_bias = early.take(D)
        const_first = early.take(CONST_FIRST[0].shape[1])
        table_views(const_first, CONST_FIRST)
        s.bgk2_t = sb("bgk2", [P, 1]); s.bgk2 = s.bgk2_t[:, :]
        s.gnw_t = sb("gnw", [P, 1]); s.gnw_half = s.gnw_t[:, :]
        s.ids_in, s.const_in, s.gla_w_in, s.vec_in = sem("ids_in"), sem("const_in"), sem("gla_w_in"), sem("vec_in")
        s.rows_in = [sem(f"rows_in{b}") for b in range(B)]
        s.gla_w_n, s.vec_n = 16 * 7, 16 * 3 + 1
        s.logits = sb("logits", [P, NT, X])
        s.wqkv, s.wo, s.wr = w3("wqkv", 3 * D), w3("wo", D), w3("wr", X)
        s.g1_t = sb("g1", [P, KC]); s.g1 = s.g1_t[:, :]
        s.g2_t = sb("g2", [P, D]); s.g2 = s.g2_t[:, :]
        s.ident16, s.future_k, s.future_q = (tables[n] for n in ("ident16", "future_k", "future_q"))
        s.att_w_in = sem("att_w_in")
        s.att_w_n = 16 * 8 + 1
        kc = lambda name: a[name].rearrange("(k p) n -> p k n", p=P)

        def gather_tokens(eng, tiles):
            for t in tiles:
                eng.indirect_dma_start(out=s.h[:, t, :], out_offset=None, in_=s.table,
                                       in_offset=bass.IndirectOffsetOnAxis(ap=s.ids[:, t:t + 1], axis=0))\
                   .then_inc(s.rows_in[t // TT], 16)

        def load_attention_weights(eng):
            for i, name in enumerate(("wq", "wk", "wv")):
                eng.dma_start(s.wqkv[:, :, i * D:(i + 1) * D], kc(name)).then_inc(s.att_w_in, 16)
            eng.dma_start(s.wo[:, :, :], kc("wo")).then_inc(s.att_w_in, 16)
            eng.dma_start(s.wr[:, :, :], kc("w_router")).then_inc(s.att_w_in, 16)
            eng.dma_start(s.g1, a["g1"]).then_inc(s.att_w_in, 16)
            eng.dma_start(s.g2, a["g2"].partition_broadcast(P)).then_inc(s.att_w_in, 16)
            eng.dma_start(const_half[:, :], a["const_half"]).then_inc(s.att_w_in, 16)

        s.gather_tokens, s.load_attention_weights = gather_tokens, load_attention_weights
        block = nc.Block()
        with block:
            @block.gpsimd
            def _(eng):
                eng.wait_ge(s.ids_in, 16)
                s.gather_tokens(eng, range(TT))

            @block.sync
            def _(eng):
                eng.dma_start(s.ids[:, :], a["ids"]).then_inc(s.ids_in, 16)
                eng.dma_start(const[:, :], a["const"]).then_inc(s.const_in, 16)
                eng.dma_start(s.gnw_half, a["gnw"]).then_inc(s.vec_in, 16)
                eng.dma_start(s.tok_bias, a["tok_bias"].partition_broadcast(P)).then_inc(s.vec_in, 16)
                eng.dma_start(s.bgk2, a["bgk2"]).then_inc(s.vec_in, 16)
                eng.dma_start(const_first, a["const_first"]).then_inc(s.const_in, 16)
                eng.dma_start(s.wgk1[:, :, :], kc("Wgk1")).then_inc(s.gla_w_in, 16)
                eng.dma_start(s.wgk2[0:LOW, :], a["Wgk2"]).then_inc(s.gla_w_in, 16)
                eng.dma_start(s.gwq[:, :, :], kc("Wq")).then_inc(s.gla_w_in, 16)
                eng.dma_start(s.gwk[:, :, :], kc("Wk")).then_inc(s.gla_w_in, 16)
                eng.dma_start(s.wvg[:, :, 0:D], kc("Wv")).then_inc(s.gla_w_in, 16)
                eng.dma_start(s.wvg[:, :, D:2 * D], kc("Wg")).then_inc(s.gla_w_in, 16)
                eng.dma_start(s.gwo[:, :, :], kc("Wo")).then_inc(s.gla_w_in, 16)

            @block.vector
            def _(eng):
                eng.wait_ge(s.vec_in, 48)
                eng.tensor_scalar(s.gnw_half, s.gnw_half, 0.5, None, ALU.mult).then_inc(s.vec_in, 1)
        with ExitStack() as stage:
            linear_attention(nc, stage, s)
        with ExitStack() as stage:
            softmax_attention(nc, stage, s)
        with ExitStack() as stage:
            routing(nc, stage, s)
        with ExitStack() as stage:
            experts(nc, stage, s)
        with ExitStack() as stage:
            combine(nc, stage, s, out)


def kernel(**inputs):
    import concourse.bacc as bacc
    from concourse.bass_utils import run_bass_kernel_spmd as run

    src = {
        "ids": inputs["x"].reshape(NT, P).T,
        "table": inputs["L0_tok_weight"].T,
        "tok_bias": inputs["L0_tok_bias"],
        "const": CONST[0],
        "const_first": CONST_FIRST[0],
        "const_half": CONST_HALF[0],
    }
    for n in ("Wq", "Wk", "Wv", "Wgk1", "Wgk2", "bgk2", "Wg", "gnw", "Wo"):
        src[n] = inputs["L0_attn_" + n]
    for n in ("wq", "wk", "wv", "wo", "w_router", "g1", "g2", "wg", "wu", "wd"):
        src[n] = inputs["L0_ffn_" + n]
    src["g1"] = src["g1"].reshape(KC, P).T
    src["gnw"] = np.tile(src["gnw"], P // DV).reshape(P, 1)
    src["bgk2"] = src["bgk2"].reshape(P, 1)
    nc = bacc.Bacc("TRN2", target_bir_lowering=False, num_devices=1)
    arrays, aps = {}, {}
    for name, v in src.items():
        v = np.ascontiguousarray(v)
        arrays["in_" + name] = v
        aps[name] = nc.dram_tensor("in_" + name, list(v.shape), mybir.dt.from_np(v.dtype), kind="ExternalInput").ap()
    out = nc.dram_tensor("out_y", [NT * P, D], F32, kind="ExternalOutput").ap()
    build(nc, aps, out)
    r = run(nc, [arrays], core_ids=[0])
    return r.results[0]["out_y"].reshape(B, T, D)
```
